# Optimizing a Trainium2 kernel written in Bass

```python
import numpy as np
import jax
import jax.numpy as jnp

def _softmax(x, axis=-1):
    return jax.nn.softmax(x, axis=axis)

def _gelu(x):
    return jax.nn.gelu(x, approximate=True)

def _silu(x):
    return jax.nn.silu(x)

def _sigmoid(x):
    return jax.nn.sigmoid(x)

def _layernorm(x, axis=-1, eps=1e-05):
    m = jnp.mean(x, axis=axis, keepdims=True)
    v = jnp.var(x, axis=axis, keepdims=True)
    return (x - m) / jnp.sqrt(v + eps)

def _scatter_add(tgt, idx, src, axis=0):
    return tgt.at[idx].add(src)

def _segment_sum(src, seg, n):
    return jax.ops.segment_sum(src, seg, n)
kernel_name = 'mk_perceiver_d1_seqx_r2_bcdeb9'

def setup_inputs(seed: int=0):
    np.random.seed(seed)
    _w = jnp.asarray

    def _rec_inputs():
        import jax
        import jax.numpy as jnp
        _rk = jax.random.key(seed)
        x = 7.22e-05 + 1 * jax.random.normal(jax.random.fold_in(_rk, 1), (16, 64, 512), jnp.float32)
        _lenS = 64 - jax.random.randint(jax.random.fold_in(_rk, 7), (16,), 0, max(1, 64 // 4) + 1, jnp.int32)
        _lenS2 = 1601 - jax.random.randint(jax.random.fold_in(_rk, 8), (16,), 0, max(1, 1601 // 4) + 1, jnp.int32)
        _ctx_1024P = jax.random.normal(jax.random.fold_in(_rk, 11), (16, 16, 512), jnp.float32)
        _ctx_1024c = jax.random.dirichlet(jax.random.fold_in(_rk, 511), 0.3 * jnp.ones((16,), jnp.float32), (16, 1601))
        _ctx_1024t = jnp.einsum('bsk,bkd->bsd', _ctx_1024c, _ctx_1024P)
        _ctx_1024t = _ctx_1024t * jax.lax.rsqrt(jnp.mean(jnp.square(_ctx_1024t)) + 1e-12) * 0.953939
        ctx_1024 = 4.13588e-05 + 0.999923 * (_ctx_1024t + 0.3 * jax.random.normal(jax.random.fold_in(_rk, 611), (16, 1601, 512), jnp.float32))
        _validS = jnp.arange(64)[None, :] < _lenS[:, None]
        _validS2 = jnp.arange(1601)[None, :] < _lenS2[:, None]
        _causal = jnp.tril(jnp.ones((64, 64), dtype=bool))
        mask_1x1xSxS2_ik0 = jnp.where(jnp.broadcast_to(_validS2[0:1, None, None, :], (1, 1, 64, 1601)), 0, 1).astype(jnp.int32)
        return (x, ctx_1024, mask_1x1xSxS2_ik0)
    x, ctx_1024, mask_1x1xSxS2_ik0 = _rec_inputs()

    def _L0_xattn_setup():
        import jax, jax.numpy as jnp
        import numpy as np
        D_MODEL = 512
        H = 16
        D_K = D_MODEL // H
        NEG = -1000000000.0
        key = jax.random.key(seed)
        ks = jax.random.split(key, 7)
        B, S = (4, 1024)
        q = jax.random.normal(ks[0], (B, S, D_MODEL), dtype=jnp.float32)
        k = jax.random.normal(ks[1], (B, S, D_MODEL), dtype=jnp.float32)
        v = jax.random.normal(ks[2], (B, S, D_MODEL), dtype=jnp.float32)
        mask = jnp.tril(jnp.ones((S, S), dtype=jnp.int32))[None, None, :, :]
        scale = 0.02
        w_q = jax.random.normal(ks[3], (D_MODEL, D_MODEL), dtype=jnp.float32) * scale
        w_k = jax.random.normal(ks[4], (D_MODEL, D_MODEL), dtype=jnp.float32) * scale
        w_v = jax.random.normal(ks[5], (D_MODEL, D_MODEL), dtype=jnp.float32) * scale
        w_o = jax.random.normal(ks[6], (D_MODEL, D_MODEL), dtype=jnp.float32) * scale
        return {'q': q, 'k': k, 'v': v, 'mask': mask, 'w_q': w_q, 'w_k': w_k, 'w_v': w_v, 'w_o': w_o}
    _L0_xattn_all = _L0_xattn_setup()
    _L0_xattn_in = {k: v for k, v in _L0_xattn_all.items() if k in ('w_q', 'w_k', 'w_v', 'w_o')}
    del _L0_xattn_all

    def _L0_attn_setup():
        import jax, jax.numpy as jnp
        import numpy as np
        B, N, C = (2, 1024, 512)
        H = 16
        HD = C // H
        R = 16
        LORA_SCALE = 32.0 / R
        ATTN_SCALE = HD ** (-0.5)
        key = jax.random.key(seed)
        ks = jax.random.split(key, 10)
        s = lambda fan_in: 1.0 / np.sqrt(fan_in)
        return {'x': jax.random.normal(ks[0], (B, N, C), dtype=jnp.float32), 'w_qkv': jax.random.normal(ks[1], (C, 3 * C), dtype=jnp.float32) * s(C), 'b_qkv': jax.random.normal(ks[2], (3 * C,), dtype=jnp.float32) * 0.02, 'a_q': jax.random.normal(ks[3], (HD, R), dtype=jnp.float32) * s(HD), 'b_q': jax.random.normal(ks[4], (R, HD), dtype=jnp.float32) * 0.02, 'a_v': jax.random.normal(ks[5], (HD, R), dtype=jnp.float32) * s(HD), 'b_v': jax.random.normal(ks[6], (R, HD), dtype=jnp.float32) * 0.02, 'w_proj': jax.random.normal(ks[7], (C, C), dtype=jnp.float32) * s(C), 'b_proj': jax.random.normal(ks[8], (C,), dtype=jnp.float32) * 0.02}
    _L0_attn_all = _L0_attn_setup()
    _L0_attn_in = {k: v for k, v in _L0_attn_all.items() if k in ('w_qkv', 'b_qkv', 'a_q', 'b_q', 'a_v', 'b_v', 'w_proj', 'b_proj')}
    del _L0_attn_all

    def _L0_ffn_setup():
        import jax, jax.numpy as jnp
        import numpy as np
        B, S, D, DO = (4, 1024, 512, 512)
        E, K = (20, 2)
        key = jax.random.key(seed)
        ks = jax.random.split(key, 6)
        sc_d = 1.0 / np.sqrt(D)
        sc_h = 1.0 / np.sqrt(D // 4)
        return {'x': jax.random.normal(ks[0], (B, S, D), jnp.float32), 'wg1': jax.random.normal(ks[1], (D, D // 4), jnp.float32) * sc_d, 'bg1': jnp.zeros((D // 4,), jnp.float32), 'wg2': jax.random.normal(ks[2], (D // 4, 2 * E), jnp.float32) * sc_h, 'bg2': jnp.zeros((2 * E,), jnp.float32), 'We': jax.random.normal(ks[3], (E, D, DO), jnp.float32) * sc_d, 'be': jnp.zeros((E, DO), jnp.float32)}
    _L0_ffn_all = _L0_ffn_setup()
    _L0_ffn_in = {k: v for k, v in _L0_ffn_all.items() if k in ('wg1', 'bg1', 'wg2', 'bg2', 'We', 'be')}
    del _L0_ffn_all
    return {'x': x, 'ctx_1024': ctx_1024, 'mask_1x1xSxS2_ik0': mask_1x1xSxS2_ik0, 'L0_xattn_w_q': _L0_xattn_in['w_q'], 'L0_xattn_w_k': _L0_xattn_in['w_k'], 'L0_xattn_w_v': _L0_xattn_in['w_v'], 'L0_xattn_w_o': _L0_xattn_in['w_o'], 'L0_attn_w_qkv': _L0_attn_in['w_qkv'], 'L0_attn_b_qkv': _L0_attn_in['b_qkv'], 'L0_attn_a_q': _L0_attn_in['a_q'], 'L0_attn_b_q': _L0_attn_in['b_q'], 'L0_attn_a_v': _L0_attn_in['a_v'], 'L0_attn_b_v': _L0_attn_in['b_v'], 'L0_attn_w_proj': _L0_attn_in['w_proj'], 'L0_attn_b_proj': _L0_attn_in['b_proj'], 'L0_ffn_wg1': _L0_ffn_in['wg1'], 'L0_ffn_bg1': _L0_ffn_in['bg1'], 'L0_ffn_wg2': _L0_ffn_in['wg2'], 'L0_ffn_bg2': _L0_ffn_in['bg2'], 'L0_ffn_We': _L0_ffn_in['We'], 'L0_ffn_be': _L0_ffn_in['be']}

def reference(x, ctx_1024, mask_1x1xSxS2_ik0, L0_xattn_w_q, L0_xattn_w_k, L0_xattn_w_v, L0_xattn_w_o, L0_attn_w_qkv, L0_attn_b_qkv, L0_attn_a_q, L0_attn_b_q, L0_attn_a_v, L0_attn_b_v, L0_attn_w_proj, L0_attn_b_proj, L0_ffn_wg1, L0_ffn_bg1, L0_ffn_wg2, L0_ffn_bg2, L0_ffn_We, L0_ffn_be):
    import jax
    import jax.numpy as jnp

    def _L0_xattn_ref(q, k, v, mask, w_q, w_k, w_v, w_o):
        import jax, jax.numpy as jnp
        import numpy as np
        D_MODEL = 512
        H = 16
        D_K = D_MODEL // H
        NEG = -1000000000.0
        B, S, _ = q.shape

        def proj(x, w):
            return (x @ w.T).reshape(B, -1, H, D_K).transpose(0, 2, 1, 3)
        query = proj(q, w_q)
        key_ = proj(k, w_k)
        value = proj(v, w_v)
        scores = jnp.einsum('bhqd,bhkd->bhqk', query, key_) / jnp.sqrt(jnp.asarray(D_K, dtype=query.dtype))
        scores = jnp.where(mask == 0, jnp.asarray(NEG, dtype=scores.dtype), scores)
        attn = jax.nn.softmax(scores, axis=-1)
        out = jnp.einsum('bhqk,bhkd->bhqd', attn, value)
        out = out.transpose(0, 2, 1, 3).reshape(B, -1, H * D_K)
        return out @ w_o.T

    def _L0_attn_ref(x, w_qkv, b_qkv, a_q, b_q, a_v, b_v, w_proj, b_proj):
        import jax, jax.numpy as jnp
        import numpy as np
        B, N, C = (2, 1024, 512)
        H = 16
        HD = C // H
        R = 16
        LORA_SCALE = 32.0 / R
        ATTN_SCALE = HD ** (-0.5)
        Bb, Nn, Cc = x.shape
        qkv = (x @ w_qkv + b_qkv).reshape(Bb, Nn, 3, H, HD).transpose(2, 0, 3, 1, 4)
        q, k, v = (qkv[0], qkv[1], qkv[2])
        q = q + jnp.einsum('bhnr,rd->bhnd', jnp.einsum('bhnd,dr->bhnr', q, a_q), b_q) * LORA_SCALE
        v = v + jnp.einsum('bhnr,rd->bhnd', jnp.einsum('bhnd,dr->bhnr', v, a_v), b_v) * LORA_SCALE
        attn = jax.nn.softmax(jnp.einsum('bhnd,bhmd->bhnm', q, k) * ATTN_SCALE, axis=-1)
        out = jnp.einsum('bhnm,bhmd->bhnd', attn, v)
        out = out.transpose(0, 2, 1, 3).reshape(Bb, Nn, Cc)
        return out @ w_proj + b_proj

    def _L0_ffn_ref(x, wg1, bg1, wg2, bg2, We, be):
        import jax, jax.numpy as jnp
        import numpy as np
        B, S, D, DO = (4, 1024, 512, 512)
        E, K = (20, 2)
        Bv, Sv, Dv = x.shape
        xf = x.reshape(-1, Dv)
        h = jax.nn.gelu(xf @ wg1 + bg1, approximate=False)
        logits = (xf @ 0.0 + (h @ wg2 + bg2))[:, :E] if False else (h @ wg2 + bg2)[:, :E]
        probs = jax.nn.softmax(logits, axis=-1)
        top_vals, top_idx = jax.lax.top_k(probs, K)
        N = xf.shape[0]
        gates = jnp.zeros((N, E), xf.dtype).at[jnp.arange(N)[:, None], top_idx].set(top_vals)

        def body(y, eb):
            We_e, be_e, g_e = eb
            return (y + g_e[:, None] * (xf @ We_e + be_e), None)
        y0 = jnp.zeros((N, be.shape[-1]), xf.dtype)
        y, _ = jax.lax.scan(body, y0, (We, be, gates.T))
        return y.reshape(Bv, Sv, -1)
    x = x + _L0_xattn_ref(_layernorm(x, axis=-1), ctx_1024, ctx_1024, mask_1x1xSxS2_ik0, L0_xattn_w_q, L0_xattn_w_k, L0_xattn_w_v, L0_xattn_w_o)
    x = x + _L0_attn_ref(_layernorm(x, axis=-1), L0_attn_w_qkv, L0_attn_b_qkv, L0_attn_a_q, L0_attn_b_q, L0_attn_a_v, L0_attn_b_v, L0_attn_w_proj, L0_attn_b_proj)
    x = x + _L0_ffn_ref(_layernorm(x, axis=-1), L0_ffn_wg1, L0_ffn_bg1, L0_ffn_wg2, L0_ffn_bg2, L0_ffn_We, L0_ffn_be)
    return x

_drawn_inputs = setup_inputs


def setup_inputs(seed=0):
    import zlib

    import numpy as np

    out = dict(_drawn_inputs(seed))
    spreads = {'L0_ffn_bg1': (0.0, 0.1), 'L0_ffn_bg2': (0.0, 0.1), 'L0_ffn_be': (0.0, 0.441)}
    factors = {'L0_xattn_w_q': 4.128, 'L0_xattn_w_k': 3.399}
    for name, (base, spread) in spreads.items():
        noise = np.random.default_rng([zlib.crc32(name.encode()), seed]).standard_normal(out[name].shape)
        drawn = base * np.exp(spread * noise) if base else spread * noise
        out[name] = jnp.asarray(drawn.astype(out[name].dtype))
    for name, factor in factors.items():
        out[name] = (out[name] * factor).astype(out[name].dtype)
    return out
```

```python
import concourse.bass as bass
from concourse import mybir
from contextlib import ExitStack


class Queue:

    def __init__(self, name):
        self.name = name
        self.items = []
        self.sem = None
        self.count = 0
        self.seen = {}

    def use(self, sem):
        self.sem, self.count, self.seen = sem, 0, {}

    def wait(self, *tokens):
        for t in tokens:
            if t is None:
                continue
            sem, value = t
            if self.seen.get(id(sem), 0) < value:
                self.seen[id(sem)] = value
                self.items.append(("wait", sem, value))
        return self

    def op(self, fn, inc=True):
        if inc:
            self.count += 1
            self.items.append(("op", fn, self.sem))
            return (self.sem, self.count)
        self.items.append(("op", fn, None))
        return None

    def alone(self, fn):
        if self.count:
            self.wait((self.sem, self.count))
        return self.op(fn)

    def dma(self, fn, sem, at):
        at[sem[1]] = at.get(sem[1], 0) + 16
        self.items.append(("dma", fn, sem[0]))
        return (sem[0], at[sem[1]])

    def run(self, eng):
        scopes = []
        for it in self.items:
            if it[0] == "wait":
                eng.wait_ge(it[1], it[2])
            elif it[0] == "op":
                ins = it[1](eng)
                if it[2] is not None:
                    ins.then_inc(it[2], 1)
            elif it[0] == "dma":
                it[1](eng).then_inc(it[2], 16)
            elif it[0] == "if":
                guard = eng.If(it[1](eng))
                guard.__enter__()
                scopes.append(guard)
            elif it[0] == "endif":
                scopes.pop().__exit__(None, None, None)
            elif it[0] == "do":
                it[1](eng)


def perceiver(nc, t, out):
    f32, f32r, i32, u32 = mybir.dt.float32, mybir.dt.float32r, mybir.dt.int32, mybir.dt.uint32
    ALU, ACT, AX = mybir.AluOpType, mybir.ActivationFunctionType, mybir.AxisListType
    NB, H, D, T, CW, SW, NC_, E = 16, 16, 512, 1024, 404, 101, 4, 20
    EPS = 1e-5
    SCALE = 32.0 ** -0.5

    root = ExitStack()
    pe, act, dve, pool, sp = Queue("pe"), Queue("act"), Queue("dve"), Queue("pool"), Queue("sp")
    engines = (pe, act, dve, pool, sp)
    at = {}

    with root:
        def sem(name):
            return root.enter_context(nc.semaphore(name))

        def sb(name, shape, dt=f32, es=root):
            return es.enter_context(nc.sbuf_tensor(name, shape, dt))

        def dsem(name):
            return (sem(name), name)

        pb = [root.enter_context(nc.psum_tensor(f"bank{i}", [128, 512], f32)) for i in range(8)]

        def new_sems(tag):
            for q in engines:
                q.use(sem(f"s_{q.name}{tag}"))

        def load(dst, src, s, after=()):
            sp.wait(*after)
            return sp.dma(lambda e: e.dma_start(dst, src), s, at)

        cst = sb("cst", [128, 384])
        x_sb = sb("x_sb", [128, 8, D])
        stats = sb("stats", [128, 8, 6])
        mv = sb("mv", [128, 8, 2])
        rstd = sb("rstd", [128, 8])
        ident = cst[:, 0:128]
        iota20 = cst[:, 160:180]

        new_sems("0")
        d_c = dsem("d_c")
        t_cst = load(cst[:, :], t["cst"], d_c)

        def mm3(o, lhs, rhs, start, stop, last=None):
            lh, ll = lhs
            rh, rl = rhs
            pe.op(lambda e: e.matmul(o, lh, rh, start=start, stop=False), inc=False)
            pe.op(lambda e: e.matmul(o, lh, rl, start=False, stop=False), inc=False)
            return pe.op(lambda e: e.matmul(o, ll, rh, start=False, stop=stop), inc=stop)

        def split_rest(dst_lo, src, hi):
            return dve.op(lambda e: e.tensor_tensor(dst_lo, src, hi.bitcast(f32), ALU.subtract))

        def split(raw, hi, lo, t_raw, hi_on=act):
            hi_on.wait(*t_raw)
            if hi_on is act:
                th = act.op(lambda e: e.activation(hi, raw, ACT.Copy))
            else:
                th = hi_on.alone(lambda e: e.tensor_copy(hi, raw))
            dve.wait(th, *t_raw)
            return th, split_rest(lo, raw, hi)

        def layernorm(i, dst, t_x, free, extra=None):
            dve.wait(*t_x)
            a = dve.op(lambda e: e.bn_stats(stats[:, i, :], x_sb[:, i, :]))
            dve.wait(a)
            a = dve.op(lambda e: e.bn_aggr(mv[:, i, :], stats[:, i, :]))
            dve.wait(a)
            a = dve.op(lambda e: e.tensor_scalar(rstd[:, i:i + 1], mv[:, i, 1:2], EPS, None, ALU.add))
            pool.wait(a, t_cst)
            a = pool.alone(lambda e: e.tensor_tensor(rstd[:, i:i + 1], rstd[:, i:i + 1], cst[:, 140:141], ALU.pow))
            if extra is not None:
                dve.wait(a, extra[1])
                a = dve.op(lambda e: e.tensor_tensor(rstd[:, i:i + 1], rstd[:, i:i + 1], extra[0], ALU.mult))
            dve.wait(a, *free)
            return dve.op(lambda e: e.tensor_scalar(dst, x_sb[:, i, :], mv[:, i, 0:1], rstd[:, i:i + 1],
                                                    ALU.subtract, ALU.mult))

        def transposed(i, src, t_src, bank, free, hi, lo):
            pe.wait(*t_src, *free)
            for k in range(4):
                tt = pe.op(lambda e, k=k: e.transpose(bank[:, k * 128:(k + 1) * 128],
                                                      src[:, k * 128:(k + 1) * 128], ident), inc=(k == 3))
            dh = hi[:, :, i * 128:(i + 1) * 128]
            dl = lo[:, :, i * 128:(i + 1) * 128]
            pv = bank[:, :].rearrange("p (k n) -> p k n", k=4)
            act.wait(tt)
            th = act.op(lambda e: e.activation(dh, pv, ACT.Copy))
            dve.wait(th, tt)
            tl = split_rest(dl, pv, dh)
            return th, tl

        acc = sb("acc", [128, NB, 8, 32])
        nm = sb("nm", [128, NB, 8])
        ls = sb("ls", [128, NB, 8])
        lasting = ExitStack()
        wk = [sb(f"wk{j}", [128, 4, D], f32r, lasting) for j in range(2)]
        wv = [sb(f"wv{j}", [128, 4, D], f32r, lasting) for j in range(2)]
        craw = sb("craw", [128, 2, 4, CW], f32, lasting)
        chi = sb("chi", [128, 2, 4, CW], f32r, lasting)
        clo = sb("clo", [128, 2, 4, CW], f32r, lasting)
        qc = sb("qc", [128, 4, T], f32, lasting)
        qh = sb("qh", [128, 2, 4, 128], f32r, lasting)
        ql = sb("ql", [128, 2, 4, 128], f32r, lasting)
        ids = sb("ids", [1, 8], i32, lasting)
        cap = sb("cap", [128, CW], f32, lasting)

        first = ExitStack()
        mska = sb("mska", [128, NC_, CW], i32, first)
        cm = sb("cm", [128, 4], f32, first)
        fl = sb("fl", [128, 16], f32, first)
        rows = sb("rows", [128, 4], f32, first)
        fr = sb("fr", [4, 1], f32, first)
        frow = sb("frow", [1, 32], f32, first)
        wq = [sb(f"wq{j}", [128, 4, D], f32r, first) for j in range(2)]
        wraw = sb("wraw", [128, 2, 4, D], f32, first)
        xt = [sb(f"xt{j}", [128, 4, T], f32r, first) for j in range(2)]
        xn = sb("xn", [128, 2, D], f32, first)

        d_m = [dsem(f"d_m{i}") for i in range(2)]
        d_x = [dsem(f"d_x{i}") for i in range(2)]
        d_w = [dsem(f"d_w{i}") for i in range(2)]
        t_m = [load(mska[64 * h:64 * h + 64, :, :], t["mask"].rearrange("c q k -> q c k"), d_m[h]) for h in range(2)]
        xv = t["x"].rearrange("(i b) q d -> i (b q) d", b=2)
        t_x = [load(x_sb[:, 4 * h:4 * h + 4, :], xv[4 * h:4 * h + 4].rearrange("i p d -> p i d"), d_x[h])
               for h in range(2)]
        t_wq = load(wraw[:, 0], t["wq"], d_w[0])
        t_wk = load(wraw[:, 1], t["wk"], d_w[1])

        for c in range(NC_):
            dve.wait(*t_m)
            a = dve.op(lambda e, c=c: e.tensor_scalar(mska[:, c, :].bitcast(f32), mska[:, c, :], 0.0, None,
                                                      ALU.not_equal))
            dve.wait(a)
            t_cm = dve.op(lambda e, c=c: e.tensor_reduce(cm[:, c:c + 1], mska[:, c, :].bitcast(f32), AX.X, ALU.max))
        dve.wait(t_cm)
        a = dve.op(lambda e: e.tensor_reduce(rows[:, 0:1], cm[:, :], AX.X, ALU.max))
        dve.wait(a)
        t_rs = dve.op(lambda e: e.tensor_scalar(rows[:, 1:2], rows[:, 0:1], SCALE, None, ALU.mult))
        a = dve.op(lambda e: e.tensor_scalar(rows[:, 2:3], rows[:, 0:1], -1.0, 1.0, ALU.mult, ALU.add))
        dve.wait(a)
        t_fl = dve.op(lambda e: e.tensor_scalar(fl[:, 0:4], cm[:, :], rows[:, 2:3], None, ALU.max))
        pe.wait(t_fl, t_cst)
        a = pe.op(lambda e: e.transpose(pb[7][0:4, 0:128], fl[:, 0:4], ident))
        dve.wait(a)
        a = dve.op(lambda e: e.tensor_reduce(fr[:, :], pb[7][0:4, 0:128], AX.X, ALU.max))
        pe.wait(a)
        a = pe.op(lambda e: e.matmul(pb[7][0:1, 0:8], fr[:, :], cst[0:4, 128:136], start=True, stop=True))
        dve.wait(a)
        a = dve.op(lambda e: e.tensor_copy(frow[:, 0:8], pb[7][0:1, 0:8]))
        dve.wait(a, t_cst)
        a = dve.op(lambda e: e.tensor_tensor(frow[:, 8:12], frow[:, 0:4], cst[0:1, 136:140], ALU.mult))
        dve.wait(a)
        for j in range(NC_):
            a = dve.op(lambda e, j=j: e.scalar_tensor_tensor(out=frow[:, 12:16], in0=frow[:, 4:8], scalar=float(j + 1),
                                                             in1=frow[:, 8:12], op0=ALU.is_equal, op1=ALU.mult,
                                                             accum_out=frow[:, 16 + j:17 + j]))
            dve.wait(a)
        a = dve.op(lambda e: e.tensor_copy(ids[:, 0:4], frow[:, 16:20]))
        t_ids = dve.op(lambda e: e.tensor_copy(ids[:, 4:5], frow[:, 7:8]))

        regs = {}

        def read_count(q):
            q.wait(t_ids)
            q.items.append(("do", lambda e: regs.__setitem__(q.name, e.value_load(ids[0:1, 4:5], min_val=1,
                                                                                  max_val=4))))

        def read_chunk(j):
            sp.wait(t_ids)
            sp.items.append(("do", lambda e: regs.__setitem__("chunk", e.value_load(ids[0:1, j:j + 1], min_val=0,
                                                                                    max_val=3))))

        t_wqs = split(wraw[:, 0], wq[0][:, :, :], wq[1][:, :, :], [t_wq])
        t_wks = split(wraw[:, 1], wk[0][:, :, :], wk[1][:, :, :], [t_wk])
        t_wv = load(wraw[:, 0], t["wv"], d_w[0], after=t_wqs)
        t_wvs = split(wraw[:, 0], wv[0][:, :, :], wv[1][:, :, :], [t_wv])

        t_z = [pool.alone(lambda e: e.memset(qh[:, :, :, :].bitcast(f32), 0.0)),
               pool.alone(lambda e: e.memset(ql[:, :, :, :].bitcast(f32), 0.0))]

        t_xt = []
        free_xn, free_b = [None, None], [None, None]
        for i in range(8):
            tn = layernorm(i, xn[:, i % 2, :], [t_x[i // 4]], [free_xn[i % 2]], (rows[:, 1:2], t_rs))
            th, tl = transposed(i, xn[:, i % 2, :], [tn, t_cst], pb[5 + i % 2], [free_b[i % 2]], xt[0], xt[1])
            free_xn[i % 2] = th
            free_b[i % 2] = tl
            t_xt.append((th, tl))
        t_q = None
        free_b = [None] * 3
        n = 0
        for hf in range(2):
            for m in range(4):
                bank = pb[n % 3]
                pe.wait(*t_wqs, *t_xt[4 * hf + 3], free_b[n % 3])
                for k in range(4):
                    tt = mm3(bank[:, :], [w[:, k, m * 128:(m + 1) * 128] for w in wq],
                             [v[:, k, hf * 512:(hf + 1) * 512] for v in xt], k == 0, k == 3)
                act.wait(tt)
                free_b[n % 3] = t_q = act.op(lambda e, m=m, hf=hf, bank=bank: e.activation(
                    qc[:, m, hf * 512:(hf + 1) * 512], bank[:, :], ACT.Copy))
                n += 1
        t_pe0 = tt
        first.close()

        second = ExitStack()
        kk = [sb(f"kk{j}", [128, 4, CW], f32r, second) for j in range(2)]
        vv = sb("vv", [SW, 4, D], f32, second)
        pp = sb("pp", [128, 8, CW], f32, second)
        pt = sb("pt", [SW, 4, 4, 128], f32, second)
        mski = sb("mski", [128, CW], i32, second)
        excl = sb("excl", [128, CW], f32, second)
        nmn = sb("nmn", [128, 2, 8], f32, second)
        lsn = sb("lsn", [128, 2, 8], f32, second)
        cor = sb("cor", [128, 2, 8], f32, second)

        d_ctx = [dsem(f"d_ctx{i}") for i in range(2)]
        d_cap = dsem("d_cap")
        for q in engines:
            read_count(q)

        st = {"kv": [t_q, t_q, t_q], "kvn": 0, "S": [None, None], "T": [None, None], "O": None, "t_split": {},
              "craw": [None, None], "cfree": [None, None], "qd": {}, "qfree": [None, None],
              "P": [t_pe0] * 8, "PT": [None] * 4, "V": None, "K": [None] * 4, "state": [None] * NB, "cap": None,
              "capread": None}

        def prepare_ctx(n, b):
            s = n % 2
            sp.wait(*(st["craw"][s] or ()))
            tl = sp.dma(lambda e: e.dma_start(craw[:, s], t["ctx"][b, bass.ds(regs["chunk"], 1)].rearrange(
                "a p k n -> (a p) k n")), d_ctx[s], at)
            pool.wait(tl, st["cfree"][s])
            th = pool.alone(lambda e: e.tensor_copy(chi[:, s], craw[:, s]))
            dve.wait(th, tl, st["cfree"][s])
            tlo = split_rest(clo[:, s], craw[:, s], chi[:, s])
            st["craw"][s] = (th, tlo)
            st["t_split"][n] = (th, tlo)
            pool.wait(t_q, st["qfree"][s], *t_z)
            tq = []
            for r in range(4):
                src = qc[32 * r:32 * r + 32, :, b * 64:b * 64 + 64]
                dh = qh[32 * r:32 * r + 32, s, :, 64 * (r % 2):64 * (r % 2) + 64]
                dl = ql[32 * r:32 * r + 32, s, :, 64 * (r % 2):64 * (r % 2) + 64]
                tq.append((pool.alone(lambda e, dh=dh, src=src: e.tensor_copy(dh, src)), dl, src, dh))
            for th_, dl, src, dh in tq:
                pool.wait(th_)
                tt_ = pool.alone(lambda e, dl=dl, src=src, dh=dh: e.tensor_tensor(dl, src, dh.bitcast(f32),
                                                                               ALU.subtract))
            st["qd"][n] = tt_

        def take_bank():
            i = st["kvn"] % 3
            st["kvn"] += 1
            return i, st["kv"][i]

        def k_part(n, g):
            i, free = take_bank()
            s = n % 2
            pe.wait(*t_wks, *st["t_split"][n], free)
            for k in range(4):
                tt = mm3(pb[i][:, 0:CW], [w[:, k, g * 128:(g + 1) * 128] for w in wk],
                         [chi[:, s, k, :], clo[:, s, k, :]], k == 0, k == 3)
            act.wait(tt, st["K"][g])
            th = act.op(lambda e: e.activation(kk[0][:, g, :], pb[i][:, 0:CW], ACT.Copy))
            dve.wait(tt, th, st["K"][g])
            tl = split_rest(kk[1][:, g, :], pb[i][:, 0:CW], kk[0][:, g, :])
            st["kv"][i] = tl
            return th, tl

        def v_part(n, i4):
            i, free = take_bank()
            s = n % 2
            pe.wait(*t_wvs, free)
            for k in range(4):
                tt = mm3(pb[i][0:SW, :], [c[:, s, k, i4 * SW:(i4 + 1) * SW] for c in (chi, clo)],
                         [w[:, k, :] for w in wv], k == 0, k == 3)
            act.wait(tt, st["V"])
            st["kv"][i] = tv = act.op(lambda e: e.activation(vv[:, i4, :], pb[i][0:SW, :], ACT.Copy))
            st["cfree"][s] = tt
            return tv

        def s_part(n, b, seg, p8, t_k):
            g, u = divmod(p8, 2)
            s = n % 2
            bank = pb[3 + u]
            pe.wait(*t_k[g], st["qd"][n], st["S"][u])
            r = slice(64 * u, 64 * u + 64)
            tt = mm3(bank[:, 0:CW], [q[r, s, g, :] for q in (qh, ql)], [w[r, g, :] for w in kk], True, True)
            st["K"][g] = tt
            st["qfree"][s] = tt
            dve.wait(tt, st["P"][p8], st["cap"])
            dst = nm[:, b, p8:p8 + 1] if seg == 0 else nmn[:, s, p8:p8 + 1]
            if seg:
                dve.wait(st["state"][b])
            ini = 3e38 if seg == 0 else nm[:, b, p8:p8 + 1]
            st["S"][u] = td = dve.op(lambda e: e.tensor_tensor_reduce(
                out=pp[:, p8, :], in0=bank[:, 0:CW], in1=cap[:, :], scale=-1.0, scalar=ini,
                op0=ALU.add, op1=ALU.min, accum_out=dst))
            act.wait(td)
            sdst = ls[:, b, p8:p8 + 1] if seg == 0 else lsn[:, s, p8:p8 + 1]
            st["capread"] = td
            return td, act.op(lambda e: e.activation(pp[:, p8, :], pp[:, p8, :], ACT.Exp, bias=dst, scale=-1.0,
                                                     accum_out=sdst))

        def t_part(n, p8, t_e):
            u = p8 % 2
            pe.wait(t_e, st["T"][u], t_cst)
            bank = pb[5 + u]
            for i4 in range(4):
                tt = pe.op(lambda e, i4=i4: e.transpose(bank[0:SW, i4 * 128:(i4 + 1) * 128],
                                                        pp[:, p8, i4 * SW:(i4 + 1) * SW], ident), inc=(i4 == 3))
            st["P"][p8] = tt
            slot = p8 % 4
            dst = pt[:, slot, :, :].rearrange("p a c -> p (a c)")
            if u:
                act.wait(tt, st["PT"][slot])
                st["T"][u] = te = act.op(lambda e: e.activation(dst, bank[0:SW, :], ACT.Copy))
            else:
                dve.wait(tt, st["PT"][slot])
                st["T"][u] = te = dve.op(lambda e: e.tensor_copy(dst, bank[0:SW, :]))
            return te

        def pv_part(n, b, p8, te, t_v):
            slot = p8 % 4
            pe.wait(te, *t_v)
            if p8 == 0:
                pe.wait(st["O"])
            for i4 in range(4):
                tt = pe.op(lambda e, i4=i4: e.matmul(pb[7][:, p8 * 64:(p8 + 1) * 64], pt[:, slot, i4, :],
                                                     vv[:, i4, p8 * 64:(p8 + 1) * 64], start=(i4 == 0),
                                                     stop=(i4 == 3)), inc=(i4 == 3))
            st["PT"][slot] = tt
            st["V"] = tt
            return tt

        def o_part(n, b, seg, t_pv, t_exp, t_max):
            ov = pb[7][:, :].rearrange("p (t c) -> p t c", t=8)
            s = n % 2
            if seg == 0:
                dve.wait(t_pv)
                for h in range(2):
                    r = slice(64 * h, 64 * h + 64)
                    tt = dve.op(lambda e, r=r, h=h: e.tensor_copy(acc[r, b, :, :], ov[r, :, 32 * h:32 * h + 32]))
                st["O"] = st["state"][b] = tt
                return
            dve.wait(t_max, t_exp, st["state"][b])
            a = dve.op(lambda e: e.tensor_tensor(cor[:, s, :], nmn[:, s, :], nm[:, b, :], ALU.subtract))
            act.wait(a)
            c = act.op(lambda e: e.activation(cor[:, s, :], cor[:, s, :], ACT.Exp))
            dve.wait(c)
            a = dve.op(lambda e: e.tensor_copy(nm[:, b, :], nmn[:, s, :]))
            a = dve.op(lambda e: e.tensor_tensor(ls[:, b, :], ls[:, b, :], cor[:, s, :], ALU.mult))
            a2 = dve.op(lambda e: e.tensor_tensor(acc[:, b, :, :], acc[:, b, :, :],
                                                  cor[:, s, :].unsqueeze(2).to_broadcast([128, 8, 32]), ALU.mult))
            dve.wait(a, a2, t_pv)
            dve.op(lambda e: e.tensor_tensor(ls[:, b, :], ls[:, b, :], lsn[:, s, :], ALU.add))
            for h in range(2):
                r = slice(64 * h, 64 * h + 64)
                tt = dve.op(lambda e, r=r, h=h: e.tensor_tensor(acc[r, b, :, :], acc[r, b, :, :],
                                                                ov[r, :, 32 * h:32 * h + 32], ALU.add))
            st["O"] = st["state"][b] = tt

        def segment(seg):
            read_chunk(seg)
            sp.wait(st["capread"], st["cap"])
            if seg == 0:
                sp.wait(t_pe0, t_q, *t_wvs)
            for src, dst in ((t["mask"], mski), (t["excl"], None)):
                if dst is not None:
                    for h in range(2):
                        tm = sp.dma(lambda e, h=h: e.dma_start(
                            mski[64 * h:64 * h + 64, :],
                            t["mask"][bass.ds(regs["chunk"], 1)].rearrange("a q k -> (a q) k")), d_cap, at)
                else:
                    tm = sp.dma(lambda e: e.dma_start(
                        excl[:, :], t["excl"][bass.ds(regs["chunk"], 1)].rearrange("a q k -> (a q) k")), d_cap, at)
            dve.wait(tm, st["capread"])
            a = dve.op(lambda e: e.tensor_scalar(cap[:, :], mski[:, :], 0.0, 1e9, ALU.not_equal, ALU.mult))
            dve.wait(a)
            st["cap"] = dve.op(lambda e: e.scalar_tensor_tensor(out=cap[:, :], in0=cap[:, :], scalar=-1e9,
                                                                in1=excl[:, :], op0=ALU.add, op1=ALU.add))
            base = 16 * seg
            prepare_ctx(base, 0)
            old = None
            for b in range(NB + 1):
                n = base + b
                t_k, evac = [], {}
                for g in range(4):
                    if b < NB:
                        t_k.append(k_part(n, g))
                    if old is not None:
                        if g:
                            for p8 in (2 * g - 2, 2 * g - 1):
                                pv_part(old["n"], old["b"], p8, evac[p8], old["v"])
                        for p8 in (2 * g, 2 * g + 1):
                            evac[p8] = t_part(old["n"], p8, old["e"][p8])
                if old is not None:
                    for p8 in (6, 7):
                        t_pv = pv_part(old["n"], old["b"], p8, evac[p8], old["v"])
                    o_part(old["n"], old["b"], seg, t_pv, old["e"][7], old["m"])
                if b == NB:
                    break
                if b + 1 < NB:
                    prepare_ctx(n + 1, b + 1)
                t_v, t_e = [], []
                for g in range(4):
                    for p8 in (2 * g, 2 * g + 1):
                        t_max, te = s_part(n, b, seg, p8, t_k)
                        t_e.append(te)
                    t_v.append(v_part(n, g))
                old = {"n": n, "b": b, "v": t_v, "e": t_e, "m": t_max}

        segment(0)
        for seg in range(1, NC_):
            for q in engines:
                q.items.append(("if", lambda e, q=q, seg=seg: regs[q.name] > seg))
            segment(seg)
        for seg in range(1, NC_):
            for q in engines:
                q.items.append(("endif",))
        s_bar = sem("s_bar")
        for q in engines:
            q.items.append(("do", lambda e: e.drain().then_inc(s_bar, 1)))
        new_sems("1")
        for q in engines:
            q.items.append(("wait", s_bar, 5))

        second.close()
        lasting.close()

        xt = [sb(f"xu{j}", [128, 4, T], f32r) for j in range(2)]
        xn = sb("xm", [128, 2, D])
        raw = sb("raw", [128, 2, 4, D])
        wh = [sb(f"wh{j}", [128, 2, 4, D], f32r) for j in range(2)]
        bro = sb("bro", [128, D + 4 * 4 + 40])
        bproj, bcol, bg2 = bro[:, 0:D], bro[:, D:D + 16], bro[:, D + 16:D + 36]
        d_raw = [dsem(f"d_raw{i}") for i in range(2)]
        d_b = dsem("d_b")
        t_bro = load(bro[:, :], t["bro"], d_b)
        ws = {"n": 0, "rawfree": [None, None], "whfree": [None, None]}

        def fetch(src):
            n = ws["n"]
            ws["n"] += 1
            s = n % 2
            return s, load(raw[:, s], src, d_raw[s], after=ws["rawfree"][s] or ())

        def weight(src):
            s, tl = fetch(src)
            act.wait(ws["whfree"][s])
            dve.wait(ws["whfree"][s])
            tt = split(raw[:, s], wh[0][:, s], wh[1][:, s], [tl])
            ws["rawfree"][s] = tt
            return s, tt

        bank = {"n": 0, "free": [None] * 3}

        def take(banks=(0, 1, 2)):
            i = bank["n"] % 3
            bank["n"] += 1
            return i, bank["free"][i]

        def heads_to_features(i, t_acc, bias, free):
            bk = pb[5 + i % 2]
            pe.wait(*t_acc, free[i % 2])
            for j in range(4):
                b2, g2 = divmod(j, 2)
                tt = pe.op(lambda e, j=j, b2=b2, g2=g2: e.transpose(
                    bk[:, j * 128:(j + 1) * 128],
                    acc[:, 2 * i + b2, 4 * g2:4 * g2 + 4, :].rearrange("p a c -> p (a c)"), ident), inc=(j == 3))
            src = bk[:, :].rearrange("p (b c q) -> p c b q", b=2, c=4)
            dst = [x[:, :, i * 128:(i + 1) * 128].rearrange("p c (b q) -> p c b q", b=2) for x in xt]
            act.wait(tt)
            if bias is None:
                th = act.op(lambda e: e.activation(dst[0], src, ACT.Copy))
                dve.wait(th, tt)
                tl = split_rest(dst[1], src, dst[0])
            else:
                act.wait(bias[1])
                for c in range(4):
                    th = act.op(lambda e, c=c: e.activation(dst[0][:, c], src[:, c], ACT.Identity,
                                                            bias=bias[0][:, c:c + 1]))
                dve.wait(th, tt, bias[1])
                for c in range(4):
                    tl = dve.op(lambda e, c=c: e.scalar_tensor_tensor(
                        out=dst[1][:, c], in0=src[:, c], scalar=bias[0][:, c:c + 1], in1=dst[0][:, c].bitcast(f32),
                        op0=ALU.add, op1=ALU.subtract))
            free[i % 2] = tl
            return th, tl

        def project(i, s, t_w, t_in, then):
            b_, free = take()
            pe.wait(*t_w, *t_in, free)
            for k in range(4):
                tt = mm3(pb[b_][:, :], [v[:, k, i * 128:(i + 1) * 128] for v in xt], [w[:, s, k, :] for w in wh],
                         k == 0, k == 3)
            bank["free"][b_] = r = then(pb[b_], tt)
            return r

        def feature_major(m, hf, s, t_w, t_in, then):
            b_, free = take()
            pe.wait(*t_w, *t_in, free)
            for k in range(4):
                tt = mm3(pb[b_][:, :], [w[:, s, k, m * 128:(m + 1) * 128] for w in wh],
                         [v[:, k, hf * 512:(hf + 1) * 512] for v in xt], k == 0, k == 3)
            ws["whfree"][s] = tt
            bank["free"][b_] = r = then(pb[b_], tt)
            return r

        def residual(i, bias):
            def then(bk, tt):
                dve.wait(tt)
                r = dve.op(lambda e: e.tensor_tensor(x_sb[:, i, :], x_sb[:, i, :], bk[:, :], ALU.add))
                if bias:
                    dve.wait(r, t_bro)
                    r = dve.op(lambda e: e.tensor_tensor(x_sb[:, i, :], x_sb[:, i, :], bproj, ALU.add))
                return r
            return then

        def norm_all(t_x):
            out_, fx, fb = [], [None, None], [None, None]
            for i in range(8):
                tn = layernorm(i, xn[:, i % 2, :], [t_x[i]], [fx[i % 2]])
                th, tl = transposed(i, xn[:, i % 2, :], [tn], pb[5 + i % 2], [fb[i % 2]], xt[0], xt[1])
                fx[i % 2], fb[i % 2] = th, tl
                out_.append((th, tl))
            return out_

        s_wo, t_wo = weight(t["wo"])
        a = dve.op(lambda e: e.reciprocal(ls[:, :, :], ls[:, :, :]))
        free = [None, None]
        t_x1 = []
        for i in range(8):
            dve.wait(a)
            ta = dve.op(lambda e, i=i: e.tensor_tensor(
                acc[:, 2 * i:2 * i + 2, :, :], acc[:, 2 * i:2 * i + 2, :, :],
                ls[:, 2 * i:2 * i + 2, :].unsqueeze(3).to_broadcast([128, 2, 8, 32]), ALU.mult))
            ti = heads_to_features(i, [ta], None, free)
            t_x1.append(project(i, s_wo, t_wo, ti, residual(i, False)))
        ws["whfree"][s_wo] = (pe.sem, pe.count)

        mid = ExitStack()
        lora = sb("lora", [16, 4, 128], f32, mid)
        mbd = sb("mbd", [128, 2, 128], f32, mid)
        bl = sb("bl", [128, 8], f32, mid)
        qT = sb("qT", [128, 4, T], f32, mid)
        kT = sb("kT", [128, 4, T], f32, mid)
        v2 = sb("v2", [128, 8, D], f32, mid)
        qd = sb("qd", [128, 2, 2, 4, 128], f32, mid)
        p2 = sb("p2", [128, 2, 8, 2, 64], f32, mid)
        pt2 = sb("pt2", [128, 8, 128], f32, mid)
        mx2 = sb("mx2", [128, 2, 16], f32, mid)
        ls2 = sb("ls2", [128, 2, 16], f32, mid)
        t_lo = load(lora[:, :, :], t["lora"], d_b)
        t_z = pool.alone(lambda e: e.memset(qd[:, :, :, :, :], 0.0))
        pe.wait(t_lo)
        for j in range(2):
            tt = pe.op(lambda e, j=j: e.matmul(pb[7][:, j * 128:(j + 1) * 128], lora[:, 2 * j, :],
                                               lora[:, 2 * j + 1, :], start=True, stop=True))
        for j in range(2):
            dve.wait(tt, t_cst)
            a = dve.op(lambda e, j=j: e.tensor_tensor(mbd[:, j, :], pb[7][:, j * 128:(j + 1) * 128], cst[:, 256:384],
                                                      ALU.mult))
            dve.wait(a)
            t_mbd = dve.op(lambda e, j=j: e.tensor_tensor(mbd[:, j, :], mbd[:, j, :], ident, ALU.add))
        pe.wait(t_mbd, t_bro)
        for c in range(4):
            pe.op(lambda e, c=c: e.matmul(pb[7][:, 256 + c:257 + c], mbd[:, 0, :], bcol[:, c:c + 1], start=True,
                                          stop=True), inc=False)
            tt = pe.op(lambda e, c=c: e.matmul(pb[7][:, 260 + c:261 + c], mbd[:, 1, :], bcol[:, 8 + c:9 + c],
                                               start=True, stop=True), inc=(c == 3))
        dve.wait(tt)
        t_bl = dve.op(lambda e: e.tensor_copy(bl[:, :], pb[7][:, 256:264]))

        t_xt = norm_all(t_x1)

        def weight_lora(src, j):
            s, tl = fetch(src)
            for k in range(4):
                b_, free_ = take()
                pe.wait(tl, t_mbd, free_)
                for g in range(4):
                    tt_ = pe.op(lambda e, g=g, k=k, b_=b_: e.matmul(
                        pb[b_][:, g * 128:(g + 1) * 128], raw[:, s, g, k * 128:(k + 1) * 128], mbd[:, j, :],
                        start=True, stop=True), inc=(g == 3))
                act.wait(tt_, ws["whfree"][s])
                th = act.op(lambda e, k=k, b_=b_: e.activation(wh[0][:, s, k, :], pb[b_][:, :], ACT.Copy))
                dve.wait(th, tt_, ws["whfree"][s])
                bank["free"][b_] = tlo = split_rest(wh[1][:, s, k, :], pb[b_][:, :], wh[0][:, s, k, :])
            ws["rawfree"][s] = (tt_,)
            return s, (th, tlo)

        def biased(dst, col, t_col):
            def then(bk, tt):
                act.wait(tt, t_col)
                return act.op(lambda e: e.activation(dst, bk[:, :], ACT.Identity, bias=col))
            return then

        def copied(dst):
            def then(bk, tt):
                act.wait(tt)
                return act.op(lambda e: e.activation(dst, bk[:, :], ACT.Copy))
            return then

        s_, tw = weight_lora(t["w2q"], 0)
        for hf in range(2):
            for m in range(4):
                t_qT = feature_major(m, hf, s_, tw, t_xt[4 * hf + 3], biased(
                    qT[:, m, hf * 512:(hf + 1) * 512], bl[:, m:m + 1], t_bl))
        s_, tw = weight(t["w2k"])
        for hf in range(2):
            for m in range(4):
                t_kT = feature_major(m, hf, s_, tw, (), biased(
                    kT[:, m, hf * 512:(hf + 1) * 512], bcol[:, 4 + m:5 + m], t_bro))
        s_, tw = weight_lora(t["w2v"], 1)
        for i in range(8):
            t_v2 = project(i, s_, tw, (), copied(v2[:, i, :]))
        ws["whfree"][s_] = t_lastv = (pe.sem, pe.count)
        s_wp, t_wp = weight(t["wproj"])

        fr2 = {"S": [None, None], "T": [None, None], "O": [bank["free"][2], None], "qd": [None, None],
               "p2": [None, None], "pt2": None, "h": [None, None]}
        t_x2 = []
        for i in range(8):
            s = i % 2
            pool.wait(t_qT, fr2["qd"][s], t_z)
            for b2 in range(2):
                for r in range(4):
                    tq = pool.alone(lambda e, b2=b2, r=r, s=s, i=i: e.tensor_copy(
                        qd[32 * r:32 * r + 32, s, b2, :, 64 * (r % 2):64 * (r % 2) + 64],
                        qT[32 * r:32 * r + 32, :, (2 * i + b2) * 64:(2 * i + b2 + 1) * 64]))
            t_sub = []
            for u in range(2):
                pe.wait(tq, t_kT, fr2["S"][u])
                for b2 in range(2):
                    for g in range(4):
                        r = slice(64 * u, 64 * u + 64)
                        tt = pe.op(lambda e, b2=b2, g=g, r=r, u=u, s=s, i=i: e.matmul(
                            pb[3 + u][:, (b2 * 4 + g) * 64:(b2 * 4 + g + 1) * 64], qd[r, s, b2, g, :],
                            kT[r, g, (2 * i + b2) * 64:(2 * i + b2 + 1) * 64], start=True, stop=True),
                            inc=(b2 == 1 and g == 3))
                fr2["qd"][s] = tt
                src = pb[3 + u][:, :].rearrange("p (c k) -> p c k", k=64)
                dve.wait(tt)
                a = dve.op(lambda e, u=u, s=s, src=src: e.tensor_reduce(mx2[:, s, 8 * u:8 * u + 8], src, AX.X,
                                                                        ALU.max))
                dve.wait(a, fr2["p2"][s])
                for b2 in range(2):
                    tb = dve.op(lambda e, u=u, s=s, b2=b2, src=src: e.tensor_tensor(
                        p2[:, s, u:8:2, b2, :], src[:, 4 * b2:4 * b2 + 4, :],
                        mx2[:, s, 8 * u + 4 * b2:8 * u + 4 * b2 + 4].unsqueeze(2).to_broadcast([128, 4, 64]),
                        ALU.subtract))
                fr2["S"][u] = tb
            pv = p2[:, s].rearrange("p t b k -> p (t b k)")
            act.wait(tb)
            te = act.op(lambda e, pv=pv: e.activation(pv, pv, ACT.Exp, scale=SCALE))
            dve.wait(te)
            a = dve.op(lambda e, s=s: e.tensor_reduce(ls2[:, s, :], p2[:, s].rearrange("p t b k -> p (t b) k"),
                                                      AX.X, ALU.add))
            dve.wait(a)
            t_rl = dve.op(lambda e, s=s: e.reciprocal(ls2[:, s, :], ls2[:, s, :]))
            ev = []
            for h in range(2):
                pe.wait(te, fr2["T"][h])
                for j in range(4):
                    tt = pe.op(lambda e, h=h, j=j, s=s: e.transpose(
                        pb[5 + h][:, j * 128:(j + 1) * 128],
                        p2[:, s, 4 * h + j].rearrange("p b k -> p (b k)"), ident), inc=(j == 3))
                dst = pt2[:, 4 * h:4 * h + 4, :].rearrange("p a c -> p (a c)")
                if h:
                    act.wait(tt, fr2["pt2"])
                    w_ = act.op(lambda e, dst=dst, h=h: e.activation(dst, pb[5 + h][:, :], ACT.Copy))
                else:
                    dve.wait(tt, fr2["pt2"])
                    w_ = dve.op(lambda e, dst=dst, h=h: e.tensor_copy(dst, pb[5 + h][:, :]))
                fr2["T"][h] = w_
                ev.append(w_)
            fr2["p2"][s] = tt
            t_acc = []
            for b2 in range(2):
                bk = pb[(7, 2)[b2]]
                pe.wait(*ev, t_v2, t_bl, fr2["O"][b2], bank["free"][2])
                for p8 in range(8):
                    r = slice(64 * b2, 64 * b2 + 64)
                    tt = pe.op(lambda e, p8=p8, r=r, bk=bk, i=i: e.matmul(
                        bk[:, p8 * 64:(p8 + 1) * 64], pt2[r, p8, :], v2[r, i, p8 * 64:(p8 + 1) * 64],
                        start=True, stop=True), inc=(p8 == 7))
                fr2["pt2"] = tt
                ov = bk[:, :].rearrange("p (t c) -> p t c", t=8)
                lv = ls2[:, s, :].rearrange("p (t b) -> p t b", b=2)
                dve.wait(tt, t_rl)
                for h in range(2):
                    r = slice(64 * h, 64 * h + 64)
                    w_ = dve.op(lambda e, r=r, h=h, b2=b2, i=i, ov=ov, lv=lv: e.tensor_tensor(
                        acc[r, 2 * i + b2, :, :], ov[r, :, 32 * h:32 * h + 32],
                        lv[r, :, b2:b2 + 1].to_broadcast([64, 8, 32]), ALU.mult))
                fr2["O"][b2] = w_
                t_acc.append(w_)
            pe.wait(t_lastv)
            fr2["T"] = list(fr2["T"])
            ti = heads_to_features(i, t_acc + [fr2["T"][i % 2]], (bl[:, 4:8], t_bl), fr2["h"])
            fr2["T"][i % 2] = ti[1]
            b_ = i % 2
            pe.wait(*t_wp, *ti, bank["free"][b_])
            for k in range(4):
                tt = mm3(pb[b_][:, :], [v[:, k, i * 128:(i + 1) * 128] for v in xt],
                         [w[:, s_wp, k, :] for w in wh], k == 0, k == 3)
            bank["free"][b_] = tr = residual(i, True)(pb[b_], tt)
            t_x2.append(tr)
        ws["whfree"][s_wp] = tt
        bank["free"][2] = fr2["O"][1]
        mid.close()

        g1raw = sb("g1raw", [128, 4, 128])
        g1 = [sb(f"g1{j}", [128, 4, 128], f32r) for j in range(2)]
        gw = sb("gw", [128, 24])
        be = sb("be", [E, D])
        hT = sb("hT", [128, T])
        pr = sb("pr", [128, 8, E])
        gt = sb("gt", [128, 8, E])
        mg = sb("mg", [128, 8, 8])
        mi = sb("mi", [128, 8, 8], u32)
        mf = sb("mf", [128, 8, 8])
        sg = sb("sg", [128, 8])
        gT = sb("gT", [E, T])
        dve.wait(t_x2[7])
        d_g = [dsem(f"d_g{i}") for i in range(3)]
        t_g1 = load(g1raw[:, :, :], t["wg1"], d_g[0], after=[t_x2[7]])
        t_gw = load(gw[:, :], t["wg2"], d_g[1])
        t_be = load(be[:, :], t["be"], d_g[2])
        act.wait(t_x2[7])
        t_g1s = split(g1raw[:, :, :], g1[0][:, :, :], g1[1][:, :, :], [t_g1])
        t_xt = norm_all(t_x2)
        for hf in range(2):
            b_, fr_ = take()
            pe.wait(*t_g1s, *t_xt[4 * hf + 3], fr_)
            for k in range(4):
                tt = mm3(pb[b_][:, :], [w[:, k, :] for w in g1], [v[:, k, hf * 512:(hf + 1) * 512] for v in xt],
                         k == 0, k == 3)
            act.wait(tt, t_gw)
            bank["free"][b_] = t_h = act.op(lambda e, b_=b_, hf=hf: e.activation(
                hT[:, hf * 512:(hf + 1) * 512], pb[b_][:, :], ACT.Gelu, bias=gw[:, 20:21]))
        pe.wait(t_h, t_gw)
        for i in range(8):
            tt = pe.op(lambda e, i=i: e.matmul(pb[7][:, i * E:(i + 1) * E], hT[:, i * 128:(i + 1) * 128],
                                               gw[:, 0:20], start=True, stop=True), inc=(i == 7))
        dve.wait(tt, t_bro)
        lg = pb[7][:, 0:8 * E].rearrange("p (i e) -> p i e", e=E)
        a = dve.op(lambda e: e.tensor_tensor(pr[:, :, :], lg, bg2.unsqueeze(1).to_broadcast([128, 8, E]), ALU.add))
        dve.wait(a)
        a = dve.op(lambda e: e.tensor_reduce(sg[:, :], pr[:, :, :], AX.X, ALU.max))
        dve.wait(a)
        a = dve.op(lambda e: e.tensor_tensor(pr[:, :, :], pr[:, :, :],
                                             sg[:, :].unsqueeze(2).to_broadcast([128, 8, E]), ALU.subtract))
        act.wait(a)
        a = act.op(lambda e: e.activation(pr[:, :, :], pr[:, :, :], ACT.Exp))
        dve.wait(a)
        a = dve.op(lambda e: e.tensor_reduce(sg[:, :], pr[:, :, :], AX.X, ALU.add))
        dve.wait(a)
        a = dve.op(lambda e: e.reciprocal(sg[:, :], sg[:, :]))
        dve.wait(a)
        a = dve.op(lambda e: e.tensor_tensor(pr[:, :, :], pr[:, :, :],
                                             sg[:, :].unsqueeze(2).to_broadcast([128, 8, E]), ALU.mult))
        dve.wait(a)
        for i in range(8):
            a = dve.op(lambda e, i=i: e.max(out=mg[:, i, :], in_=pr[:, i, :]))
        dve.wait(a)
        for i in range(8):
            a = dve.op(lambda e, i=i: e.max_index(mi[:, i, :], mg[:, i, :], pr[:, i, :]))
        dve.wait(a)
        a = dve.op(lambda e: e.tensor_copy(mf[:, :, :], mi[:, :, :]))
        dve.wait(a)
        for i in range(8):
            a = dve.op(lambda e, i=i: e.tensor_scalar(gt[:, i, :], iota20, mf[:, i, 0:1], None, ALU.is_equal))
        dve.wait(a)
        for i in range(8):
            a = dve.op(lambda e, i=i: e.scalar_tensor_tensor(out=gt[:, i, :], in0=iota20, scalar=mf[:, i, 1:2],
                                                             in1=gt[:, i, :], op0=ALU.is_equal, op1=ALU.add))
        dve.wait(a)
        t_gt = dve.op(lambda e: e.tensor_tensor(gt[:, :, :], gt[:, :, :], pr[:, :, :], ALU.mult))

        pe.wait(t_gt)
        for hf in range(2):
            for j in range(4):
                i = 4 * hf + j
                tt = pe.op(lambda e, i=i, j=j, hf=hf: e.transpose(pb[5 + hf][0:E, j * 128:(j + 1) * 128],
                                                                  gt[:, i, :], ident), inc=(j == 3))
            dve.wait(tt)
            t_gT = dve.op(lambda e, hf=hf: e.tensor_copy(gT[:, hf * 512:(hf + 1) * 512], pb[5 + hf][0:E, :]))
        t_y = []
        for i in range(8):
            b_, fr_ = take()
            pe.wait(t_gT, t_be, fr_)
            tt = pe.op(lambda e, i=i, b_=b_: e.matmul(pb[b_][:, :], gT[:, i * 128:(i + 1) * 128], be[:, :],
                                                      start=True, stop=True))
            bank["free"][b_] = r_ = residual(i, False)(pb[b_], tt)
            t_y.append(r_)

        def gated(i, x_):
            def then(bk, tt):
                dve.wait(tt, t_y[i])
                t_y[i] = dve.op(lambda e: e.scalar_tensor_tensor(
                    out=x_sb[:, i, :], in0=bk[:, :], scalar=gt[:, i, x_:x_ + 1], in1=x_sb[:, i, :], op0=ALU.mult,
                    op1=ALU.add))
                return t_y[i]
            return then

        d_out = dsem("d_out")
        nxt = weight(t["We"][0])
        for x_ in range(E):
            s_, tw = nxt
            if x_ + 1 < E:
                nxt = weight(t["We"][x_ + 1])
            for i in range(8):
                r_ = project(i, s_, tw, (), gated(i, x_))
                if x_ == E - 1:
                    sp.wait(r_)
                    t_o = sp.dma(lambda e, i=i: e.dma_start(out.rearrange("(i b) q d -> i (b q) d", b=2)[i],
                                                            x_sb[:, i, :]), d_out, at)
            ws["whfree"][s_] = (pe.sem, pe.count)
        sp.wait(t_o)

        block = root.enter_context(nc.Block())

        @block.sync
        def _(eng):
            sp.run(eng)

        @block.gpsimd
        def _(eng):
            pool.run(eng)

        @block.scalar
        def _(eng):
            act.run(eng)

        @block.vector
        def _(eng):
            dve.run(eng)

        @block.tensor
        def _(eng):
            pe.run(eng)


def kernel(**inputs):
    import numpy as _np
    import concourse.bacc as _bacc
    from concourse import mybir as _mybir
    from concourse.bass_utils import run_bass_kernel_spmd as _run

    v = {k: _np.asarray(a) for k, a in inputs.items()}
    NC, CW, K = 4, 404, 1601
    lead = NC * CW - K

    def kmajor(w):
        return w.reshape(4, 128, -1).transpose(1, 0, 2)

    ctx = _np.concatenate([_np.zeros((16, lead, 512), _np.float32), v["ctx_1024"]], 1)
    mask = _np.concatenate([_np.zeros((64, lead), _np.int32), v["mask_1x1xSxS2_ik0"][0, 0]], 1)
    excl = _np.zeros((NC, 128, CW), _np.float32)
    excl[0, :, :lead] = -3e38
    cst = _np.zeros((128, 384), _np.float32)
    cst[:, 0:128] = _np.eye(128)
    cst[0:4, 128:132] = _np.eye(4)
    cst[0:4, 132:136] = _np.triu(_np.ones((4, 4)))
    cst[0, 136:140] = _np.arange(4)
    cst[:, 140] = -0.5
    cst[:, 160:180] = _np.arange(20)
    cst[:, 256:384] = 2.0 * _np.kron(_np.eye(4), _np.ones((32, 32)))

    def heads(w):
        return w.reshape(2, 4, 2, 32, -1).transpose(1, 3, 0, 2, 4).reshape(128, 4, -1)

    wqkv, bqkv = v["L0_attn_w_qkv"], v["L0_attn_b_qkv"]
    bro = _np.zeros((128, 568), _np.float32)
    bro[:, 0:512] = v["L0_attn_b_proj"]
    bro[:, 512:516] = bqkv[0:512].reshape(4, 128).T
    bro[:, 516:520] = bqkv[512:1024].reshape(4, 128).T
    bro[:, 520:524] = heads(bqkv[1024:1536])[:, :, 0]
    bro[:, 528:548] = v["L0_ffn_bg2"][:20]
    wg2 = _np.zeros((128, 24), _np.float32)
    wg2[:, 0:20] = v["L0_ffn_wg2"][:, :20]
    wg2[:, 20] = v["L0_ffn_bg1"]
    lora = _np.stack([_np.tile(v["L0_attn_a_q"].T, (1, 4)), _np.tile(v["L0_attn_b_q"], (1, 4)),
                      _np.tile(v["L0_attn_a_v"].T, (1, 4)), _np.tile(v["L0_attn_b_v"], (1, 4))], 1)
    arrays = {
        "x": v["x"],
        "ctx": ctx.reshape(16, NC, CW, 4, 128).transpose(0, 1, 4, 3, 2),
        "mask": mask.reshape(64, NC, CW).transpose(1, 0, 2),
        "excl": excl,
        "cst": cst,
        "bro": bro,
        "wq": kmajor(v["L0_xattn_w_q"].T),
        "wk": kmajor(v["L0_xattn_w_k"].T),
        "wv": kmajor(v["L0_xattn_w_v"].T),
        "wo": heads(v["L0_xattn_w_o"].T),
        "w2q": kmajor(wqkv[:, 0:512].T),
        "w2k": kmajor(wqkv[:, 512:1024]),
        "w2v": kmajor(wqkv[:, 1024:1536].T),
        "wproj": heads(v["L0_attn_w_proj"]),
        "lora": lora,
        "wg1": kmajor(v["L0_ffn_wg1"]),
        "wg2": wg2,
        "be": v["L0_ffn_be"],
        "We": v["L0_ffn_We"].reshape(20, 4, 128, 512).transpose(0, 2, 1, 3),
    }
    nc = _bacc.Bacc("TRN2", target_bir_lowering=False, num_devices=1)
    fed, t = {}, {}
    for name, a in arrays.items():
        a = _np.ascontiguousarray(a)
        fed[f"in_{name}"] = a
        t[name] = nc.dram_tensor(f"in_{name}", a.shape, _mybir.dt.from_np(a.dtype), kind="ExternalInput").ap()
    out = nc.dram_tensor("out_0_dram", (16, 64, 512), _mybir.dt.float32, kind="ExternalOutput").ap()
    perceiver(nc, t, out)
    r = _run(nc, [fed], core_ids=[0])
    return r.results[0]["out_0_dram"]
```

```python
import concourse.bass as bass
from concourse import mybir
from contextlib import ExitStack


class Queue:

    def __init__(self, name):
        self.name = name
        self.items = []
        self.sem = None
        self.count = 0
        self.seen = {}

    def use(self, sem):
        self.sem, self.count, self.seen = sem, 0, {}

    def wait(self, *tokens):
        for t in tokens:
            if t is None:
                continue
            sem, value = t
            if self.seen.get(id(sem), 0) < value:
                self.seen[id(sem)] = value
                self.items.append(("wait", sem, value))
        return self

    def op(self, fn, inc=True):
        if inc:
            self.count += 1
            self.items.append(("op", fn, self.sem))
            return (self.sem, self.count)
        self.items.append(("op", fn, None))
        return None

    def alone(self, fn):
        if self.count:
            self.wait((self.sem, self.count))
        return self.op(fn)

    def dma(self, fn, sem, at):
        at[sem[1]] = at.get(sem[1], 0) + 16
        self.items.append(("dma", fn, sem[0]))
        return (sem[0], at[sem[1]])

    def run(self, eng):
        scopes = []
        for it in self.items:
            if it[0] == "wait":
                eng.wait_ge(it[1], it[2])
            elif it[0] == "op":
                ins = it[1](eng)
                if it[2] is not None:
                    ins.then_inc(it[2], 1)
            elif it[0] == "dma":
                it[1](eng).then_inc(it[2], 16)
            elif it[0] == "if":
                guard = eng.If(it[1](eng))
                guard.__enter__()
                scopes.append(guard)
            elif it[0] == "endif":
                scopes.pop().__exit__(None, None, None)
            elif it[0] == "else":
                guard = eng.Else()
                guard.__enter__()
                scopes.append(guard)
            elif it[0] == "do":
                it[1](eng)


def perceiver(nc, t, out):
    f32, f32r, i32, u32 = mybir.dt.float32, mybir.dt.float32r, mybir.dt.int32, mybir.dt.uint32
    ALU, ACT, AX = mybir.AluOpType, mybir.ActivationFunctionType, mybir.AxisListType
    NB, H, D, T, CW, SW, NC_, E = 16, 16, 512, 1024, 404, 101, 4, 20
    EPS = 1e-5
    SCALE = 32.0 ** -0.5

    root = ExitStack()
    pe, act, dve, pool, sp = Queue("pe"), Queue("act"), Queue("dve"), Queue("pool"), Queue("sp")
    engines = (pe, act, dve, pool, sp)
    at = {}

    with root:
        def sem(name):
            return root.enter_context(nc.semaphore(name))

        def sb(name, shape, dt=f32, es=root):
            return es.enter_context(nc.sbuf_tensor(name, shape, dt))

        def dsem(name):
            return (sem(name), name)

        pb = [root.enter_context(nc.psum_tensor(f"bank{i}", [128, 512], f32)) for i in range(8)]

        def new_sems(tag):
            for q in engines:
                q.use(sem(f"s_{q.name}{tag}"))

        def load(dst, src, s, after=()):
            sp.wait(*after)
            return sp.dma(lambda e: e.dma_start(dst, src), s, at)

        cst = sb("cst", [128, 384])
        x_sb = sb("x_sb", [128, 8, D])
        stats = sb("stats", [128, 8, 6])
        mv = sb("mv", [128, 8, 2])
        rstd = sb("rstd", [128, 8])
        ident = cst[:, 0:128]
        iota20 = cst[:, 160:180]

        new_sems("0")
        d_c = dsem("d_c")
        t_cst = load(cst[:, :], t["cst"], d_c)

        def mm3(o, lhs, rhs, start, stop, last=None):
            lh, ll = lhs
            rh, rl = rhs
            pe.op(lambda e: e.matmul(o, lh, rh, start=start, stop=False), inc=False)
            pe.op(lambda e: e.matmul(o, lh, rl, start=False, stop=False), inc=False)
            return pe.op(lambda e: e.matmul(o, ll, rh, start=False, stop=stop), inc=stop)

        def split_rest(dst_lo, src, hi):
            return dve.op(lambda e: e.tensor_tensor(dst_lo, src, hi.bitcast(f32), ALU.subtract))

        def split(raw, hi, lo, t_raw, hi_on=act):
            hi_on.wait(*t_raw)
            if hi_on is act:
                th = act.op(lambda e: e.activation(hi, raw, ACT.Copy))
            else:
                th = hi_on.alone(lambda e: e.tensor_copy(hi, raw))
            dve.wait(th, *t_raw)
            return th, split_rest(lo, raw, hi)

        def layernorm(i, dst, t_x, free, extra=None):
            dve.wait(*t_x)
            a = dve.op(lambda e: e.bn_stats(stats[:, i, :], x_sb[:, i, :]))
            dve.wait(a)
            a = dve.op(lambda e: e.bn_aggr(mv[:, i, :], stats[:, i, :]))
            dve.wait(a)
            a = dve.op(lambda e: e.tensor_scalar(rstd[:, i:i + 1], mv[:, i, 1:2], EPS, None, ALU.add))
            pool.wait(a, t_cst)
            a = pool.alone(lambda e: e.tensor_tensor(rstd[:, i:i + 1], rstd[:, i:i + 1], cst[:, 140:141], ALU.pow))
            if extra is not None:
                dve.wait(a, extra[1])
                a = dve.op(lambda e: e.tensor_tensor(rstd[:, i:i + 1], rstd[:, i:i + 1], extra[0], ALU.mult))
            dve.wait(a, *free)
            return dve.op(lambda e: e.tensor_scalar(dst, x_sb[:, i, :], mv[:, i, 0:1], rstd[:, i:i + 1],
                                                    ALU.subtract, ALU.mult))

        def transposed(i, src, t_src, bank, free, hi, lo):
            pe.wait(*t_src, *free)
            for k in range(4):
                tt = pe.op(lambda e, k=k: e.transpose(bank[:, k * 128:(k + 1) * 128],
                                                      src[:, k * 128:(k + 1) * 128], ident), inc=(k == 3))
            dh = hi[:, :, i * 128:(i + 1) * 128]
            dl = lo[:, :, i * 128:(i + 1) * 128]
            pv = bank[:, :].rearrange("p (k n) -> p k n", k=4)
            act.wait(tt)
            th = act.op(lambda e: e.activation(dh, pv, ACT.Copy))
            dve.wait(th, tt)
            tl = split_rest(dl, pv, dh)
            return th, tl

        acc = sb("acc", [128, NB, 8, 32])
        nm = sb("nm", [128, NB, 8])
        ls = sb("ls", [128, NB, 8])
        lasting = ExitStack()
        wk = [sb(f"wk{j}", [128, 4, D], f32r, lasting) for j in range(2)]
        wv = [sb(f"wv{j}", [128, 4, D], f32r, lasting) for j in range(2)]
        craw = sb("craw", [128, 2, 4, CW], f32, lasting)
        chi = sb("chi", [128, 2, 4, CW], f32r, lasting)
        clo = sb("clo", [128, 2, 4, CW], f32r, lasting)
        qc = sb("qc", [128, 4, T], f32, lasting)
        qh = sb("qh", [128, 2, 4, 128], f32r, lasting)
        ql = sb("ql", [128, 2, 4, 128], f32r, lasting)
        ids = sb("ids", [1, 8], i32, lasting)
        cap = sb("cap", [128, CW], f32, lasting)

        zero = sb("zero", [128, 128], f32, lasting)
        d_z = dsem("d_z")
        t_zero = pool.alone(lambda e: e.memset(zero[:, :], 0.0))

        first = ExitStack()
        mska = sb("mska", [128, NC_, CW], i32, first)
        cm = sb("cm", [128, 4], f32, first)
        fl = sb("fl", [128, 16], f32, first)
        rows = sb("rows", [128, 4], f32, first)
        fr = sb("fr", [4, 1], f32, first)
        frow = sb("frow", [1, 32], f32, first)
        wq = [sb(f"wq{j}", [128, 4, D], f32r, first) for j in range(2)]
        wraw = sb("wraw", [128, 2, 4, D], f32, first)
        xt = [sb(f"xt{j}", [128, 4, T], f32r, first) for j in range(2)]
        xn = sb("xn", [128, 2, D], f32, first)

        d_m = [dsem(f"d_m{i}") for i in range(2)]
        d_x = [dsem(f"d_x{i}") for i in range(2)]
        d_w = [dsem(f"d_w{i}") for i in range(2)]
        t_m = [load(mska[64 * h:64 * h + 64, :, :], t["mask"].rearrange("c q k -> q c k"), d_m[h]) for h in range(2)]
        xv = t["x"].rearrange("(i b) q d -> i (b q) d", b=2)
        t_x = [load(x_sb[:, 4 * h:4 * h + 4, :], xv[4 * h:4 * h + 4].rearrange("i p d -> p i d"), d_x[h])
               for h in range(2)]
        t_wq = load(wraw[:, 0], t["wq"], d_w[0])
        t_wk = load(wraw[:, 1], t["wk"], d_w[1])

        for c in range(NC_):
            dve.wait(*t_m)
            a = dve.op(lambda e, c=c: e.tensor_scalar(mska[:, c, :].bitcast(f32), mska[:, c, :], 0.0, None,
                                                      ALU.not_equal))
            dve.wait(a)
            t_cm = dve.op(lambda e, c=c: e.tensor_reduce(cm[:, c:c + 1], mska[:, c, :].bitcast(f32), AX.X, ALU.max))
        dve.wait(t_cm)
        a = dve.op(lambda e: e.tensor_reduce(rows[:, 0:1], cm[:, :], AX.X, ALU.max))
        dve.wait(a)
        t_rs = dve.op(lambda e: e.tensor_scalar(rows[:, 1:2], rows[:, 0:1], SCALE, None, ALU.mult))
        a = dve.op(lambda e: e.tensor_scalar(rows[:, 2:3], rows[:, 0:1], -1.0, 1.0, ALU.mult, ALU.add))
        dve.wait(a)
        t_fl = dve.op(lambda e: e.tensor_scalar(fl[:, 0:4], cm[:, :], rows[:, 2:3], None, ALU.max))
        pe.wait(t_fl, t_cst)
        a = pe.op(lambda e: e.transpose(pb[7][0:4, 0:128], fl[:, 0:4], ident))
        dve.wait(a)
        a = dve.op(lambda e: e.tensor_reduce(fr[:, :], pb[7][0:4, 0:128], AX.X, ALU.max))
        pe.wait(a)
        a = pe.op(lambda e: e.matmul(pb[7][0:1, 0:8], fr[:, :], cst[0:4, 128:136], start=True, stop=True))
        dve.wait(a)
        a = dve.op(lambda e: e.tensor_copy(frow[:, 0:8], pb[7][0:1, 0:8]))
        dve.wait(a, t_cst)
        a = dve.op(lambda e: e.tensor_tensor(frow[:, 8:12], frow[:, 0:4], cst[0:1, 136:140], ALU.mult))
        dve.wait(a)
        for j in range(NC_):
            a = dve.op(lambda e, j=j: e.scalar_tensor_tensor(out=frow[:, 12:16], in0=frow[:, 4:8], scalar=float(j + 1),
                                                             in1=frow[:, 8:12], op0=ALU.is_equal, op1=ALU.mult,
                                                             accum_out=frow[:, 16 + j:17 + j]))
            dve.wait(a)
        a = dve.op(lambda e: e.tensor_copy(ids[:, 0:4], frow[:, 16:20]))
        t_ids = dve.op(lambda e: e.tensor_copy(ids[:, 4:5], frow[:, 7:8]))

        regs = {}

        def read_count(q):
            q.wait(t_ids)
            q.items.append(("do", lambda e: regs.__setitem__(q.name, e.value_load(ids[0:1, 4:5], min_val=1,
                                                                                  max_val=4))))

        def read_chunk(j):
            sp.wait(t_ids)
            sp.items.append(("do", lambda e: regs.__setitem__("chunk", e.value_load(ids[0:1, j:j + 1], min_val=0,
                                                                                    max_val=3))))

        t_wqs = split(wraw[:, 0], wq[0][:, :, :], wq[1][:, :, :], [t_wq])
        t_wks = split(wraw[:, 1], wk[0][:, :, :], wk[1][:, :, :], [t_wk])
        t_wv = load(wraw[:, 0], t["wv"], d_w[0], after=t_wqs)
        t_wvs = split(wraw[:, 0], wv[0][:, :, :], wv[1][:, :, :], [t_wv])

        t_z = [pool.alone(lambda e: e.memset(qh[:, :, :, :].bitcast(f32), 0.0)),
               pool.alone(lambda e: e.memset(ql[:, :, :, :].bitcast(f32), 0.0))]

        t_xt = []
        free_xn, free_b = [None, None], [None, None]
        for i in range(8):
            tn = layernorm(i, xn[:, i % 2, :], [t_x[i // 4]], [free_xn[i % 2]], (rows[:, 1:2], t_rs))
            th, tl = transposed(i, xn[:, i % 2, :], [tn, t_cst], pb[5 + i % 2], [free_b[i % 2]], xt[0], xt[1])
            free_xn[i % 2] = th
            free_b[i % 2] = tl
            t_xt.append((th, tl))
        t_q = None
        free_b = [None] * 3
        n = 0
        for hf in range(2):
            for m in range(4):
                bank = pb[n % 3]
                pe.wait(*t_wqs, *t_xt[4 * hf + 3], free_b[n % 3])
                for k in range(4):
                    tt = mm3(bank[:, :], [w[:, k, m * 128:(m + 1) * 128] for w in wq],
                             [v[:, k, hf * 512:(hf + 1) * 512] for v in xt], k == 0, k == 3)
                act.wait(tt)
                free_b[n % 3] = t_q = act.op(lambda e, m=m, hf=hf, bank=bank: e.activation(
                    qc[:, m, hf * 512:(hf + 1) * 512], bank[:, :], ACT.Copy))
                n += 1
        t_pe0 = tt
        first.close()

        second = ExitStack()
        kk = [sb(f"kk{j}", [128, 4, CW], f32r, second) for j in range(2)]
        vv = sb("vv", [SW, 4, D], f32, second)
        pp = sb("pp", [128, 8, CW], f32, second)
        pt = sb("pt", [SW, 4, 4, 128], f32, second)
        mski = sb("mski", [128, CW], i32, second)
        excl = sb("excl", [128, CW], f32, second)
        nmn = sb("nmn", [128, 2, 8], f32, second)
        lsn = sb("lsn", [128, 2, 8], f32, second)
        cor = sb("cor", [128, 2, 8], f32, second)

        d_ctx = [dsem(f"d_ctx{i}") for i in range(2)]
        d_cap = dsem("d_cap")
        for q in engines:
            read_count(q)

        sp.wait(t_zero)
        for name, first_, n_ in [("xg", 7 * j, 7) for j in range(5)] + [("yg", E + 5 * j, 5) for j in range(3)]:
            for k in range(4):
                t_xg0 = sp.dma(lambda e, name=name, first_=first_, n_=n_, k=k: e.dma_start(
                    t[name][first_ * 128:(first_ + n_) * 128, k * 128:(k + 1) * 128].rearrange(
                        "(a p) n -> p a n", p=128), zero[:, :].unsqueeze(1).to_broadcast([128, n_, 128])), d_z, at)

        st = {"kv": [t_q, t_q, t_q], "kvn": 0, "S": [None, None], "T": [None, None], "O": None, "t_split": {},
              "craw": [None, None], "cfree": [None, None], "qd": {}, "qfree": [None, None],
              "P": [t_pe0] * 8, "PT": [None] * 4, "V": None, "K": [None] * 4, "state": [None] * NB, "cap": None,
              "capread": None}

        def prepare_ctx(n, b):
            s = n % 2
            sp.wait(*(st["craw"][s] or ()))
            tl = sp.dma(lambda e: e.dma_start(craw[:, s], t["ctx"][b, bass.ds(regs["chunk"], 1)].rearrange(
                "a p k n -> (a p) k n")), d_ctx[s], at)
            pool.wait(tl, st["cfree"][s])
            th = pool.alone(lambda e: e.tensor_copy(chi[:, s], craw[:, s]))
            dve.wait(th, tl, st["cfree"][s])
            tlo = split_rest(clo[:, s], craw[:, s], chi[:, s])
            st["craw"][s] = (th, tlo)
            st["t_split"][n] = (th, tlo)
            pool.wait(t_q, st["qfree"][s], *t_z)
            tq = []
            for r in range(4):
                src = qc[32 * r:32 * r + 32, :, b * 64:b * 64 + 64]
                dh = qh[32 * r:32 * r + 32, s, :, 64 * (r % 2):64 * (r % 2) + 64]
                dl = ql[32 * r:32 * r + 32, s, :, 64 * (r % 2):64 * (r % 2) + 64]
                tq.append((pool.alone(lambda e, dh=dh, src=src: e.tensor_copy(dh, src)), dl, src, dh))
            for th_, dl, src, dh in tq:
                pool.wait(th_)
                tt_ = pool.alone(lambda e, dl=dl, src=src, dh=dh: e.tensor_tensor(dl, src, dh.bitcast(f32),
                                                                               ALU.subtract))
            st["qd"][n] = tt_

        def take_bank():
            i = st["kvn"] % 3
            st["kvn"] += 1
            return i, st["kv"][i]

        def k_part(n, g):
            i, free = take_bank()
            s = n % 2
            pe.wait(*t_wks, *st["t_split"][n], free)
            for k in range(4):
                tt = mm3(pb[i][:, 0:CW], [w[:, k, g * 128:(g + 1) * 128] for w in wk],
                         [chi[:, s, k, :], clo[:, s, k, :]], k == 0, k == 3)
            act.wait(tt, st["K"][g])
            th = act.op(lambda e: e.activation(kk[0][:, g, :], pb[i][:, 0:CW], ACT.Copy))
            dve.wait(tt, th, st["K"][g])
            tl = split_rest(kk[1][:, g, :], pb[i][:, 0:CW], kk[0][:, g, :])
            st["kv"][i] = tl
            return th, tl

        def v_part(n, i4):
            i, free = take_bank()
            s = n % 2
            pe.wait(*t_wvs, free)
            for k in range(4):
                tt = mm3(pb[i][0:SW, :], [c[:, s, k, i4 * SW:(i4 + 1) * SW] for c in (chi, clo)],
                         [w[:, k, :] for w in wv], k == 0, k == 3)
            act.wait(tt, st["V"])
            st["kv"][i] = tv = act.op(lambda e: e.activation(vv[:, i4, :], pb[i][0:SW, :], ACT.Copy))
            st["cfree"][s] = tt
            return tv

        def s_part(n, b, seg, p8, t_k):
            g, u = divmod(p8, 2)
            s = n % 2
            bank = pb[3 + u]
            pe.wait(*t_k[g], st["qd"][n], st["S"][u])
            r = slice(64 * u, 64 * u + 64)
            tt = mm3(bank[:, 0:CW], [q[r, s, g, :] for q in (qh, ql)], [w[r, g, :] for w in kk], True, True)
            st["K"][g] = tt
            st["qfree"][s] = tt
            dve.wait(tt, st["P"][p8], st["cap"])
            dst = nm[:, b, p8:p8 + 1] if seg == 0 else nmn[:, s, p8:p8 + 1]
            if seg:
                dve.wait(st["state"][b])
            ini = 3e38 if seg == 0 else nm[:, b, p8:p8 + 1]
            st["S"][u] = td = dve.op(lambda e: e.tensor_tensor_reduce(
                out=pp[:, p8, :], in0=bank[:, 0:CW], in1=cap[:, :], scale=-1.0, scalar=ini,
                op0=ALU.add, op1=ALU.min, accum_out=dst))
            act.wait(td)
            sdst = ls[:, b, p8:p8 + 1] if seg == 0 else lsn[:, s, p8:p8 + 1]
            st["capread"] = td
            return td, act.op(lambda e: e.activation(pp[:, p8, :], pp[:, p8, :], ACT.Exp, bias=dst, scale=-1.0,
                                                     accum_out=sdst))

        def t_part(n, p8, t_e):
            u = p8 % 2
            pe.wait(t_e, st["T"][u], t_cst)
            bank = pb[5 + u]
            for i4 in range(4):
                tt = pe.op(lambda e, i4=i4: e.transpose(bank[0:SW, i4 * 128:(i4 + 1) * 128],
                                                        pp[:, p8, i4 * SW:(i4 + 1) * SW], ident), inc=(i4 == 3))
            st["P"][p8] = tt
            slot = p8 % 4
            dst = pt[:, slot, :, :].rearrange("p a c -> p (a c)")
            if u:
                act.wait(tt, st["PT"][slot])
                st["T"][u] = te = act.op(lambda e: e.activation(dst, bank[0:SW, :], ACT.Copy))
            else:
                dve.wait(tt, st["PT"][slot])
                st["T"][u] = te = dve.op(lambda e: e.tensor_copy(dst, bank[0:SW, :]))
            return te

        def pv_part(n, b, p8, te, t_v):
            slot = p8 % 4
            pe.wait(te, *t_v)
            if p8 == 0:
                pe.wait(st["O"])
            for i4 in range(4):
                tt = pe.op(lambda e, i4=i4: e.matmul(pb[7][:, p8 * 64:(p8 + 1) * 64], pt[:, slot, i4, :],
                                                     vv[:, i4, p8 * 64:(p8 + 1) * 64], start=(i4 == 0),
                                                     stop=(i4 == 3)), inc=(i4 == 3))
            st["PT"][slot] = tt
            st["V"] = tt
            return tt

        def o_part(n, b, seg, t_pv, t_exp, t_max):
            ov = pb[7][:, :].rearrange("p (t c) -> p t c", t=8)
            s = n % 2
            if seg == 0:
                dve.wait(t_pv)
                for h in range(2):
                    r = slice(64 * h, 64 * h + 64)
                    tt = dve.op(lambda e, r=r, h=h: e.tensor_copy(acc[r, b, :, :], ov[r, :, 32 * h:32 * h + 32]))
                st["O"] = st["state"][b] = tt
                return
            dve.wait(t_max, t_exp, st["state"][b])
            a = dve.op(lambda e: e.tensor_tensor(cor[:, s, :], nmn[:, s, :], nm[:, b, :], ALU.subtract))
            act.wait(a)
            c = act.op(lambda e: e.activation(cor[:, s, :], cor[:, s, :], ACT.Exp))
            dve.wait(c)
            a = dve.op(lambda e: e.tensor_copy(nm[:, b, :], nmn[:, s, :]))
            a = dve.op(lambda e: e.tensor_tensor(ls[:, b, :], ls[:, b, :], cor[:, s, :], ALU.mult))
            a2 = dve.op(lambda e: e.tensor_tensor(acc[:, b, :, :], acc[:, b, :, :],
                                                  cor[:, s, :].unsqueeze(2).to_broadcast([128, 8, 32]), ALU.mult))
            dve.wait(a, a2, t_pv)
            dve.op(lambda e: e.tensor_tensor(ls[:, b, :], ls[:, b, :], lsn[:, s, :], ALU.add))
            for h in range(2):
                r = slice(64 * h, 64 * h + 64)
                tt = dve.op(lambda e, r=r, h=h: e.tensor_tensor(acc[r, b, :, :], acc[r, b, :, :],
                                                                ov[r, :, 32 * h:32 * h + 32], ALU.add))
            st["O"] = st["state"][b] = tt

        def segment(seg):
            read_chunk(seg)
            sp.wait(st["capread"], st["cap"])
            if seg == 0:
                sp.wait(t_pe0, t_q, *t_wvs)
            for src, dst in ((t["mask"], mski), (t["excl"], None)):
                if dst is not None:
                    for h in range(2):
                        tm = sp.dma(lambda e, h=h: e.dma_start(
                            mski[64 * h:64 * h + 64, :],
                            t["mask"][bass.ds(regs["chunk"], 1)].rearrange("a q k -> (a q) k")), d_cap, at)
                else:
                    tm = sp.dma(lambda e: e.dma_start(
                        excl[:, :], t["excl"][bass.ds(regs["chunk"], 1)].rearrange("a q k -> (a q) k")), d_cap, at)
            dve.wait(tm, st["capread"])
            a = dve.op(lambda e: e.tensor_scalar(cap[:, :], mski[:, :], 0.0, 1e9, ALU.not_equal, ALU.mult))
            dve.wait(a)
            st["cap"] = dve.op(lambda e: e.scalar_tensor_tensor(out=cap[:, :], in0=cap[:, :], scalar=-1e9,
                                                                in1=excl[:, :], op0=ALU.add, op1=ALU.add))
            base = 16 * seg
            prepare_ctx(base, 0)
            old = None
            for b in range(NB + 1):
                n = base + b
                t_k, evac = [], {}
                for g in range(4):
                    if b < NB:
                        t_k.append(k_part(n, g))
                    if old is not None:
                        if g:
                            for p8 in (2 * g - 2, 2 * g - 1):
                                pv_part(old["n"], old["b"], p8, evac[p8], old["v"])
                        for p8 in (2 * g, 2 * g + 1):
                            evac[p8] = t_part(old["n"], p8, old["e"][p8])
                if old is not None:
                    for p8 in (6, 7):
                        t_pv = pv_part(old["n"], old["b"], p8, evac[p8], old["v"])
                    o_part(old["n"], old["b"], seg, t_pv, old["e"][7], old["m"])
                if b == NB:
                    break
                if b + 1 < NB:
                    prepare_ctx(n + 1, b + 1)
                t_v, t_e = [], []
                for g in range(4):
                    for p8 in (2 * g, 2 * g + 1):
                        t_max, te = s_part(n, b, seg, p8, t_k)
                        t_e.append(te)
                    t_v.append(v_part(n, g))
                old = {"n": n, "b": b, "v": t_v, "e": t_e, "m": t_max}

        segment(0)
        for seg in range(1, NC_):
            for q in engines:
                q.items.append(("if", lambda e, q=q, seg=seg: regs[q.name] > seg))
            segment(seg)
        for seg in range(1, NC_):
            for q in engines:
                q.items.append(("endif",))
        s_bar = sem("s_bar")
        for q in engines:
            q.items.append(("do", lambda e: e.drain().then_inc(s_bar, 1)))
        new_sems("1")
        for q in engines:
            q.items.append(("wait", s_bar, 5))

        second.close()
        lasting.close()

        xt = [sb(f"xu{j}", [128, 4, T], f32r) for j in range(2)]
        xn = sb("xm", [128, 2, D])
        raw = sb("raw", [128, 2, 4, D])
        wh = [sb(f"wh{j}", [128, 2, 4, D], f32r) for j in range(2)]
        bro = sb("bro", [128, D + 4 * 4 + 40])
        bproj, bcol, bg2 = bro[:, 0:D], bro[:, D:D + 16], bro[:, D + 16:D + 36]
        d_raw = [dsem(f"d_raw{i}") for i in range(2)]
        d_b = dsem("d_b")
        t_bro = load(bro[:, :], t["bro"], d_b)
        ws = {"n": 0, "rawfree": [None, None], "whfree": [None, None]}

        def fetch(src):
            n = ws["n"]
            ws["n"] += 1
            s = n % 2
            return s, load(raw[:, s], src, d_raw[s], after=ws["rawfree"][s] or ())

        def weight(src):
            s, tl = fetch(src)
            act.wait(ws["whfree"][s])
            dve.wait(ws["whfree"][s])
            tt = split(raw[:, s], wh[0][:, s], wh[1][:, s], [tl])
            ws["rawfree"][s] = tt
            return s, tt

        bank = {"n": 0, "free": [None] * 3}

        def take(banks=(0, 1, 2)):
            i = bank["n"] % 3
            bank["n"] += 1
            return i, bank["free"][i]

        def heads_to_features(i, t_acc, bias, free):
            bk = pb[5 + i % 2]
            pe.wait(*t_acc, free[i % 2])
            for j in range(4):
                b2, g2 = divmod(j, 2)
                tt = pe.op(lambda e, j=j, b2=b2, g2=g2: e.transpose(
                    bk[:, j * 128:(j + 1) * 128],
                    acc[:, 2 * i + b2, 4 * g2:4 * g2 + 4, :].rearrange("p a c -> p (a c)"), ident), inc=(j == 3))
            src = bk[:, :].rearrange("p (b c q) -> p c b q", b=2, c=4)
            dst = [x[:, :, i * 128:(i + 1) * 128].rearrange("p c (b q) -> p c b q", b=2) for x in xt]
            act.wait(tt)
            if bias is None:
                th = act.op(lambda e: e.activation(dst[0], src, ACT.Copy))
                dve.wait(th, tt)
                tl = split_rest(dst[1], src, dst[0])
            else:
                act.wait(bias[1])
                for c in range(4):
                    th = act.op(lambda e, c=c: e.activation(dst[0][:, c], src[:, c], ACT.Identity,
                                                            bias=bias[0][:, c:c + 1]))
                dve.wait(th, tt, bias[1])
                for c in range(4):
                    tl = dve.op(lambda e, c=c: e.scalar_tensor_tensor(
                        out=dst[1][:, c], in0=src[:, c], scalar=bias[0][:, c:c + 1], in1=dst[0][:, c].bitcast(f32),
                        op0=ALU.add, op1=ALU.subtract))
            free[i % 2] = tl
            return th, tl

        def project(i, s, t_w, t_in, then):
            b_, free = take()
            pe.wait(*t_w, *t_in, free)
            for k in range(4):
                tt = mm3(pb[b_][:, :], [v[:, k, i * 128:(i + 1) * 128] for v in xt], [w[:, s, k, :] for w in wh],
                         k == 0, k == 3)
            bank["free"][b_] = r = then(pb[b_], tt)
            return r

        def feature_major(m, hf, s, t_w, t_in, then):
            b_, free = take()
            pe.wait(*t_w, *t_in, free)
            for k in range(4):
                tt = mm3(pb[b_][:, :], [w[:, s, k, m * 128:(m + 1) * 128] for w in wh],
                         [v[:, k, hf * 512:(hf + 1) * 512] for v in xt], k == 0, k == 3)
            ws["whfree"][s] = tt
            bank["free"][b_] = r = then(pb[b_], tt)
            return r

        def residual(i, bias):
            def then(bk, tt):
                dve.wait(tt)
                r = dve.op(lambda e: e.tensor_tensor(x_sb[:, i, :], x_sb[:, i, :], bk[:, :], ALU.add))
                if bias:
                    dve.wait(r, t_bro)
                    r = dve.op(lambda e: e.tensor_tensor(x_sb[:, i, :], x_sb[:, i, :], bproj, ALU.add))
                return r
            return then

        def norm_all(t_x, keep=None):
            out_, fx, fb = [], [None, None], [None, None]
            for i in range(8):
                dst = xn[:, i % 2, :] if keep is None else keep[:, i, :]
                tn = layernorm(i, dst, [t_x[i]], [fx[i % 2]])
                th, tl = transposed(i, dst, [tn], pb[5 + i % 2], [fb[i % 2]], xt[0], xt[1])
                fx[i % 2], fb[i % 2] = th, tl
                out_.append((th, tl))
            return out_

        s_wo, t_wo = weight(t["wo"])
        a = dve.op(lambda e: e.reciprocal(ls[:, :, :], ls[:, :, :]))
        free = [None, None]
        t_x1 = []
        for i in range(8):
            dve.wait(a)
            ta = dve.op(lambda e, i=i: e.tensor_tensor(
                acc[:, 2 * i:2 * i + 2, :, :], acc[:, 2 * i:2 * i + 2, :, :],
                ls[:, 2 * i:2 * i + 2, :].unsqueeze(3).to_broadcast([128, 2, 8, 32]), ALU.mult))
            ti = heads_to_features(i, [ta], None, free)
            t_x1.append(project(i, s_wo, t_wo, ti, residual(i, False)))
        ws["whfree"][s_wo] = (pe.sem, pe.count)

        mid = ExitStack()
        lora = sb("lora", [16, 4, 128], f32, mid)
        mbd = sb("mbd", [128, 2, 128], f32, mid)
        bl = sb("bl", [128, 8], f32, mid)
        qT = sb("qT", [128, 4, T], f32, mid)
        kT = sb("kT", [128, 4, T], f32, mid)
        v2 = sb("v2", [128, 8, D], f32, mid)
        qd = sb("qd", [128, 2, 2, 4, 128], f32, mid)
        p2 = sb("p2", [128, 2, 8, 2, 64], f32, mid)
        pt2 = sb("pt2", [128, 8, 128], f32, mid)
        mx2 = sb("mx2", [128, 2, 16], f32, mid)
        ls2 = sb("ls2", [128, 2, 16], f32, mid)
        t_lo = load(lora[:, :, :], t["lora"], d_b)
        t_z = pool.alone(lambda e: e.memset(qd[:, :, :, :, :], 0.0))
        pe.wait(t_lo)
        for j in range(2):
            tt = pe.op(lambda e, j=j: e.matmul(pb[7][:, j * 128:(j + 1) * 128], lora[:, 2 * j, :],
                                               lora[:, 2 * j + 1, :], start=True, stop=True))
        for j in range(2):
            dve.wait(tt, t_cst)
            a = dve.op(lambda e, j=j: e.tensor_tensor(mbd[:, j, :], pb[7][:, j * 128:(j + 1) * 128], cst[:, 256:384],
                                                      ALU.mult))
            dve.wait(a)
            t_mbd = dve.op(lambda e, j=j: e.tensor_tensor(mbd[:, j, :], mbd[:, j, :], ident, ALU.add))
        pe.wait(t_mbd, t_bro)
        for c in range(4):
            pe.op(lambda e, c=c: e.matmul(pb[7][:, 256 + c:257 + c], mbd[:, 0, :], bcol[:, c:c + 1], start=True,
                                          stop=True), inc=False)
            tt = pe.op(lambda e, c=c: e.matmul(pb[7][:, 260 + c:261 + c], mbd[:, 1, :], bcol[:, 8 + c:9 + c],
                                               start=True, stop=True), inc=(c == 3))
        dve.wait(tt)
        t_bl = dve.op(lambda e: e.tensor_copy(bl[:, :], pb[7][:, 256:264]))

        t_xt = norm_all(t_x1)

        def weight_lora(src, j):
            s, tl = fetch(src)
            for k in range(4):
                b_, free_ = take()
                pe.wait(tl, t_mbd, free_)
                for g in range(4):
                    tt_ = pe.op(lambda e, g=g, k=k, b_=b_: e.matmul(
                        pb[b_][:, g * 128:(g + 1) * 128], raw[:, s, g, k * 128:(k + 1) * 128], mbd[:, j, :],
                        start=True, stop=True), inc=(g == 3))
                act.wait(tt_, ws["whfree"][s])
                th = act.op(lambda e, k=k, b_=b_: e.activation(wh[0][:, s, k, :], pb[b_][:, :], ACT.Copy))
                dve.wait(th, tt_, ws["whfree"][s])
                bank["free"][b_] = tlo = split_rest(wh[1][:, s, k, :], pb[b_][:, :], wh[0][:, s, k, :])
            ws["rawfree"][s] = (tt_,)
            return s, (th, tlo)

        def biased(dst, col, t_col):
            def then(bk, tt):
                act.wait(tt, t_col)
                return act.op(lambda e: e.activation(dst, bk[:, :], ACT.Identity, bias=col))
            return then

        def copied(dst):
            def then(bk, tt):
                act.wait(tt)
                return act.op(lambda e: e.activation(dst, bk[:, :], ACT.Copy))
            return then

        s_, tw = weight_lora(t["w2q"], 0)
        for hf in range(2):
            for m in range(4):
                t_qT = feature_major(m, hf, s_, tw, t_xt[4 * hf + 3], biased(
                    qT[:, m, hf * 512:(hf + 1) * 512], bl[:, m:m + 1], t_bl))
        s_, tw = weight(t["w2k"])
        for hf in range(2):
            for m in range(4):
                t_kT = feature_major(m, hf, s_, tw, (), biased(
                    kT[:, m, hf * 512:(hf + 1) * 512], bcol[:, 4 + m:5 + m], t_bro))
        s_, tw = weight_lora(t["w2v"], 1)
        for i in range(8):
            t_v2 = project(i, s_, tw, (), copied(v2[:, i, :]))
        ws["whfree"][s_] = t_lastv = (pe.sem, pe.count)
        s_wp, t_wp = weight(t["wproj"])

        fr2 = {"S": [None, None], "T": [None, None], "O": [bank["free"][2], None], "qd": [None, None],
               "p2": [None, None], "pt2": None, "h": [None, None]}
        t_x2 = []
        for i in range(8):
            s = i % 2
            pool.wait(t_qT, fr2["qd"][s], t_z)
            for b2 in range(2):
                for r in range(4):
                    tq = pool.alone(lambda e, b2=b2, r=r, s=s, i=i: e.tensor_copy(
                        qd[32 * r:32 * r + 32, s, b2, :, 64 * (r % 2):64 * (r % 2) + 64],
                        qT[32 * r:32 * r + 32, :, (2 * i + b2) * 64:(2 * i + b2 + 1) * 64]))
            t_sub = []
            for u in range(2):
                pe.wait(tq, t_kT, fr2["S"][u])
                for b2 in range(2):
                    for g in range(4):
                        r = slice(64 * u, 64 * u + 64)
                        tt = pe.op(lambda e, b2=b2, g=g, r=r, u=u, s=s, i=i: e.matmul(
                            pb[3 + u][:, (b2 * 4 + g) * 64:(b2 * 4 + g + 1) * 64], qd[r, s, b2, g, :],
                            kT[r, g, (2 * i + b2) * 64:(2 * i + b2 + 1) * 64], start=True, stop=True),
                            inc=(b2 == 1 and g == 3))
                fr2["qd"][s] = tt
                src = pb[3 + u][:, :].rearrange("p (c k) -> p c k", k=64)
                dve.wait(tt)
                a = dve.op(lambda e, u=u, s=s, src=src: e.tensor_reduce(mx2[:, s, 8 * u:8 * u + 8], src, AX.X,
                                                                        ALU.max))
                dve.wait(a, fr2["p2"][s])
                for b2 in range(2):
                    tb = dve.op(lambda e, u=u, s=s, b2=b2, src=src: e.tensor_tensor(
                        p2[:, s, u:8:2, b2, :], src[:, 4 * b2:4 * b2 + 4, :],
                        mx2[:, s, 8 * u + 4 * b2:8 * u + 4 * b2 + 4].unsqueeze(2).to_broadcast([128, 4, 64]),
                        ALU.subtract))
                fr2["S"][u] = tb
            pv = p2[:, s].rearrange("p t b k -> p (t b k)")
            act.wait(tb)
            te = act.op(lambda e, pv=pv: e.activation(pv, pv, ACT.Exp, scale=SCALE))
            dve.wait(te)
            a = dve.op(lambda e, s=s: e.tensor_reduce(ls2[:, s, :], p2[:, s].rearrange("p t b k -> p (t b) k"),
                                                      AX.X, ALU.add))
            dve.wait(a)
            t_rl = dve.op(lambda e, s=s: e.reciprocal(ls2[:, s, :], ls2[:, s, :]))
            ev = []
            for h in range(2):
                pe.wait(te, fr2["T"][h])
                for j in range(4):
                    tt = pe.op(lambda e, h=h, j=j, s=s: e.transpose(
                        pb[5 + h][:, j * 128:(j + 1) * 128],
                        p2[:, s, 4 * h + j].rearrange("p b k -> p (b k)"), ident), inc=(j == 3))
                dst = pt2[:, 4 * h:4 * h + 4, :].rearrange("p a c -> p (a c)")
                if h:
                    act.wait(tt, fr2["pt2"])
                    w_ = act.op(lambda e, dst=dst, h=h: e.activation(dst, pb[5 + h][:, :], ACT.Copy))
                else:
                    dve.wait(tt, fr2["pt2"])
                    w_ = dve.op(lambda e, dst=dst, h=h: e.tensor_copy(dst, pb[5 + h][:, :]))
                fr2["T"][h] = w_
                ev.append(w_)
            fr2["p2"][s] = tt
            t_acc = []
            for b2 in range(2):
                bk = pb[(7, 2)[b2]]
                pe.wait(*ev, t_v2, t_bl, fr2["O"][b2], bank["free"][2])
                for p8 in range(8):
                    r = slice(64 * b2, 64 * b2 + 64)
                    tt = pe.op(lambda e, p8=p8, r=r, bk=bk, i=i: e.matmul(
                        bk[:, p8 * 64:(p8 + 1) * 64], pt2[r, p8, :], v2[r, i, p8 * 64:(p8 + 1) * 64],
                        start=True, stop=True), inc=(p8 == 7))
                fr2["pt2"] = tt
                ov = bk[:, :].rearrange("p (t c) -> p t c", t=8)
                lv = ls2[:, s, :].rearrange("p (t b) -> p t b", b=2)
                dve.wait(tt, t_rl)
                for h in range(2):
                    r = slice(64 * h, 64 * h + 64)
                    w_ = dve.op(lambda e, r=r, h=h, b2=b2, i=i, ov=ov, lv=lv: e.tensor_tensor(
                        acc[r, 2 * i + b2, :, :], ov[r, :, 32 * h:32 * h + 32],
                        lv[r, :, b2:b2 + 1].to_broadcast([64, 8, 32]), ALU.mult))
                fr2["O"][b2] = w_
                t_acc.append(w_)
            pe.wait(t_lastv)
            fr2["T"] = list(fr2["T"])
            ti = heads_to_features(i, t_acc + [fr2["T"][i % 2]], (bl[:, 4:8], t_bl), fr2["h"])
            fr2["T"][i % 2] = ti[1]
            b_ = i % 2
            pe.wait(*t_wp, *ti, bank["free"][b_])
            for k in range(4):
                tt = mm3(pb[b_][:, :], [v[:, k, i * 128:(i + 1) * 128] for v in xt],
                         [w[:, s_wp, k, :] for w in wh], k == 0, k == 3)
            bank["free"][b_] = tr = residual(i, True)(pb[b_], tt)
            t_x2.append(tr)
        ws["whfree"][s_wp] = tt
        bank["free"][2] = fr2["O"][1]
        mid.close()

        g1raw = sb("g1raw", [128, 4, 128])
        g1 = [sb(f"g1{j}", [128, 4, 128], f32r) for j in range(2)]
        gw = sb("gw", [128, 24])
        be = sb("be", [E, D])
        hT = sb("hT", [128, T])
        pr = sb("pr", [128, 8, E])
        gt = sb("gt", [128, 8, E])
        mg = sb("mg", [128, 8, 8])
        mi = sb("mi", [128, 8, 8], u32)
        mf = sb("mf", [128, 8, 8])
        sg = sb("sg", [128, 8])
        gT = sb("gT", [E, T])
        m1 = sb("m1", [128, 8, E])
        m2 = sb("m2", [128, 8, E])
        sel = sb("sel", [128, 8, E])
        pre = sb("pre", [128, 9, E])
        sl = sb("sl", [128, 8, E])
        sm2 = sb("sm2", [128, 8, E])
        sf = sb("sf", [128, 2, 8])
        si = sb("si", [128, 2, 8], u32)
        sm = sb("sm", [E, 10])
        orep = sb("orep", [E, 128])
        ob = sb("ob", [128, 60])
        jc = sb("jc", [1, 15, E])
        jf = sb("jf", [1, 16])
        ji = sb("ji", [1, 16], i32)
        cs2 = sb("cs2", [128, 660])
        wr = sb("wr", [128, 5, 4, D])
        xi = sb("xi", [128, 3, D])
        xo = [sb(f"xo{j}", [128, 2, 4, 128], f32r) for j in range(2)]
        yo = xn
        yga = wr[:, 0:2].rearrange("p r (a c) n -> p (r a) c n", c=2)
        dve.wait(t_x2[7])
        d_g = [dsem(f"d_g{i}") for i in range(3)]
        t_g1 = load(g1raw[:, :, :], t["wg1"], d_g[0], after=[t_x2[7]])
        t_gw = load(gw[:, :], t["wg2"], d_g[1])
        t_be = load(be[:, :], t["be"], d_g[2])
        t_cs2 = load(cs2[:, :], t["cs2"], dsem("d_cs2"))
        act.wait(t_x2[7])
        t_g1s = split(g1raw[:, :, :], g1[0][:, :, :], g1[1][:, :, :], [t_g1])
        xall = acc[:, :, :, :].rearrange("p b t c -> p (b t c)").rearrange("p (i n) -> p i n", i=8)
        t_xt = norm_all(t_x2, xall)
        for hf in range(2):
            b_, fr_ = take()
            pe.wait(*t_g1s, *t_xt[4 * hf + 3], fr_)
            for k in range(4):
                tt = mm3(pb[b_][:, :], [w[:, k, :] for w in g1], [v[:, k, hf * 512:(hf + 1) * 512] for v in xt],
                         k == 0, k == 3)
            act.wait(tt, t_gw)
            bank["free"][b_] = t_h = act.op(lambda e, b_=b_, hf=hf: e.activation(
                hT[:, hf * 512:(hf + 1) * 512], pb[b_][:, :], ACT.Gelu, bias=gw[:, 20:21]))
        pe.wait(t_h, t_gw)
        for i in range(8):
            tt = pe.op(lambda e, i=i: e.matmul(pb[7][:, i * E:(i + 1) * E], hT[:, i * 128:(i + 1) * 128],
                                               gw[:, 0:20], start=True, stop=True), inc=(i == 7))
        dve.wait(tt, t_bro)
        lg = pb[7][:, 0:8 * E].rearrange("p (i e) -> p i e", e=E)
        a = dve.op(lambda e: e.tensor_tensor(pr[:, :, :], lg, bg2.unsqueeze(1).to_broadcast([128, 8, E]), ALU.add))
        dve.wait(a)
        a = dve.op(lambda e: e.tensor_reduce(sg[:, :], pr[:, :, :], AX.X, ALU.max))
        dve.wait(a)
        a = dve.op(lambda e: e.tensor_tensor(pr[:, :, :], pr[:, :, :],
                                             sg[:, :].unsqueeze(2).to_broadcast([128, 8, E]), ALU.subtract))
        act.wait(a)
        a = act.op(lambda e: e.activation(pr[:, :, :], pr[:, :, :], ACT.Exp))
        dve.wait(a)
        a = dve.op(lambda e: e.tensor_reduce(sg[:, :], pr[:, :, :], AX.X, ALU.add))
        dve.wait(a)
        a = dve.op(lambda e: e.reciprocal(sg[:, :], sg[:, :]))
        dve.wait(a)
        a = dve.op(lambda e: e.tensor_tensor(pr[:, :, :], pr[:, :, :],
                                             sg[:, :].unsqueeze(2).to_broadcast([128, 8, E]), ALU.mult))
        dve.wait(a)
        for i in range(8):
            a = dve.op(lambda e, i=i: e.max(out=mg[:, i, :], in_=pr[:, i, :]))
        dve.wait(a)
        for i in range(8):
            a = dve.op(lambda e, i=i: e.max_index(mi[:, i, :], mg[:, i, :], pr[:, i, :]))
        dve.wait(a)
        a = dve.op(lambda e: e.tensor_copy(mf[:, :, :], mi[:, :, :]))
        dve.wait(a)
        for i in range(8):
            a = dve.op(lambda e, i=i: e.tensor_scalar(m1[:, i, :], iota20, mf[:, i, 0:1], None, ALU.is_equal))
            a = dve.op(lambda e, i=i: e.tensor_scalar(m2[:, i, :], iota20, mf[:, i, 1:2], None, ALU.is_equal))
        dve.wait(a)
        t_sel = dve.op(lambda e: e.tensor_tensor(sel[:, :, :], m1[:, :, :], m2[:, :, :], ALU.add))
        dve.wait(t_sel)
        a = t_sel
        dve.op(lambda e: e.memset(pre[:, 0, :], 0.0))
        a = dve.op(lambda e: e.tensor_copy(pre[:, 1, :], sel[:, 0, :]))
        for i in range(1, 8):
            dve.wait(a)
            a = dve.op(lambda e, i=i: e.tensor_tensor(pre[:, i + 1, :], pre[:, i, :], sel[:, i, :], ALU.add))
        t_gt = dve.op(lambda e: e.tensor_tensor(gt[:, :, :], sel[:, :, :], pr[:, :, :], ALU.mult))

        upper, ones = cs2[:, 0:128], cs2[:, 128:256]
        tri, ks, e128, esh, jg = cs2[0:E, 256:296], cs2[0:E, 300:307], cs2[:, 320:340], cs2[:, 340:360], \
            cs2[0:1, 360:660]
        pe.wait(a, t_sel, t_cs2)
        pe.op(lambda e: e.matmul(pb[7][:, 0:160], upper, sel[:, :, :].rearrange("p i e -> p (i e)"), start=True,
                                 stop=False), inc=False)
        pe.op(lambda e: e.matmul(pb[7][:, 0:160], ones, pre[:, 0:8, :].rearrange("p i e -> p (i e)"), start=False,
                                 stop=True), inc=False)
        t_pos = pe.op(lambda e: e.matmul(pb[3][0:E, 0:1], pre[:, 8, :], ones[:, 0:1], start=True, stop=True))
        dve.wait(t_pos, t_cs2)
        a = dve.op(lambda e: e.tensor_copy(sm[0:E, 8:9], pb[3][0:E, 0:1]))
        dve.wait(a)
        a = dve.op(lambda e: e.tensor_scalar(sm[0:E, 0:7], ks, sm[0:E, 8:9], None, ALU.is_lt))
        dve.wait(a)
        a = dve.op(lambda e: e.tensor_reduce(sm[0:E, 9:10], sm[0:E, 0:7], AX.X, ALU.add))
        dve.wait(a)
        a = dve.op(lambda e: e.tensor_scalar(orep[:, :], ones[0:E, :], sm[0:E, 9:10], None, ALU.mult))
        pe.wait(a)
        a = pe.op(lambda e: e.matmul(pb[4][:, 0:40], orep[:, :], tri, start=True, stop=True))
        dve.wait(a)
        a = dve.op(lambda e: e.tensor_copy(ob[:, 0:40], pb[4][:, 0:40]))
        dve.wait(a)
        a = dve.op(lambda e: e.scalar_tensor_tensor(out=ob[:, 40:60], in0=ob[:, 0:20], scalar=128.0, in1=esh,
                                                    op0=ALU.mult, op1=ALU.add))
        b0 = dve.op(lambda e: e.tensor_tensor(jc[:, :, :], ob[0:1, 20:40].unsqueeze(1).to_broadcast([1, 15, E]),
                                              jg.rearrange("p (j e) -> p j e", e=E), ALU.is_le))
        dve.wait(a, b0)
        posv = pb[7][:, 0:160].rearrange("p (i e) -> p i e", e=E)
        a = dve.op(lambda e: e.tensor_scalar(sl[:, :, :], posv, 128.0, None, ALU.is_ge))
        b0 = dve.op(lambda e: e.tensor_reduce(jf[:, 0:15], jc[:, :, :], AX.X, ALU.add))
        dve.wait(a)
        a = dve.op(lambda e: e.tensor_tensor(sl[:, :, :], sl[:, :, :],
                                             ob[:, 40:60].unsqueeze(1).to_broadcast([128, 8, E]), ALU.mult))
        dve.wait(a, b0)
        a = dve.op(lambda e: e.tensor_tensor(sl[:, :, :], sl[:, :, :], posv, ALU.add))
        b0 = dve.op(lambda e: e.tensor_scalar(ji[:, 0:15], jf[:, 0:15], float(E - 1), None, ALU.min))
        t_ji = dve.op(lambda e: e.tensor_copy(ji[:, 15:16], ob[0:1, 39:40]))
        dve.wait(a)
        a = dve.op(lambda e: e.tensor_tensor(sl[:, :, :], sl[:, :, :],
                                             e128.unsqueeze(1).to_broadcast([128, 8, E]), ALU.add))
        dve.wait(a)
        for m_, col in ((m1, 0), (m2, 1)):
            a = dve.op(lambda e, m_=m_: e.tensor_tensor(sm2[:, :, :], m_[:, :, :], sl[:, :, :], ALU.mult))
            dve.wait(a)
            a = dve.op(lambda e, col=col: e.tensor_reduce(sf[:, col, :], sm2[:, :, :], AX.X, ALU.add))
            dve.wait(a)
        t_slot = dve.op(lambda e: e.tensor_copy(si[:, :, :], sf[:, :, :]))

        d_sc, d_ga = dsem("d_sc"), dsem("d_ga")
        pool.wait(t_slot, t_xg0, t_xt[7][0])
        for i in range(8):
            for c in range(2):
                t_sc = pool.dma(lambda e, i=i, c=c: e.indirect_dma_start(
                    out=t["xg"][:, :], out_offset=bass.IndirectOffsetOnAxis(ap=si[:, c, i:i + 1], axis=0),
                    in_=xall[:, i, :], in_offset=None), d_sc, at)

        pe.wait(t_gt)
        for hf in range(2):
            for j in range(4):
                i = 4 * hf + j
                tt = pe.op(lambda e, i=i, j=j, hf=hf: e.transpose(pb[5 + hf][0:E, j * 128:(j + 1) * 128],
                                                                  gt[:, i, :], ident), inc=(j == 3))
            dve.wait(tt)
            t_gT = dve.op(lambda e, hf=hf: e.tensor_copy(gT[:, hf * 512:(hf + 1) * 512], pb[5 + hf][0:E, :]))
        t_y = []
        for i in range(8):
            b_, fr_ = take()
            pe.wait(t_gT, t_be, fr_)
            tt = pe.op(lambda e, i=i, b_=b_: e.matmul(pb[b_][:, :], gT[:, i * 128:(i + 1) * 128], be[:, :],
                                                      start=True, stop=True))
            bank["free"][b_] = r_ = residual(i, False)(pb[b_], tt)
            t_y.append(r_)

        R = 5
        d_we = [dsem(f"d_we{i}") for i in range(R)]
        d_xi = [dsem(f"d_xi{i}") for i in range(3)]
        d_yo = [dsem(f"d_yo{i}") for i in range(2)]
        fe = {"raw": [None] * R, "xi": [None] * 3, "xo": [None, None], "yo": [None] * 2, "T": [t_gT, t_gT],
              "wh": [ws["whfree"][0], ws["whfree"][1]], "y": [None, None]}
        ybank = [pb[3], pb[4]]
        ystore = {}
        fe["y"] = [t_slot, t_slot]

        def expert_weight(n, src, free=()):
            r = n % R
            sp.wait(*(fe["raw"][r] or ()), *free)
            return sp.dma(lambda e: e.dma_start(wr[:, r], src(e)), d_we[r], at)

        def expert_tokens(n):
            r = n % 3
            sp.wait(t_sc, fe["xi"][r])
            return sp.dma(lambda e: e.dma_start(xi[:, r, :], t["xg"][n * 128:(n + 1) * 128, :]), d_xi[r], at)

        def prepare(n, tw_, tx_):
            s_, r, h = n % 2, n % R, n % 2
            act.wait(tw_, fe["wh"][s_])
            th = act.op(lambda e: e.activation(wh[0][:, s_], wr[:, r], ACT.Copy))
            dve.wait(th, tw_, fe["wh"][s_])
            tl = split_rest(wh[1][:, s_], wr[:, r], wh[0][:, s_])
            fe["raw"][r] = (th, tl)
            bk = pb[5 + h]
            pe.wait(tx_, fe["T"][h])
            for k in range(4):
                tt = pe.op(lambda e, k=k: e.transpose(bk[:, k * 128:(k + 1) * 128],
                                                      xi[:, n % 3, k * 128:(k + 1) * 128], ident), inc=(k == 3))
            fe["xi"][n % 3] = tt
            pv = bk[:, :].rearrange("p (k n) -> p k n", k=4)
            act.wait(tt, fe["xo"][h])
            xh = act.op(lambda e: e.activation(xo[0][:, h], pv, ACT.Copy))
            dve.wait(xh, tt, fe["xo"][h])
            fe["T"][h] = xl = split_rest(xo[1][:, h], pv, xo[0][:, h])
            return th, tl, xh, xl

        def block_of(n, ready):
            s_ = n % 2
            pe.wait(*ready, fe["y"][s_])
            for k in range(4):
                tt = mm3(ybank[s_][:, :], [v[:, s_, k, :] for v in xo], [w[:, s_, k, :] for w in wh], k == 0, k == 3)
            fe["wh"][s_] = fe["xo"][s_] = tt
            act.wait(tt, fe["yo"][n % 2])
            fe["y"][s_] = ty = act.op(lambda e: e.activation(yo[:, n % 2, :], ybank[s_][:, :], ACT.Copy))
            sp.wait(ty)
            ystore[n] = fe["yo"][n % 2] = sp.dma(lambda e: e.dma_start(t["yg"][n * 128:(n + 1) * 128, :], yo[:, n % 2, :]),
                                     d_yo[n % 2], at)

        we_tok = {n: expert_weight(n, lambda e, n=n: t["We"][n], free=[t_x2[7]]) for n in range(R)}
        xi_tok = {n: expert_tokens(n) for n in range(2)}
        ready = prepare(0, we_tok[0], xi_tok[0])
        for n in range(E):
            if n + 2 < E:
                xi_tok[n + 2] = expert_tokens(n + 2)
            nxt = prepare(n + 1, we_tok[n + 1], xi_tok[n + 1]) if n + 1 < E else None
            if n + R < E:
                we_tok[n + R] = expert_weight(n + R, lambda e, n=n: t["We"][n + R])
            block_of(n, ready)
            ready = nxt

        for q in engines:
            q.wait(t_ji)
            q.items.append(("do", lambda e, q=q: regs.__setitem__(q.name, e.value_load(
                ji[0:1, 15:16], min_val=0, max_val=15))))
        def over_loads(j):
            if j >= 15:
                return None
            sp.items.append(("do", lambda e: regs.__setitem__("x", e.value_load(
                ji[0:1, j:j + 1], min_val=0, max_val=E - 1))))
            tw_ = expert_weight(E + j, lambda e: t["We"][bass.ds(regs["x"], 1)].rearrange(
                "a p k n -> (a p) k n"))
            return tw_, expert_tokens(E + j)

        loads = {j: over_loads(j) for j in range(2)}
        ready = prepare(E, *loads[0])
        for j in range(15):
            for q in engines:
                q.items.append(("if", lambda e, q=q, j=j: regs[q.name] > j))
            loads[j + 2] = over_loads(j + 2)
            nxt = prepare(E + j + 1, *loads[j + 1]) if j + 1 < 15 else None
            block_of(E + j, ready)
            ready = nxt
        for d, s_ in zip(d_yo, range(2)):
            sp.items.append(("wait", d[0], at[d[1]]))
        for j in range(14, -1, -1):
            for q in engines:
                q.items.append(("endif",))
            sp.items.append(("else",))
            if j + 1 < 15:
                for tok in loads[j + 1]:
                    sp.items.append(("wait", *tok))
            for n_ in (E + j - 1, E + j - 2):
                sp.items.append(("wait", *ystore[n_]))
            sp.items.append(("endif",))
        s_bar2 = sem("s_bar2")
        for q in engines:
            q.items.append(("do", lambda e: e.drain().then_inc(s_bar2, 1)))
        new_sems("2")
        for q in engines:
            q.items.append(("wait", s_bar2, 5))

        d_ga = [dsem(f"d_ga{i}") for i in range(4)]
        d_out = dsem("d_out")
        gf = [None] * 4
        for i in range(8):
            r = i % 4
            pool.wait(gf[r])
            for c in range(2):
                tg = pool.dma(lambda e, i=i, c=c, r=r: e.indirect_dma_start(
                    out=yga[:, r, c, :], out_offset=None, in_=t["yg"][:, :],
                    in_offset=bass.IndirectOffsetOnAxis(ap=si[:, c, i:i + 1], axis=0)), d_ga[r], at)
            dve.wait(tg)
            a = dve.op(lambda e, i=i, r=r: e.scalar_tensor_tensor(
                out=x_sb[:, i, :], in0=yga[:, r, 0, :], scalar=mg[:, i, 0:1], in1=x_sb[:, i, :], op0=ALU.mult,
                op1=ALU.add))
            dve.wait(a)
            gf[r] = a = dve.op(lambda e, i=i, r=r: e.scalar_tensor_tensor(
                out=x_sb[:, i, :], in0=yga[:, r, 1, :], scalar=mg[:, i, 1:2], in1=x_sb[:, i, :], op0=ALU.mult,
                op1=ALU.add))
            sp.wait(a)
            t_o = sp.dma(lambda e, i=i: e.dma_start(out.rearrange("(i b) q d -> i (b q) d", b=2)[i],
                                                    x_sb[:, i, :]), d_out, at)
        sp.wait(t_o)

        block = root.enter_context(nc.Block())

        @block.sync
        def _(eng):
            sp.run(eng)

        @block.gpsimd
        def _(eng):
            pool.run(eng)

        @block.scalar
        def _(eng):
            act.run(eng)

        @block.vector
        def _(eng):
            dve.run(eng)

        @block.tensor
        def _(eng):
            pe.run(eng)


def kernel(**inputs):
    import numpy as _np
    import concourse.bacc as _bacc
    from concourse import mybir as _mybir
    from concourse.bass_utils import run_bass_kernel_spmd as _run

    v = {k: _np.asarray(a) for k, a in inputs.items()}
    NC, CW, K = 4, 404, 1601
    lead = NC * CW - K

    def kmajor(w):
        return w.reshape(4, 128, -1).transpose(1, 0, 2)

    ctx = _np.concatenate([_np.zeros((16, lead, 512), _np.float32), v["ctx_1024"]], 1)
    mask = _np.concatenate([_np.zeros((64, lead), _np.int32), v["mask_1x1xSxS2_ik0"][0, 0]], 1)
    excl = _np.zeros((NC, 128, CW), _np.float32)
    excl[0, :, :lead] = -3e38
    cst = _np.zeros((128, 384), _np.float32)
    cst[:, 0:128] = _np.eye(128)
    cst[0:4, 128:132] = _np.eye(4)
    cst[0:4, 132:136] = _np.triu(_np.ones((4, 4)))
    cst[0, 136:140] = _np.arange(4)
    cst[:, 140] = -0.5
    cst[:, 160:180] = _np.arange(20)
    cst[:, 256:384] = 2.0 * _np.kron(_np.eye(4), _np.ones((32, 32)))

    cs2 = _np.zeros((128, 660), _np.float32)
    cs2[:, 0:128] = _np.triu(_np.ones((128, 128)), 1)
    cs2[:, 128:256] = 1.0
    cs2[0:20, 256:276] = _np.triu(_np.ones((20, 20)), 1)
    cs2[0:20, 276:296] = _np.triu(_np.ones((20, 20)))
    cs2[0:20, 300:307] = 128.0 * _np.arange(1, 8)
    cs2[:, 320:340] = 128.0 * _np.arange(20)
    cs2[:, 340:360] = 128.0 * (19 - _np.arange(20))
    cs2[:, 360:660] = _np.repeat(_np.arange(15), 20)

    def heads(w):
        return w.reshape(2, 4, 2, 32, -1).transpose(1, 3, 0, 2, 4).reshape(128, 4, -1)

    wqkv, bqkv = v["L0_attn_w_qkv"], v["L0_attn_b_qkv"]
    bro = _np.zeros((128, 568), _np.float32)
    bro[:, 0:512] = v["L0_attn_b_proj"]
    bro[:, 512:516] = bqkv[0:512].reshape(4, 128).T
    bro[:, 516:520] = bqkv[512:1024].reshape(4, 128).T
    bro[:, 520:524] = heads(bqkv[1024:1536])[:, :, 0]
    bro[:, 528:548] = v["L0_ffn_bg2"][:20]
    wg2 = _np.zeros((128, 24), _np.float32)
    wg2[:, 0:20] = v["L0_ffn_wg2"][:, :20]
    wg2[:, 20] = v["L0_ffn_bg1"]
    lora = _np.stack([_np.tile(v["L0_attn_a_q"].T, (1, 4)), _np.tile(v["L0_attn_b_q"], (1, 4)),
                      _np.tile(v["L0_attn_a_v"].T, (1, 4)), _np.tile(v["L0_attn_b_v"], (1, 4))], 1)
    arrays = {
        "x": v["x"],
        "ctx": ctx.reshape(16, NC, CW, 4, 128).transpose(0, 1, 4, 3, 2),
        "mask": mask.reshape(64, NC, CW).transpose(1, 0, 2),
        "excl": excl,
        "cst": cst,
        "cs2": cs2,
        "bro": bro,
        "wq": kmajor(v["L0_xattn_w_q"].T),
        "wk": kmajor(v["L0_xattn_w_k"].T),
        "wv": kmajor(v["L0_xattn_w_v"].T),
        "wo": heads(v["L0_xattn_w_o"].T),
        "w2q": kmajor(wqkv[:, 0:512].T),
        "w2k": kmajor(wqkv[:, 512:1024]),
        "w2v": kmajor(wqkv[:, 1024:1536].T),
        "wproj": heads(v["L0_attn_w_proj"]),
        "lora": lora,
        "wg1": kmajor(v["L0_ffn_wg1"]),
        "wg2": wg2,
        "be": v["L0_ffn_be"],
        "We": v["L0_ffn_We"].reshape(20, 4, 128, 512).transpose(0, 2, 1, 3),
    }
    nc = _bacc.Bacc("TRN2", target_bir_lowering=False, num_devices=1)
    fed, t = {}, {}
    for name, a in arrays.items():
        a = _np.ascontiguousarray(a)
        fed[f"in_{name}"] = a
        t[name] = nc.dram_tensor(f"in_{name}", a.shape, _mybir.dt.from_np(a.dtype), kind="ExternalInput").ap()
    for name in ("xg", "yg"):
        t[name] = nc.dram_tensor(f"scratch_{name}", (35 * 128, 512), _mybir.dt.float32, kind="Internal").ap()
    out = nc.dram_tensor("out_0_dram", (16, 64, 512), _mybir.dt.float32, kind="ExternalOutput").ap()
    perceiver(nc, t, out)
    r = _run(nc, [fed], core_ids=[0])
    return r.results[0]["out_0_dram"]
```

```python
import concourse.bass as bass
from concourse import mybir
from contextlib import ExitStack


class Same(list):

    def __init__(self, token):
        super().__init__([token, token])

    def __setitem__(self, key, token):
        super().__setitem__(0, token)
        super().__setitem__(1, token)


class Queue:

    def __init__(self, name):
        self.name = name
        self.items = []
        self.sem = None
        self.count = 0
        self.seen = {}

    def use(self, sem):
        self.sem, self.count, self.seen = sem, 0, {}

    def wait(self, *tokens):
        for t in tokens:
            if t is None:
                continue
            sem, value = t
            if self.seen.get(id(sem), 0) < value:
                self.seen[id(sem)] = value
                self.items.append(("wait", sem, value))
        return self

    def op(self, fn, inc=True):
        if inc:
            self.count += 1
            self.items.append(("op", fn, self.sem))
            return (self.sem, self.count)
        self.items.append(("op", fn, None))
        return None

    def alone(self, fn):
        if self.count:
            self.wait((self.sem, self.count))
        return self.op(fn)

    def dma(self, fn, sem, at):
        at[sem[1]] = at.get(sem[1], 0) + 16
        self.items.append(("dma", fn, sem[0]))
        return (sem[0], at[sem[1]])

    def run(self, eng):
        scopes = []
        for it in self.items:
            if it[0] == "wait":
                eng.wait_ge(it[1], it[2])
            elif it[0] == "op":
                ins = it[1](eng)
                if it[2] is not None:
                    ins.then_inc(it[2], 1)
            elif it[0] == "dma":
                it[1](eng).then_inc(it[2], 16)
            elif it[0] == "if":
                guard = eng.If(it[1](eng))
                guard.__enter__()
                scopes.append(guard)
            elif it[0] == "endif":
                scopes.pop().__exit__(None, None, None)
            elif it[0] == "else":
                guard = eng.Else()
                guard.__enter__()
                scopes.append(guard)
            elif it[0] == "do":
                it[1](eng)


def perceiver(nc, t, out):
    f32, f32r, i32, u32 = mybir.dt.float32, mybir.dt.float32r, mybir.dt.int32, mybir.dt.uint32
    ALU, ACT, AX = mybir.AluOpType, mybir.ActivationFunctionType, mybir.AxisListType
    NB, H, D, T, CW, SW, NC_, E = 16, 16, 512, 1024, 404, 101, 4, 20
    EPS = 1e-5
    SCALE = 32.0 ** -0.5

    root = ExitStack()
    pe, act, dve, pool, sp = Queue("pe"), Queue("act"), Queue("dve"), Queue("pool"), Queue("sp")
    engines = (pe, act, dve, pool, sp)
    at = {}

    with root:
        def sem(name):
            return root.enter_context(nc.semaphore(name))

        def sb(name, shape, dt=f32, es=root):
            return es.enter_context(nc.sbuf_tensor(name, shape, dt))

        def dsem(name):
            return (sem(name), name)

        pb = [root.enter_context(nc.psum_tensor(f"bank{i}", [128, 512], f32)) for i in range(8)]

        def new_sems(tag):
            for q in engines:
                q.use(sem(f"s_{q.name}{tag}"))

        def load(dst, src, s, after=()):
            sp.wait(*after)
            return sp.dma(lambda e: e.dma_start(dst, src), s, at)

        cst = sb("cst", [128, 384])
        x_sb = sb("x_sb", [128, 8, D])
        stats = sb("stats", [128, 8, 6])
        mv = sb("mv", [128, 8, 2])
        rstd = sb("rstd", [128, 8])
        ident = cst[:, 0:128]
        iota20 = cst[:, 160:180]

        new_sems("0")
        d_c = dsem("d_c")
        t_cst = load(cst[:, :], t["cst"], d_c)

        def mm3(o, lhs, rhs, start, stop, last=None):
            lh, ll = lhs
            rh, rl = rhs
            pe.op(lambda e: e.matmul(o, lh, rh, start=start, stop=False), inc=False)
            pe.op(lambda e: e.matmul(o, lh, rl, start=False, stop=False), inc=False)
            return pe.op(lambda e: e.matmul(o, ll, rh, start=False, stop=stop), inc=stop)

        def split_rest(dst_lo, src, hi):
            return dve.op(lambda e: e.tensor_tensor(dst_lo, src, hi.bitcast(f32), ALU.subtract))

        def split(raw, hi, lo, t_raw, hi_on=act):
            hi_on.wait(*t_raw)
            if hi_on is act:
                th = act.op(lambda e: e.activation(hi, raw, ACT.Copy))
            else:
                th = hi_on.alone(lambda e: e.tensor_copy(hi, raw))
            dve.wait(th, *t_raw)
            return th, split_rest(lo, raw, hi)

        def norm_stats(i, t_x):
            dve.wait(*t_x)
            a = dve.op(lambda e: e.bn_stats(stats[:, i, :], x_sb[:, i, :]))
            dve.wait(a)
            return dve.op(lambda e: e.bn_aggr(mv[:, i, :], stats[:, i, :]))

        def norm_scale(i, n, t_mv, extra=None):
            dve.wait(t_mv)
            a = dve.op(lambda e: e.tensor_scalar(rstd[:, i:i + n], mv[:, i:i + n, 1], EPS, None, ALU.add))
            pool.wait(a, t_cst)
            a = pool.alone(lambda e: e.tensor_tensor(rstd[:, i:i + n], rstd[:, i:i + n],
                                                     cst[:, 140:141].to_broadcast([128, n]), ALU.pow))
            if extra is not None:
                dve.wait(a, extra[1])
                a = dve.op(lambda e: e.tensor_scalar(rstd[:, i:i + n], rstd[:, i:i + n], extra[0], None, ALU.mult))
            return a

        def norm_apply(i, dst, t_r, free):
            dve.wait(t_r, *free)
            return dve.op(lambda e: e.tensor_scalar(dst, x_sb[:, i, :], mv[:, i, 0:1], rstd[:, i:i + 1],
                                                    ALU.subtract, ALU.mult))

        def pipeline(stages, n=8):
            for step in range(n + max(lag for _, lag in stages)):
                for fn, lag in stages:
                    if 0 <= step - lag < n:
                        fn(step - lag)

        def transposed(i, src, t_src, bank, free, hi, lo, xfree=()):
            pe.wait(*t_src, *free)
            for k in range(4):
                tt = pe.op(lambda e, k=k: e.transpose(bank[:, k * 128:(k + 1) * 128],
                                                      src[:, k * 128:(k + 1) * 128], ident), inc=(k == 3))
            dh = hi[:, :, i * 128:(i + 1) * 128]
            dl = lo[:, :, i * 128:(i + 1) * 128]
            pv = bank[:, :].rearrange("p (k n) -> p k n", k=4)
            act.wait(tt, *xfree)
            th = act.op(lambda e: e.activation(dh, pv, ACT.Copy))
            dve.wait(th, tt, *xfree)
            tl = split_rest(dl, pv, dh)
            return th, tl

        acc = sb("acc", [128, NB, 8, 32])
        nm = sb("nm", [128, NB, 8])
        ls = sb("ls", [128, NB, 8])
        raw = sb("raw", [128, 2, 4, D])
        wh = [[sb(f"wh0{j}", [128, 4, D], f32r) for j in range(2)]]
        lasting = ExitStack()
        wk = [sb(f"wk{j}", [128, 4, D], f32r, lasting) for j in range(2)]
        wv = [sb(f"wv{j}", [128, 4, D], f32r, lasting) for j in range(2)]
        craw = sb("craw", [128, 2, 4, CW], f32, lasting)
        chi = sb("chi", [128, 2, 4, CW], f32r, lasting)
        clo = sb("clo", [128, 2, 4, CW], f32r, lasting)
        qc = sb("qc", [128, 4, T], f32, lasting)
        qh = sb("qh", [128, 2, 4, 128], f32r, lasting)
        ql = sb("ql", [128, 2, 4, 128], f32r, lasting)
        ids = sb("ids", [1, 8], i32, lasting)
        cap = sb("cap", [128, CW], f32, lasting)
        excl = sb("excl", [128, CW], f32, lasting)
        mski = sb("mski", [128, CW], i32, lasting)

        zero = sb("zero", [128, 128], f32, lasting)
        d_z = dsem("d_z")
        t_zero = pool.alone(lambda e: e.memset(zero[:, :], 0.0))

        kk = [sb(f"kk{j}", [128, 4, CW], f32r, lasting) for j in range(2)]
        vv = sb("vv", [SW, 4, D], f32, lasting)
        nmn = sb("nmn", [128, 2, 8], f32, lasting)
        lsn = sb("lsn", [128, 2, 8], f32, lasting)
        cor = sb("cor", [128, 2, 8], f32, lasting)

        first = ExitStack()
        mska = craw[:, 1].bitcast(i32)
        cm = sb("cm", [128, 4], f32, first)
        fl = sb("fl", [128, 16], f32, first)
        rows = sb("rows", [128, 4], f32, first)
        fr = sb("fr", [4, 1], f32, first)
        frow = sb("frow", [1, 32], f32, first)
        wq = wh[0]
        wraw = raw
        xt = [sb(f"xt{j}", [128, 4, 512], f32r, first) for j in range(2)]
        xn = sb("xn", [128, 2, D], f32, first)

        d_raw = [dsem(f"d_raw{i}") for i in range(2)]
        d_m = [dsem(f"d_m{i}") for i in range(2)]
        d_x = [dsem(f"d_x{i}") for i in range(2)]
        d_w = [dsem(f"d_w{i}") for i in range(2)]
        t_m = [load(mska[64 * h:64 * h + 64, :, :], t["mask"].rearrange("c q k -> q c k"), d_m[h]) for h in range(2)]
        xv = t["x"].rearrange("(i b) q d -> i (b q) d", b=2)
        t_x = [None, None]
        t_x[0] = load(x_sb[:, 0:4, :], xv[0:4].rearrange("i p d -> p i d"), d_x[0])
        t_wq = load(wraw[:, 0], t["wq"], d_w[0])
        t_x[1] = load(x_sb[:, 4:8, :], xv[4:8].rearrange("i p d -> p i d"), d_x[1])
        t_wk = load(wraw[:, 1], t["wk"], d_w[1])

        dve.wait(*t_m)
        t_cm = dve.op(lambda e: e.tensor_reduce(cm[:, :], mska, AX.X, ALU.max, apply_absolute_value=True))
        dve.wait(t_cm)
        a = dve.op(lambda e: e.tensor_scalar(cm[:, :], cm[:, :], 0.0, None, ALU.not_equal))
        dve.wait(a)
        a = dve.op(lambda e: e.tensor_reduce(rows[:, 0:1], cm[:, :], AX.X, ALU.max))
        dve.wait(a)
        t_rs = dve.op(lambda e: e.tensor_scalar(rows[:, 1:2], rows[:, 0:1], SCALE, None, ALU.mult))
        a = dve.op(lambda e: e.tensor_scalar(rows[:, 2:3], rows[:, 0:1], -1.0, 1.0, ALU.mult, ALU.add))
        dve.wait(a)
        t_fl = dve.op(lambda e: e.tensor_scalar(fl[:, 0:4], cm[:, :], rows[:, 2:3], None, ALU.max))
        pe.wait(t_fl, t_cst)
        a = pe.op(lambda e: e.transpose(pb[7][0:4, 0:128], fl[:, 0:4], ident))
        norm_stats(0, [t_x[0]])
        dve.wait(a)
        a = dve.op(lambda e: e.tensor_reduce(fr[:, :], pb[7][0:4, 0:128], AX.X, ALU.max))
        pe.wait(a)
        a = pe.op(lambda e: e.matmul(pb[7][0:1, 0:8], fr[:, :], cst[0:4, 128:136], start=True, stop=True))
        norm_stats(1, [t_x[0]])
        dve.wait(a)
        a = dve.op(lambda e: e.tensor_copy(frow[:, 0:8], pb[7][0:1, 0:8]))
        dve.wait(a, t_cst)
        a = dve.op(lambda e: e.tensor_tensor(frow[:, 8:12], frow[:, 0:4], cst[0:1, 136:140], ALU.mult))
        dve.wait(a)
        for j in range(NC_):
            a = dve.op(lambda e, j=j: e.scalar_tensor_tensor(out=frow[:, 12:16], in0=frow[:, 4:8], scalar=float(j + 1),
                                                             in1=frow[:, 8:12], op0=ALU.is_equal, op1=ALU.mult,
                                                             accum_out=frow[:, 16 + j:17 + j]))
            dve.wait(a)
        a = dve.op(lambda e: e.tensor_copy(ids[:, 0:4], frow[:, 16:20]))
        t_ids = dve.op(lambda e: e.tensor_copy(ids[:, 4:5], frow[:, 7:8]))

        regs = {}

        def read_count(q):
            q.wait(t_ids)
            q.items.append(("do", lambda e: regs.__setitem__(q.name, e.value_load(ids[0:1, 4:5], min_val=1,
                                                                                  max_val=4))))

        def read_chunk(j):
            sp.wait(t_ids)
            sp.items.append(("do", lambda e: regs.__setitem__("chunk", e.value_load(ids[0:1, j:j + 1], min_val=0,
                                                                                    max_val=3))))

        t_z = [pool.alone(lambda e: e.memset(qh[:, :, :, :].bitcast(f32), 0.0)),
               pool.alone(lambda e: e.memset(ql[:, :, :, :].bitcast(f32), 0.0))]

        t_xt, t_r, t_n = {}, {}, {}
        free_xn, free_b = [None, None], [None, None]

        def n_apply(i):
            t_n[i] = norm_apply(i, xn[:, i % 2, :], t_r[i // 4], [free_xn[i % 2]])

        xt_free = [None]

        def n_turn(i):
            t_xt[i] = transposed(i % 4, xn[:, i % 2, :], [t_n[i], t_cst], pb[5 + i % 2], [free_b[i % 2]], xt[0], xt[1], [xt_free[i // 4]])
            free_xn[i % 2], free_b[i % 2] = t_xt[i]

        for i in (2, 3):
            a = norm_stats(i, [t_x[0]])
        t_r[0] = norm_scale(0, 4, a, (rows[:, 1:2], t_rs))
        n_apply(0)
        n_apply(1)
        t_wqs = split(wraw[:, 0], wq[0][:, :, :], wq[1][:, :, :], [t_wq])
        for i in range(4):
            n_turn(i)
            if i < 2:
                n_apply(i + 2)
        t_q = {}
        d_ctx = [dsem(f"d_ctx{i}") for i in range(2)]
        d_cap = dsem("d_cap")
        read_chunk(0)
        st = {"kv": [None] * 3, "kvn": 0, "S": [None, None], "T": [None, None], "O": None, "t_split": {},
              "craw": [None, (t_cm,)], "cfree": [None, None], "qd": {}, "qfree": [None, None],
              "P": [None] * 8, "PT": [None] * 4, "V": None, "K": [None] * 4, "state": [None] * NB, "cap": None,
              "capread": None}

        def prepare_ctx(n, b):
            s = n % 2
            sp.wait(*(st["craw"][s] or ()))
            tl = sp.dma(lambda e: e.dma_start(craw[:, s], t["ctx"][b, bass.ds(regs["chunk"], 1)].rearrange(
                "a p k n -> (a p) k n")), d_ctx[s], at)
            act.wait(tl, st["cfree"][s])
            th = act.op(lambda e: e.activation(chi[:, s], craw[:, s], ACT.Copy))
            dve.wait(th, tl, st["cfree"][s])
            tlo = split_rest(clo[:, s], craw[:, s], chi[:, s])
            st["craw"][s] = (th, tlo)
            st["t_split"][n] = (th, tlo)

        def prepare_q(n, b):
            s = n % 2
            pool.wait(t_q[b // 8], st["qfree"][s], *t_z)
            tq = []
            for r in range(4):
                src = qc[32 * r:32 * r + 32, :, b * 64:b * 64 + 64]
                dh = qh[32 * r:32 * r + 32, s, :, 64 * (r % 2):64 * (r % 2) + 64]
                dl = ql[32 * r:32 * r + 32, s, :, 64 * (r % 2):64 * (r % 2) + 64]
                tq.append((pool.alone(lambda e, dh=dh, src=src: e.tensor_copy(dh, src)), dl, src, dh))
            for th_, dl, src, dh in tq:
                pool.wait(th_)
                tt_ = pool.alone(lambda e, dl=dl, src=src, dh=dh: e.tensor_tensor(dl, src, dh.bitcast(f32),
                                                                               ALU.subtract))
            st["qd"][n] = tt_

        def load_cap():
            sp.wait(st["cap"])
            for h in range(2):
                sp.dma(lambda e, h=h: e.dma_start(
                    mski[64 * h:64 * h + 64],
                    t["mask"][bass.ds(regs["chunk"], 1)].rearrange("a q k -> (a q) k")), d_cap, at)
            st["capload"] = sp.dma(lambda e: e.dma_start(
                excl[:, :], t["excl"][bass.ds(regs["chunk"], 1)].rearrange("a q k -> (a q) k")), d_cap, at)

        def make_cap():
            dve.wait(st["capload"], st["capread"])
            a = dve.op(lambda e: e.tensor_scalar(cap[:, :], mski[:, :], 0.0, 1e9, ALU.not_equal, ALU.mult))
            dve.wait(a)
            st["cap"] = dve.op(lambda e: e.scalar_tensor_tensor(out=cap[:, :], in0=cap[:, :], scalar=-1e9,
                                                                in1=excl[:, :], op0=ALU.add, op1=ALU.add))

        def take_bank():
            i = st["kvn"] % 3
            st["kvn"] += 1
            return i, st["kv"][i]

        def k_part(n, g):
            i, free = take_bank()
            s = n % 2
            pe.wait(*t_wks, *st["t_split"][n], free)
            for k in range(4):
                tt = mm3(pb[i][:, 0:CW], [w[:, k, g * 128:(g + 1) * 128] for w in wk],
                         [chi[:, s, k, :], clo[:, s, k, :]], k == 0, k == 3)
            act.wait(tt, st["K"][g])
            th = act.op(lambda e: e.activation(kk[0][:, g, :], pb[i][:, 0:CW], ACT.Copy))
            dve.wait(tt, th, st["K"][g])
            tl = split_rest(kk[1][:, g, :], pb[i][:, 0:CW], kk[0][:, g, :])
            st["kv"][i] = tl
            return th, tl

        def queries(hf):
            for m in range(4):
                i, free_ = take_bank()
                pe.wait(*t_wqs, *t_xt[4 * hf + 3], free_)
                for k in range(4):
                    tt = mm3(pb[i][:, :], [w[:, k, m * 128:(m + 1) * 128] for w in wq], [v[:, k, :] for v in xt],
                             k == 0, k == 3)
                act.wait(tt)
                st["kv"][i] = t_q[hf] = act.op(lambda e, m=m, i=i: e.activation(
                    qc[:, m, hf * 512:(hf + 1) * 512], pb[i][:, :], ACT.Copy))
            xt_free.append(tt)
            return tt

        prepare_ctx(0, 0)
        load_cap()
        t_wv = load(wraw[:, 0], t["wv"], d_w[0], after=t_wqs)
        t_wks = split(wraw[:, 1], wk[0][:, :, :], wk[1][:, :, :], [t_wk])
        for i in range(4, 8):
            a = norm_stats(i, [t_x[1]])
        t_r[1] = norm_scale(4, 4, a, (rows[:, 1:2], t_rs))
        n_apply(4)
        n_apply(5)
        t_wvs = split(wraw[:, 0], wv[0][:, :, :], wv[1][:, :, :], [t_wv])
        make_cap()
        queries(0)
        prepare_q(0, 0)
        n_turn(4)
        n_apply(6)
        n_turn(5)
        n_apply(7)
        t_k0 = [k_part(0, g) for g in range(2)]
        n_turn(6)
        n_turn(7)
        t_k0 += [k_part(0, g) for g in range(2, 4)]
        t_pe0 = queries(1)
        st["P"] = [t_pe0] * 8
        first.close()

        second = ExitStack()
        pp = sb("pp", [128, 8, CW], f32, second)
        pt = sb("pt", [SW, 4, 4, 128], f32, second)
        def v_part(n, i4):
            i, free = take_bank()
            s = n % 2
            pe.wait(*t_wvs, free)
            for k in range(4):
                tt = mm3(pb[i][0:SW, :], [c[:, s, k, i4 * SW:(i4 + 1) * SW] for c in (chi, clo)],
                         [w[:, k, :] for w in wv], k == 0, k == 3)
            act.wait(tt, st["V"])
            st["kv"][i] = tv = act.op(lambda e: e.activation(vv[:, i4, :], pb[i][0:SW, :], ACT.Copy))
            st["cfree"][s] = tt
            return tv

        def s_part(n, b, seg, p8, t_k):
            g, u = divmod(p8, 2)
            s = n % 2
            bank = pb[3 + u]
            pe.wait(*t_k[g], st["qd"][n], st["S"][u])
            r = slice(64 * u, 64 * u + 64)
            tt = mm3(bank[:, 0:CW], [q[r, s, g, :] for q in (qh, ql)], [w[r, g, :] for w in kk], True, True)
            st["K"][g] = tt
            st["qfree"][s] = tt
            dve.wait(tt, st["P"][p8], st["cap"])
            dst = nm[:, b, p8:p8 + 1] if seg == 0 else nmn[:, s, p8:p8 + 1]
            if seg:
                dve.wait(st["state"][b])
            ini = 3e38 if seg == 0 else nm[:, b, p8:p8 + 1]
            st["S"][u] = td = dve.op(lambda e: e.tensor_tensor_reduce(
                out=pp[:, p8, :], in0=bank[:, 0:CW], in1=cap[:, :], scale=-1.0, scalar=ini,
                op0=ALU.add, op1=ALU.min, accum_out=dst))
            act.wait(td)
            sdst = ls[:, b, p8:p8 + 1] if seg == 0 else lsn[:, s, p8:p8 + 1]
            st["capread"] = td
            return td, act.op(lambda e: e.activation(pp[:, p8, :], pp[:, p8, :], ACT.Exp, bias=dst, scale=-1.0,
                                                     accum_out=sdst))

        def t_part(n, p8, t_e):
            u = p8 % 2
            pe.wait(t_e, st["T"][u], t_cst)
            bank = pb[5 + u]
            for i4 in range(4):
                tt = pe.op(lambda e, i4=i4: e.transpose(bank[0:SW, i4 * 128:(i4 + 1) * 128],
                                                        pp[:, p8, i4 * SW:(i4 + 1) * SW], ident), inc=(i4 == 3))
            st["P"][p8] = tt
            slot = p8 % 4
            dst = pt[:, slot, :, :].rearrange("p a c -> p (a c)")
            if u:
                act.wait(tt, st["PT"][slot])
                st["T"][u] = te = act.op(lambda e: e.activation(dst, bank[0:SW, :], ACT.Copy))
            else:
                dve.wait(tt, st["PT"][slot])
                st["T"][u] = te = dve.op(lambda e: e.tensor_copy(dst, bank[0:SW, :]))
            return te

        def pv_part(n, b, p8, te, t_v):
            slot = p8 % 4
            pe.wait(te, *t_v)
            if p8 == 0:
                pe.wait(st["O"])
            for i4 in range(4):
                tt = pe.op(lambda e, i4=i4: e.matmul(pb[7][:, p8 * 64:(p8 + 1) * 64], pt[:, slot, i4, :],
                                                     vv[:, i4, p8 * 64:(p8 + 1) * 64], start=(i4 == 0),
                                                     stop=(i4 == 3)), inc=(i4 == 3))
            st["PT"][slot] = tt
            st["V"] = tt
            return tt

        def o_part(n, b, seg, t_pv, t_exp, t_max):
            ov = pb[7][:, :].rearrange("p (t c) -> p t c", t=8)
            s = n % 2
            if seg == 0:
                dve.wait(t_pv)
                for h in range(2):
                    r = slice(64 * h, 64 * h + 64)
                    tt = dve.op(lambda e, r=r, h=h: e.tensor_copy(acc[r, b, :, :], ov[r, :, 32 * h:32 * h + 32]))
                st["O"] = st["state"][b] = tt
                return
            dve.wait(t_max, t_exp, st["state"][b])
            a = dve.op(lambda e: e.tensor_tensor(cor[:, s, :], nmn[:, s, :], nm[:, b, :], ALU.subtract))
            act.wait(a)
            c = act.op(lambda e: e.activation(cor[:, s, :], cor[:, s, :], ACT.Exp))
            dve.wait(c)
            a = dve.op(lambda e: e.tensor_copy(nm[:, b, :], nmn[:, s, :]))
            a = dve.op(lambda e: e.tensor_tensor(ls[:, b, :], ls[:, b, :], cor[:, s, :], ALU.mult))
            a2 = dve.op(lambda e: e.tensor_tensor(acc[:, b, :, :], acc[:, b, :, :],
                                                  cor[:, s, :].unsqueeze(2).to_broadcast([128, 8, 32]), ALU.mult))
            dve.wait(a, a2, t_pv)
            dve.op(lambda e: e.tensor_tensor(ls[:, b, :], ls[:, b, :], lsn[:, s, :], ALU.add))
            for h in range(2):
                r = slice(64 * h, 64 * h + 64)
                tt = dve.op(lambda e, r=r, h=h: e.tensor_tensor(acc[r, b, :, :], acc[r, b, :, :],
                                                                ov[r, :, 32 * h:32 * h + 32], ALU.add))
            st["O"] = st["state"][b] = tt

        ws = {"n": 0, "rawfree": [t_wvs, t_wks], "whfree": [t_pe0, None]}

        def fetch(src):
            n = ws["n"]
            ws["n"] += 1
            s = n % 2
            return s, load(raw[:, s], src, d_raw[s], after=ws["rawfree"][s] or ())

        def weight(src):
            s, tl = fetch(src)
            act.wait(ws["whfree"][s])
            dve.wait(ws["whfree"][s])
            tt = split(raw[:, s], wh[s][0][:, :, :], wh[s][1][:, :, :], [tl])
            ws["rawfree"][s] = tt
            return s, tt

        mbd0 = raw[:, 0, 2, 0:256].rearrange("p (j n) -> p j n", j=2)
        d_l = dsem("d_l")

        def lora_matrix():
            lora = raw[0:16, 0, 0, :].rearrange("p (j n) -> p j n", j=4)
            tl = load(lora, t["lora"], d_l, after=ws["rawfree"][0])
            i, free = take_bank()
            pe.wait(tl, free)
            for j in range(2):
                tt = pe.op(lambda e, j=j: e.matmul(pb[i][:, j * 128:(j + 1) * 128], lora[:, 2 * j, :],
                                                   lora[:, 2 * j + 1, :], start=True, stop=True))
            for j in range(2):
                dve.wait(tt, t_cst, *ws["rawfree"][0])
                a = dve.op(lambda e, j=j: e.tensor_tensor(mbd0[:, j, :], pb[i][:, j * 128:(j + 1) * 128],
                                                          cst[:, 256:384], ALU.mult))
                dve.wait(a)
                st["kv"][i] = dve.op(lambda e, j=j: e.tensor_tensor(mbd0[:, j, :], mbd0[:, j, :], ident, ALU.add))

        def clear_scratch():
            sp.wait(t_zero)
            for name, first_, n_ in [("xg", 7 * j, 7) for j in range(5)] + [("yg", E + 5 * j, 5) for j in range(3)]:
                for k in range(4):
                    t_xg0 = sp.dma(lambda e, name=name, first_=first_, n_=n_, k=k: e.dma_start(
                        t[name][first_ * 128:(first_ + n_) * 128, k * 128:(k + 1) * 128].rearrange(
                            "(a p) n -> p a n", p=128), zero[:, :].unsqueeze(1).to_broadcast([128, n_, 128])), d_z, at)
            return t_xg0

        def segment(seg):
            if seg:
                read_chunk(seg)
                prepare_ctx(16 * seg, 0)
                prepare_q(16 * seg, 0)
                load_cap()
                make_cap()
            base = 16 * seg
            old = None
            for b in range(NB + 1):
                n = base + b
                t_k, evac = [], {}
                for g in range(4):
                    if old is not None:
                        for p8 in (2 * g, 2 * g + 1):
                            evac[p8] = t_part(old["n"], p8, old["e"][p8])
                    if b < NB:
                        t_k.append(t_k0[g] if n == 0 else k_part(n, g))
                    if old is not None:
                        for p8 in (2 * g, 2 * g + 1):
                            t_pv = pv_part(old["n"], old["b"], p8, evac[p8], old["v"])
                if old is not None:
                    o_part(old["n"], old["b"], seg, t_pv, old["e"][7], old["m"])
                if b == NB:
                    break
                if b + 1 < NB:
                    prepare_ctx(n + 1, b + 1)
                    prepare_q(n + 1, b + 1)
                if seg == 0 and b == 2:
                    st["cleared"] = clear_scratch()
                if seg == 0 and b == 4:
                    st["wo"] = weight(t["wo"])
                if seg == 0 and b == 5:
                    st["w2q"] = fetch(t["w2q"])
                if seg == 0 and b == 6:
                    lora_matrix()
                t_v, t_e = [], []
                for g in range(4):
                    for p8 in (2 * g, 2 * g + 1):
                        t_max, te = s_part(n, b, seg, p8, t_k)
                        t_e.append(te)
                    t_v.append(v_part(n, g))
                old = {"n": n, "b": b, "v": t_v, "e": t_e, "m": t_max}

        segment(0)
        for q in engines:
            read_count(q)
        for seg in range(1, NC_):
            for q in engines:
                q.items.append(("if", lambda e, q=q, seg=seg: regs[q.name] > seg))
            segment(seg)
        for seg in range(1, NC_):
            for q in engines:
                q.items.append(("endif",))
        s_bar = sem("s_bar")
        for q in engines:
            q.items.append(("do", lambda e: e.drain().then_inc(s_bar, 1)))
        new_sems("1")
        for q in engines:
            q.items.append(("wait", s_bar, 5))

        second.close()
        lasting.close()

        xt = [sb(f"xu{j}", [128, 4, T], f32r) for j in range(2)]
        xn = sb("xm", [128, 2, D])
        wh.append([sb(f"wh1{j}", [128, 4, D], f32r) for j in range(2)])
        bro = sb("bro", [128, D + 4 * 4 + 40])
        bproj, bcol, bg2 = bro[:, 0:D], bro[:, D:D + 16], bro[:, D + 16:D + 36]
        d_b = dsem("d_b")
        t_bro = load(bro[:, :], t["bro"], d_b)
        bank = {"n": 0, "free": [None] * 3}

        def take(banks=(0, 1, 2)):
            i = bank["n"] % 3
            bank["n"] += 1
            return i, bank["free"][i]

        def stages_of_heads(t_acc, bias, banks, bfree, t_out):
            t_tr, t_hi = {}, {}

            def views(i):
                src = pb[banks[i % 2]][:, :].rearrange("p (b c q) -> p c b q", b=2, c=4)
                return src, [x[:, :, i * 128:(i + 1) * 128].rearrange("p c (b q) -> p c b q", b=2) for x in xt]

            def turn_(i):
                pe.wait(*t_acc[i], bfree[i % 2])
                for j in range(4):
                    b2, g2 = divmod(j, 2)
                    t_tr[i] = pe.op(lambda e, j=j, b2=b2, g2=g2: e.transpose(
                        pb[banks[i % 2]][:, j * 128:(j + 1) * 128],
                        acc[:, 2 * i + b2, 4 * g2:4 * g2 + 4, :].rearrange("p a c -> p (a c)"), ident), inc=(j == 3))

            def head_(i):
                src, dst = views(i)
                act.wait(t_tr[i])
                if bias is None:
                    t_hi[i] = act.op(lambda e: e.activation(dst[0], src, ACT.Copy))
                else:
                    act.wait(bias[1])
                    for c in range(4):
                        t_hi[i] = act.op(lambda e, c=c: e.activation(dst[0][:, c], src[:, c], ACT.Identity,
                                                                     bias=bias[0][:, c:c + 1]))

            def rest_(i):
                src, dst = views(i)
                dve.wait(t_hi[i], t_tr[i])
                if bias is None:
                    tl = split_rest(dst[1], src, dst[0])
                else:
                    for c in range(4):
                        tl = dve.op(lambda e, c=c: e.scalar_tensor_tensor(
                            out=dst[1][:, c], in0=src[:, c], scalar=bias[0][:, c:c + 1],
                            in1=dst[0][:, c].bitcast(f32), op0=ALU.add, op1=ALU.subtract))
                bfree[i % 2] = tl
                t_out[i] = (t_hi[i], tl)
            return turn_, head_, rest_

        def project(i, s, t_w, t_in, then):
            b_, free = take()
            pe.wait(*t_w, *t_in, free)
            for k in range(4):
                tt = mm3(pb[b_][:, :], [v[:, k, i * 128:(i + 1) * 128] for v in xt], [w[:, k, :] for w in wh[s]],
                         k == 0, k == 3)
            bank["free"][b_] = r = then(pb[b_], tt)
            return r

        def feature_major(m, hf, s, t_w, t_in, then):
            b_, free = take()
            pe.wait(*t_w, *t_in, free)
            for k in range(4):
                tt = mm3(pb[b_][:, :], [w[:, k, m * 128:(m + 1) * 128] for w in wh[s]],
                         [v[:, k, hf * 512:(hf + 1) * 512] for v in xt], k == 0, k == 3)
            ws["whfree"][s] = tt
            bank["free"][b_] = r = then(pb[b_], tt)
            return r

        def residual(i):
            def then(bk, tt):
                dve.wait(tt)
                return dve.op(lambda e: e.tensor_tensor(x_sb[:, i, :], x_sb[:, i, :], bk[:, :], ALU.add))
            return then

        turn = {"free": [None, None], "xn": [None, None]}

        def stages_of_norm(t_x, t_r, t_n, t_xt, banks, keep=None):
            def first_(i):
                t_r[i] = norm_scale(i, 1, norm_stats(i, [t_x[i]]))

            def second_(i):
                dst = xn[:, i % 2, :] if keep is None else keep[:, i, :]
                t_n[i] = norm_apply(i, dst, t_r[i], [turn["xn"][i % 2]])

            t_tr, t_hi = {}, {}

            def third_(i):
                src = xn[:, i % 2, :] if keep is None else keep[:, i, :]
                pe.wait(t_n[i], turn["free"][i % len(banks)])
                for k in range(4):
                    t_tr[i] = pe.op(lambda e, k=k: e.transpose(
                        pb[banks[i % len(banks)]][:, k * 128:(k + 1) * 128], src[:, k * 128:(k + 1) * 128], ident),
                        inc=(k == 3))
                turn["xn"][i % 2] = t_tr[i]

            def fourth_(i):
                pv = pb[banks[i % len(banks)]][:, :].rearrange("p (k n) -> p k n", k=4)
                act.wait(t_tr[i])
                t_hi[i] = act.op(lambda e: e.activation(xt[0][:, :, i * 128:(i + 1) * 128], pv, ACT.Copy))

            def fifth_(i):
                pv = pb[banks[i % len(banks)]][:, :].rearrange("p (k n) -> p k n", k=4)
                dve.wait(t_hi[i], t_tr[i])
                tl = split_rest(xt[1][:, :, i * 128:(i + 1) * 128], pv, xt[0][:, :, i * 128:(i + 1) * 128])
                turn["free"][i % len(banks)] = tl
                t_xt[i] = (t_hi[i], tl)
            return first_, second_, third_, fourth_, fifth_

        s_wo, t_wo = st["wo"]
        ws["rawfree"], ws["whfree"] = [None, None], [None, None]
        a = dve.op(lambda e: e.reciprocal(ls[:, :, :], ls[:, :, :]))
        t_ls = a
        t_x1, t_h2f, t_r, t_n, t_xt, t_na, t_pj = {}, {}, {}, {}, {}, {}, {}

        def o_gate(i):
            dve.wait(t_ls)
            t_na[i] = (dve.op(lambda e, i=i: e.tensor_tensor(
                acc[:, 2 * i:2 * i + 2, :, :], acc[:, 2 * i:2 * i + 2, :, :],
                ls[:, 2 * i:2 * i + 2, :].unsqueeze(3).to_broadcast([128, 2, 8, 32]), ALU.mult)),)
        h1, h2, h3 = stages_of_heads(t_na, None, (5, 6), [None, None], t_h2f)

        def o_project(i):
            b_, free_ = take()
            pe.wait(*t_wo, *t_h2f[i], free_)
            for k in range(4):
                tt = mm3(pb[b_][:, :], [v[:, k, i * 128:(i + 1) * 128] for v in xt],
                         [w[:, k, :] for w in wh[s_wo]], k == 0, k == 3)
            t_pj[i] = (b_, tt)
            ws["whfree"][s_wo] = tt

        def o_residual(i):
            b_, tt = t_pj[i]
            bank["free"][b_] = t_x1[i] = residual(i)(pb[b_], tt)

        n1, n2, n3, n4, n5 = stages_of_norm(t_x1, t_r, t_n, t_xt, (3, 4))

        mid = ExitStack()
        mbd = sb("mbd", [128, 2, 128], f32, mid)
        bl = sb("bl", [128, 8], f32, mid)
        kT = sb("kT", [128, 4, T], f32, mid)
        v2 = sb("v2", [128, 8, D], f32, mid)
        qd = sb("qd", [128, NB, 4, 128], f32, mid)
        p2 = sb("p2", [128, 2, 8, 2, 64], f32, mid)
        pt2 = sb("pt2", [128, 2, 8, 128], f32, mid)
        mx2 = sb("mx2", [128, 2, 16], f32, mid)
        ls2 = sb("ls2", [128, 3, 16], f32, mid)
        t_mbd = act.op(lambda e: e.activation(mbd[:, :, :], mbd0, ACT.Copy))
        ws["rawfree"][0] = (t_mbd,)
        t_z = pool.alone(lambda e: e.memset(qd[:, :, :, :], 0.0))

        def weight_lora(fetched, j):
            s, tl = fetched
            for k in range(4):
                b_, free_ = take()
                pe.wait(tl, t_mbd, free_)
                for g in range(4):
                    tt_ = pe.op(lambda e, g=g, k=k, b_=b_: e.matmul(
                        pb[b_][:, g * 128:(g + 1) * 128], raw[:, s, g, k * 128:(k + 1) * 128], mbd[:, j, :],
                        start=True, stop=True), inc=(g == 3))
                act.wait(tt_, ws["whfree"][s])
                th = act.op(lambda e, k=k, b_=b_: e.activation(wh[s][0][:, k, :], pb[b_][:, :], ACT.Copy))
                dve.wait(th, tt_, ws["whfree"][s])
                bank["free"][b_] = tlo = split_rest(wh[s][1][:, k, :], pb[b_][:, :], wh[s][0][:, k, :])
            ws["rawfree"][s] = (tt_,)
            return s, (th, tlo)

        s_, tw = weight_lora(st["w2q"], 0)
        pe.wait(t_mbd, t_bro)
        for c in range(4):
            pe.op(lambda e, c=c: e.matmul(pb[7][:, 256 + c:257 + c], mbd[:, 0, :], bcol[:, c:c + 1], start=True,
                                          stop=True), inc=False)
            tt = pe.op(lambda e, c=c: e.matmul(pb[7][:, 260 + c:261 + c], mbd[:, 1, :], bcol[:, 8 + c:9 + c],
                                               start=True, stop=True), inc=(c == 3))
        dve.wait(tt)
        t_bl = dve.op(lambda e: e.tensor_copy(bl[:, :], pb[7][:, 256:264]))

        def biased(dst, col, t_col):
            def then(bk, tt):
                act.wait(tt, t_col)
                return act.op(lambda e: e.activation(dst, bk[:, :], ACT.Identity, bias=col))
            return then

        def copied(dst):
            def then(bk, tt):
                act.wait(tt)
                return act.op(lambda e: e.activation(dst, bk[:, :], ACT.Copy))
            return then

        def diagonal(m, hf):
            def then(bk, tt):
                for r in (0, 2, 1, 3):
                    p_ = slice(32 * r, 32 * r + 32)
                    src = bk[p_, :].rearrange("p (b q) -> p b q", b=8)
                    dst = qd[p_, 8 * hf:8 * hf + 8, m, 64 * (r % 2):64 * (r % 2) + 64]
                    if r % 2 == 0:
                        act.wait(tt, t_bl, t_z)
                        a_ = act.op(lambda e, p_=p_, src=src, dst=dst: e.activation(
                            dst, src, ACT.Identity, bias=bl[p_, m:m + 1]))
                    else:
                        dve.wait(tt, t_bl, t_z, a_)
                        d_ = dve.op(lambda e, p_=p_, src=src, dst=dst: e.tensor_scalar(
                            dst, src, bl[p_, m:m + 1], None, ALU.add))
                return d_
            return then

        def q_early(i):
            if i >= 4:
                feature_major(i - 4, 0, s_, tw, t_xt[3], diagonal(i - 4, 0))

        pipeline([(o_gate, 0), (h1, 1), (h2, 1), (h3, 1), (o_project, 2), (o_residual, 3), (n1, 3), (n2, 4), (n5, 6),
                  (n3, 5), (n4, 5), (q_early, 6)])
        s_k, twk = weight(t["w2k"])
        for m in range(4):
            t_qT = feature_major(m, 1, s_, tw, t_xt[7], diagonal(m, 1))
        for hf in range(2):
            for m in range(4):
                t_kT = feature_major(m, hf, s_k, twk, (), biased(
                    kT[:, m, hf * 512:(hf + 1) * 512], bcol[:, 4 + m:5 + m], t_bro))
            if hf == 0:
                s_v, twv = weight_lora(fetch(t["w2v"]), 1)
        for i in range(8):
            t_v2 = project(i, s_v, twv, (), copied(v2[:, i, :]))
            if i == 1:
                s_wp, t_wp = weight(t["wproj"])
        ws["whfree"][s_v] = (pe.sem, pe.count)

        R, X = 8, 6
        xflat = [v[:, :, :].rearrange("p k n -> p (k n)") for v in xt]
        xo = [xflat[1][:, j * 1024:(j + 1) * 1024].rearrange("p (h k n) -> p h k n", h=2, k=4) for j in range(2)]
        wraws = [raw[:, r] for r in range(2)]
        wsplit = [[v[:, :, :] for v in wh[s_v]], [v[:, :, :] for v in wh[s_wp]],
                  [xflat[0][:, j * 2048:(j + 1) * 2048].rearrange("p (k n) -> p k n", k=4) for j in range(2)]]

        d_we = [dsem(f"d_we{i}") for i in range(R)]
        d_yo = [dsem(f"d_yo{i}") for i in range(4)]
        fe = {"raw": [ws["rawfree"][0], ws["rawfree"][1]] + [None] * (R - 2), "xi": [None] * X, "yo": [None] * 4,
              "T": [None, None], "wh": [ws["whfree"][s_v], None, None]}
        we_tok, t_ws = {}, {}

        def if_more(q, j, fn):
            if j >= 0:
                seen = dict(q.seen)
                q.items.append(("if", lambda e: regs[q.name] > j))
            fn()
            if j >= 0:
                q.items.append(("endif",))
                q.seen = seen

        def load_weight(n):
            r = n % R

            def fixed():
                sp.wait(*fe["raw"][r])
                we_tok[n] = sp.dma(lambda e: e.dma_start(wraws[r], t["We"][n]), d_we[r], at)

            def chosen():
                j = n - E
                sp.wait(*fe["raw"][r])
                sp.items.append(("do", lambda e: regs.__setitem__("x", e.value_load(
                    ji[0:1, j:j + 1], min_val=0, max_val=E - 1))))
                we_tok[n] = sp.dma(lambda e: e.dma_start(wraws[r], t["We"][bass.ds(regs["x"], 1)].rearrange(
                    "a p k n -> (a p) k n")), d_we[r], at)

            if n < E:
                fixed()
            elif n < E + 15:
                if_more(sp, n - E, chosen)

        wcount = {"act": 0, "dve": 0}
        s_w = {"act": sem("s_w_act"), "dve": sem("s_w_dve")}

        def split_weight(n, rest=dve):
            if n >= E + 15:
                return
            s_, r = n % 3, n % R
            head = lambda e: e.activation(wsplit[s_][0], wraws[r], ACT.Copy)
            tail = lambda e: e.tensor_tensor(wsplit[s_][1], wraws[r], wsplit[s_][0].bitcast(f32), ALU.subtract)
            if n < E:
                act.wait(we_tok[n], fe["wh"][s_])
                th = act.op(head)
                rest.wait(th, we_tok[n], fe["wh"][s_])
                tl = rest.op(tail) if rest is dve else rest.alone(tail)
            else:
                def apart(q, fn, *tokens):
                    def go():
                        q.wait(*tokens)
                        q.items.append(("op", fn, s_w[q.name]))
                    if_more(q, n - E, go)
                    wcount[q.name] += 1
                    return s_w[q.name], wcount[q.name]

                th = apart(act, head, we_tok[n], fe["wh"][s_])
                tl = apart(dve, tail, th, we_tok[n], fe["wh"][s_])
            fe["raw"][r] = t_ws[n] = (th, tl)

        load_weight(0)
        load_weight(1)
        split_weight(0, pool)
        load_weight(R)

        for i in range(8):
            pool.wait(t_n[i], t_x1[i], t_bro)
            t_xb = pool.alone(lambda e, i=i: e.tensor_tensor(x_sb[:, i, :], x_sb[:, i, :], bproj, ALU.add))

        fr2 = {"S": [None, None], "T": [None, None], "O": [None, None], "p2": [None, None], "pt2": [None, None],
               "E": None}
        hb = Same(bank["free"][0])
        t_e2, t_rl, t_pt, t_ac, t_x2, t_r3, t_n3, t_xt3 = {}, {}, {}, {}, {}, {}, {}, {}

        t_sc_, t_sum, t_vv, t_tn = {}, {}, {}, {}

        def a_scores(i):
            for u in range(2):
                pe.wait(t_qT, t_kT, fr2["S"][u])
                for b2 in range(2):
                    for g in range(4):
                        r = slice(64 * u, 64 * u + 64)
                        tt = pe.op(lambda e, b2=b2, g=g, r=r, u=u: e.matmul(
                            pb[3 + u][:, (b2 * 4 + g) * 64:(b2 * 4 + g + 1) * 64], qd[r, 2 * i + b2, g, :],
                            kT[r, g, (2 * i + b2) * 64:(2 * i + b2 + 1) * 64], start=True, stop=True),
                            inc=(b2 == 1 and g == 3))
                t_sc_[i, u] = tt

        def a_softmax(i):
            s = i % 2
            for u in range(2):
                src = pb[3 + u][:, :].rearrange("p (c k) -> p c k", k=64)
                dve.wait(t_sc_[i, u])
                a = dve.op(lambda e, u=u, src=src: e.tensor_reduce(mx2[:, s, 8 * u:8 * u + 8], src, AX.X, ALU.max))
            dve.wait(a, *(fr2["p2"][s] or ()))
            for u in range(2):
                src = pb[3 + u][:, :].rearrange("p (c k) -> p c k", k=64)
                for b2 in range(2):
                    tb = dve.op(lambda e, u=u, b2=b2, src=src: e.tensor_tensor(
                        p2[:, s, u:8:2, b2, :], src[:, 4 * b2:4 * b2 + 4, :],
                        mx2[:, s, 8 * u + 4 * b2:8 * u + 4 * b2 + 4].unsqueeze(2).to_broadcast([128, 4, 64]),
                        ALU.subtract))
                fr2["S"][u] = tb
            pv = p2[:, s].rearrange("p t b k -> p (t b k)")
            act.wait(tb)
            t_e2[i] = act.op(lambda e: e.activation(pv, pv, ACT.Exp, scale=SCALE))

        def a_sum(i):
            s = i % 2
            dve.wait(t_e2[i])
            t_sum[i] = a = dve.op(lambda e: e.tensor_reduce(
                ls2[:, i % 3, :], p2[:, s].rearrange("p t b k -> p (t b) k"), AX.X, ALU.add))
            dve.wait(a)
            t_rl[i] = dve.op(lambda e: e.reciprocal(ls2[:, i % 3, :], ls2[:, i % 3, :]))
            fr2["p2"][s] = (t_tn[i], a)

        def a_turn(i):
            s = i % 2
            ev = []
            for h in range(2):
                pe.wait(t_e2[i], fr2["T"][h])
                for j in range(4):
                    tt = pe.op(lambda e, h=h, j=j: e.transpose(
                        pb[5 + h][:, j * 128:(j + 1) * 128],
                        p2[:, s, 4 * h + j].rearrange("p b k -> p (b k)"), ident), inc=(j == 3))
                dst = pt2[:, s, 4 * h:4 * h + 4, :].rearrange("p a c -> p (a c)")
                act.wait(tt, fr2["pt2"][s])
                w_ = act.op(lambda e, dst=dst, h=h: e.activation(dst, pb[5 + h][:, :], ACT.Copy))
                fr2["T"][h] = w_
                ev.append(w_)
            t_pt[i] = ev
            t_tn[i] = tt

        def a_values(i):
            for b2 in range(2):
                bk = pb[(7, 2)[b2]]
                pe.wait(*t_pt[i], t_v2, t_bl, fr2["O"][b2], bank["free"][2])
                for p8 in range(8):
                    r = slice(64 * b2, 64 * b2 + 64)
                    tt = pe.op(lambda e, p8=p8, r=r, bk=bk: e.matmul(
                        bk[:, p8 * 64:(p8 + 1) * 64], pt2[r, i % 2, p8, :], v2[r, i, p8 * 64:(p8 + 1) * 64],
                        start=True, stop=True), inc=(p8 == 7))
                fr2["pt2"][i % 2] = tt
                t_vv[i, b2] = tt

        def a_out(i):
            t_ac[i] = []
            for b2 in range(2):
                ov = pb[(7, 2)[b2]][:, :].rearrange("p (t c) -> p t c", t=8)
                lv = ls2[:, i % 3, :].rearrange("p (t b) -> p t b", b=2)
                dve.wait(t_vv[i, b2], t_rl[i])
                for h in range(2):
                    r = slice(64 * h, 64 * h + 64)
                    w_ = dve.op(lambda e, r=r, h=h, b2=b2, ov=ov, lv=lv: e.tensor_tensor(
                        acc[r, 2 * i + b2, :, :], ov[r, :, 32 * h:32 * h + 32],
                        lv[r, :, b2:b2 + 1].to_broadcast([64, 8, 32]), ALU.mult))
                fr2["O"][b2] = w_
                t_ac[i].append(w_)

        t_h2f2 = {}
        h1, h2, h3 = stages_of_heads(t_ac, (bl[:, 4:8], t_bl), (0, 0), hb, t_h2f2)

        def a_project(i):
            pe.wait(*t_wp, *t_h2f2[i], bank["free"][1])
            for k in range(4):
                tt = mm3(pb[1][:, :], [v[:, k, i * 128:(i + 1) * 128] for v in xt],
                         [w[:, k, :] for w in wh[s_wp]], k == 0, k == 3)
            t_pj[i] = tt
            ws["whfree"][s_wp] = tt

        def a_residual(i):
            dve.wait(t_xb)
            bank["free"][1] = t_x2[i] = residual(i)(pb[1], t_pj[i])

        def a_stats(i):
            t_r[i] = norm_scale(i, 1, norm_stats(i, [t_x2[i]]))

        t_r = {}
        xall = acc[:, :, :, :].rearrange("p b t c -> p (b t c)").rearrange("p (i n) -> p i n", i=8)
        t_n, t_xt = {}, {}
        _, n2, n3, n4, n5 = stages_of_norm(t_x2, t_r, t_n, t_xt, (3, 4, 5, 6), xall)
        pipeline([(a_out, 3), (h3, 4), (a_residual, 5), (a_stats, 5), (n2, 6), (a_scores, 0),
                  (a_turn, 1), (a_sum, 1), (a_values, 2), (h1, 3), (h2, 3), (a_project, 4), (a_softmax, 0)])
        bank["free"][2] = fr2["O"][1]
        turn["free"] = list(fr2["S"]) + list(fr2["T"])
        mid.close()

        g1raw = sb("g1raw", [128, 4, 128])
        g1 = [sb(f"g1{j}", [128, 4, 128], f32r) for j in range(2)]
        gw = sb("gw", [128, 24])
        be = sb("be", [E, D])
        hT = sb("hT", [128, T])
        pr = sb("pr", [128, 8, E])
        gt = sb("gt", [128, 8, E])
        mg = sb("mg", [128, 8, 8])
        mi = sb("mi", [128, 8, 8], u32)
        mf = sb("mf", [128, 8, 8])
        sg = sb("sg", [128, 8])
        gT = sb("gT", [E, T])
        m12 = sb("m12", [128, 2, 8, E])
        sel = sb("sel", [128, 8, E])
        pre = sb("pre", [128, 9, E])
        sl = sb("sl", [128, 8, E])
        sm2 = hT[:, 0:320].rearrange("p (c i e) -> p c i e", c=2, i=8)
        sf = sb("sf", [128, 2, 8])
        si = sb("si", [128, 2, 8], u32)
        sm = sb("sm", [E, 10])
        orep = sb("orep", [E, 128])
        ob = sb("ob", [128, 60])
        jc = sb("jc", [1, 15, E])
        jf = sb("jf", [1, 16])
        ji = sb("ji", [1, 16], i32)
        cs2 = sb("cs2", [128, 660])
        wr = sb("wr", [128, 6, 4, D])
        xi = sb("xi", [128, 6, D])
        yo = [xn[:, 0, :], xn[:, 1, :], hT[:, 0:D], hT[:, D:T]]
        yga = wr[:, 0:2].rearrange("p r (a c) n -> p (r a) c n", c=2)
        dve.wait(t_x2[7])
        d_g = [dsem(f"d_g{i}") for i in range(3)]
        t_g1 = load(g1raw[:, :, :], t["wg1"], d_g[0], after=[t_x2[7]])
        t_gw = load(gw[:, :], t["wg2"], d_g[1])
        t_be = load(be[:, :], t["be"], d_g[2])
        t_cs2 = load(cs2[:, :], t["cs2"], dsem("d_cs2"))
        act.wait(t_x2[7])
        t_g1s = []

        def split_g1(i):
            if i == 5:
                t_g1s.extend(split(g1raw[:, :, :], g1[0][:, :, :], g1[1][:, :, :], [t_g1]))

        pipeline([(n3, 0), (n4, 0), (n5, 0), (split_g1, 0)])
        fe["raw"][2:] = [(t_x2[7],)] * (R - 2)
        fe["wh"][1] = ws["whfree"][s_wp]
        wraws += [wr[:, r] for r in range(6)]
        for n in range(2, R):
            load_weight(n)
        split_weight(1)
        load_weight(R + 1)
        t_xall = t_n[7]
        for hf in range(2):
            b_, fr_ = take()
            pe.wait(*t_g1s, *t_xt[4 * hf + 3], fr_)
            for k in range(4):
                tt = mm3(pb[b_][:, :], [w[:, k, :] for w in g1], [v[:, k, hf * 512:(hf + 1) * 512] for v in xt],
                         k == 0, k == 3)
            act.wait(tt, t_gw)
            bank["free"][b_] = t_h = act.op(lambda e, b_=b_, hf=hf: e.activation(
                hT[:, hf * 512:(hf + 1) * 512], pb[b_][:, :], ACT.Gelu, bias=gw[:, 20:21]))
        t_gate = tt
        pe.wait(t_h, t_gw)
        for i in range(8):
            tt = pe.op(lambda e, i=i: e.matmul(pb[7][:, i * E:(i + 1) * E], hT[:, i * 128:(i + 1) * 128],
                                               gw[:, 0:20], start=True, stop=True), inc=(i == 7))
        dve.wait(tt, t_bro)
        lg = pb[7][:, 0:8 * E].rearrange("p (i e) -> p i e", e=E)
        a = dve.op(lambda e: e.tensor_tensor(pr[:, :, :], lg, bg2.unsqueeze(1).to_broadcast([128, 8, E]), ALU.add))
        dve.wait(a)
        a = dve.op(lambda e: e.tensor_reduce(sg[:, :], pr[:, :, :], AX.X, ALU.max))
        dve.wait(a)
        a = dve.op(lambda e: e.tensor_tensor(pr[:, :, :], pr[:, :, :],
                                             sg[:, :].unsqueeze(2).to_broadcast([128, 8, E]), ALU.subtract))
        act.wait(a)
        a = act.op(lambda e: e.activation(pr[:, :, :], pr[:, :, :], ACT.Exp))
        fe["wh"][2] = t_gate
        split_weight(2, pool)
        load_weight(R + 2)
        dve.wait(a)
        a = dve.op(lambda e: e.tensor_reduce(sg[:, :], pr[:, :, :], AX.X, ALU.add))
        dve.wait(a)
        a = dve.op(lambda e: e.reciprocal(sg[:, :], sg[:, :]))
        dve.wait(a)
        a = dve.op(lambda e: e.tensor_tensor(pr[:, :, :], pr[:, :, :],
                                             sg[:, :].unsqueeze(2).to_broadcast([128, 8, E]), ALU.mult))
        dve.wait(a)
        for i in range(8):
            a = dve.op(lambda e, i=i: e.max(out=mg[:, i, :], in_=pr[:, i, :]))
        dve.wait(a)
        for i in range(8):
            a = dve.op(lambda e, i=i: e.max_index(mi[:, i, :], mg[:, i, :], pr[:, i, :]))
        dve.wait(a)
        a = dve.op(lambda e: e.tensor_copy(mf[:, :, :], mi[:, :, :]))
        dve.wait(a)
        for c in range(2):
            a = dve.op(lambda e, c=c: e.tensor_tensor(
                m12[:, c, :, :], iota20.unsqueeze(1).to_broadcast([128, 8, E]),
                mf[:, :, c:c + 1].to_broadcast([128, 8, E]), ALU.is_equal))
        dve.wait(a)
        t_sel = dve.op(lambda e: e.tensor_tensor(sel[:, :, :], m12[:, 0, :, :], m12[:, 1, :, :], ALU.add))
        dve.wait(t_sel)
        t_all = dve.op(lambda e: e.tensor_reduce(pre[:, 8, :], sel[:, :, :].rearrange("p i e -> p e i"), AX.X,
                                                 ALU.add))
        dve.op(lambda e: e.memset(pre[:, 0, :], 0.0))
        a = dve.op(lambda e: e.tensor_copy(pre[:, 1, :], sel[:, 0, :]))
        for i in range(1, 7):
            dve.wait(a)
            a = dve.op(lambda e, i=i: e.tensor_tensor(pre[:, i + 1, :], pre[:, i, :], sel[:, i, :], ALU.add))

        upper, ones = cs2[:, 0:128], cs2[:, 128:256]
        tri, ks, e128, esh, jg = cs2[0:E, 256:296], cs2[0:E, 300:307], cs2[:, 320:340], cs2[:, 340:360], \
            cs2[0:1, 360:660]
        pe.wait(t_all, t_cs2)
        t_cnt = pe.op(lambda e: e.matmul(pb[3][0:E, 0:1], pre[:, 8, :], ones[:, 0:1], start=True, stop=True))
        pe.wait(a, t_sel)
        pe.op(lambda e: e.matmul(pb[7][:, 0:160], upper, sel[:, :, :].rearrange("p i e -> p (i e)"), start=True,
                                 stop=False), inc=False)
        t_pos = pe.op(lambda e: e.matmul(pb[7][:, 0:160], ones, pre[:, 0:8, :].rearrange("p i e -> p (i e)"),
                                         start=False, stop=True))
        dve.wait(t_cnt, t_cs2)
        a = dve.op(lambda e: e.tensor_copy(sm[0:E, 8:9], pb[3][0:E, 0:1]))
        dve.wait(a)
        a = dve.op(lambda e: e.tensor_scalar(sm[0:E, 0:7], ks, sm[0:E, 8:9], None, ALU.is_lt))
        dve.wait(a)
        a = dve.op(lambda e: e.tensor_reduce(sm[0:E, 9:10], sm[0:E, 0:7], AX.X, ALU.add))
        dve.wait(a)
        a = dve.op(lambda e: e.tensor_scalar(orep[:, :], ones[0:E, :], sm[0:E, 9:10], None, ALU.mult))
        pe.wait(a)
        t_ob = pe.op(lambda e: e.matmul(pb[4][:, 0:40], orep[:, :], tri, start=True, stop=True))
        posv = pb[7][:, 0:160].rearrange("p (i e) -> p i e", e=E)
        dve.wait(t_pos)
        a0 = dve.op(lambda e: e.tensor_tensor(sl[:, :, :], posv, e128.unsqueeze(1).to_broadcast([128, 8, E]),
                                              ALU.add))
        dve.wait(t_ob)
        a = dve.op(lambda e: e.tensor_copy(ob[:, 0:40], pb[4][:, 0:40]))
        dve.wait(a)
        a = dve.op(lambda e: e.scalar_tensor_tensor(out=ob[:, 40:60], in0=ob[:, 0:20], scalar=128.0, in1=esh,
                                                    op0=ALU.mult, op1=ALU.add))
        b0 = dve.op(lambda e: e.tensor_tensor(jc[:, :, :], ob[0:1, 20:40].unsqueeze(1).to_broadcast([1, 15, E]),
                                              jg.rearrange("p (j e) -> p j e", e=E), ALU.is_le))
        dve.wait(a, a0)
        a = dve.op(lambda e: e.scalar_tensor_tensor(
            out=sel[:, :, :], in0=posv, scalar=128.0, in1=ob[:, 40:60].unsqueeze(1).to_broadcast([128, 8, E]),
            op0=ALU.is_ge, op1=ALU.mult))
        dve.wait(b0)
        b0 = dve.op(lambda e: e.tensor_reduce(jf[:, 0:15], jc[:, :, :], AX.X, ALU.add))
        dve.wait(a)
        a = dve.op(lambda e: e.tensor_tensor(sl[:, :, :], sl[:, :, :], sel[:, :, :], ALU.add))
        dve.wait(a)
        a = dve.op(lambda e: e.tensor_tensor(sm2[:, :, :, :], m12[:, :, :, :],
                                             sl[:, :, :].unsqueeze(1).to_broadcast([128, 2, 8, E]), ALU.mult))
        dve.wait(a)
        a = dve.op(lambda e: e.tensor_reduce(sf[:, :, :], sm2[:, :, :, :], AX.X, ALU.add))
        dve.wait(a)
        t_slot = dve.op(lambda e: e.tensor_copy(si[:, :, :], sf[:, :, :]))
        b0 = dve.op(lambda e: e.tensor_scalar(ji[:, 0:15], jf[:, 0:15], float(E - 1), None, ALU.min))
        t_ji = dve.op(lambda e: e.tensor_copy(ji[:, 15:16], ob[0:1, 39:40]))
        dve.wait(a)
        dve.op(lambda e: e.tensor_tensor(gt[:, :, :], m12[:, 0, :, :], m12[:, 1, :, :], ALU.add))
        dve.wait((dve.sem, dve.count))
        t_gt = dve.op(lambda e: e.tensor_tensor(gt[:, :, :], gt[:, :, :], pr[:, :, :], ALU.mult))

        d_sc, d_ga = dsem("d_sc"), dsem("d_ga")
        pool.wait(t_slot, st["cleared"], t_xall)
        for i in range(8):
            for c in range(2):
                t_sc = pool.dma(lambda e, i=i, c=c: e.indirect_dma_start(
                    out=t["xg"][:, :], out_offset=bass.IndirectOffsetOnAxis(ap=si[:, c, i:i + 1], axis=0),
                    in_=xall[:, i, :], in_offset=None), d_sc, at)

        fe["xo"] = [t_gate, t_gate]
        fe["y"] = [t_slot, t_slot]
        d_xi = [dsem(f"d_xi{i}") for i in range(X)]
        ybank = [pb[3], pb[4]]
        ystore, xi_tok, t_xs = {}, {}, {}

        def load_tokens(n):
            r = n % X

            def go():
                sp.wait(t_sc, fe["xi"][r])
                xi_tok[n] = sp.dma(lambda e: e.dma_start(xi[:, r, :], t["xg"][n * 128:(n + 1) * 128, :]), d_xi[r], at)

            if n < E + 15:
                if_more(sp, n - E - 1, go)

        def turn_tokens(n):
            if n >= E + 15:
                return
            h = n % 2
            bk = pb[5 + h]
            pe.wait(xi_tok[n], fe["T"][h])
            for k in range(4):
                tt = pe.op(lambda e, k=k: e.transpose(bk[:, k * 128:(k + 1) * 128],
                                                      xi[:, n % X, k * 128:(k + 1) * 128], ident), inc=(k == 3))
            fe["xi"][n % X] = tt
            pv = bk[:, :].rearrange("p (k n) -> p k n", k=4)
            act.wait(tt, fe["xo"][h])
            xh = act.op(lambda e: e.activation(xo[0][:, h], pv, ACT.Copy))
            dve.wait(xh, tt, fe["xo"][h])
            fe["T"][h] = xl = split_rest(xo[1][:, h], pv, xo[0][:, h])
            t_xs[n] = (xh, xl)

        def block_of(n):
            s_, h = n % 3, n % 2
            turn_tokens(n + 1)
            if n:
                split_weight(n + 2)
                load_weight(n + 2 + R)
            load_tokens(n + 1 + X)
            pe.wait(*t_ws[n], *t_xs[n], fe["y"][h])
            for k in range(4):
                tt = mm3(ybank[h][:, :], [v[:, h, k, :] for v in xo], [w[:, k, :] for w in wsplit[s_]], k == 0, k == 3)
            fe["wh"][s_] = fe["xo"][h] = tt
            act.wait(tt, fe["yo"][n % 4])
            fe["y"][h] = ty = act.op(lambda e: e.activation(yo[n % 4], ybank[h][:, :], ACT.Copy))
            act.wait(ty)
            ystore[n] = fe["yo"][n % 4] = act.dma(lambda e: e.dma_start(
                t["yg"][n * 128:(n + 1) * 128, :], yo[n % 4]), d_yo[n % 4], at)

        pe.wait(t_gt)
        for hf in range(2):
            for j in range(4):
                i = 4 * hf + j
                tt = pe.op(lambda e, i=i, j=j, hf=hf: e.transpose(pb[5 + hf][0:E, j * 128:(j + 1) * 128],
                                                                  gt[:, i, :], ident), inc=(j == 3))
            dve.wait(tt)
            t_gT = dve.op(lambda e, hf=hf: e.tensor_copy(gT[:, hf * 512:(hf + 1) * 512], pb[5 + hf][0:E, :]))
        t_y = []
        for i in range(8):
            b_, fr_ = take()
            pe.wait(t_gT, t_be, fr_)
            tt = pe.op(lambda e, i=i, b_=b_: e.matmul(pb[b_][:, :], gT[:, i * 128:(i + 1) * 128], be[:, :],
                                                      start=True, stop=True))
            bank["free"][b_] = r_ = residual(i)(pb[b_], tt)
            t_y.append(r_)

        fe["T"] = [t_gT, t_gT]
        for q in engines:
            q.wait(t_ji)
            q.items.append(("do", lambda e, q=q: regs.__setitem__(q.name, e.value_load(
                ji[0:1, 15:16], min_val=0, max_val=15))))
        for n in range(X):
            load_tokens(n)
        turn_tokens(0)
        load_tokens(X)
        for n in range(E):
            block_of(n)

        for j in range(15):
            for q in engines:
                q.items.append(("if", lambda e, q=q, j=j: regs[q.name] > j))
            block_of(E + j)
        for d in d_yo:
            sp.items.append(("wait", d[0], at[d[1]]))
        for j in range(14, -1, -1):
            for q in engines:
                q.items.append(("endif",))
            sp.items.append(("else",))
            for n_ in range(E + j - 4, E + j):
                sp.items.append(("wait", *ystore[n_]))
            sp.items.append(("endif",))
        s_bar2 = sem("s_bar2")
        for q in engines:
            q.items.append(("do", lambda e: e.drain().then_inc(s_bar2, 1)))
        new_sems("2")
        for q in engines:
            q.items.append(("wait", s_bar2, 5))

        d_ga = [dsem(f"d_ga{i}") for i in range(4)]
        d_out = dsem("d_out")
        gf = [None] * 4
        for i in range(8):
            r = i % 4
            pool.wait(gf[r])
            for c in range(2):
                tg = pool.dma(lambda e, i=i, c=c, r=r: e.indirect_dma_start(
                    out=yga[:, r, c, :], out_offset=None, in_=t["yg"][:, :],
                    in_offset=bass.IndirectOffsetOnAxis(ap=si[:, c, i:i + 1], axis=0)), d_ga[r], at)
            dve.wait(tg)
            a = dve.op(lambda e, i=i, r=r: e.scalar_tensor_tensor(
                out=x_sb[:, i, :], in0=yga[:, r, 0, :], scalar=mg[:, i, 0:1], in1=x_sb[:, i, :], op0=ALU.mult,
                op1=ALU.add))
            dve.wait(a)
            gf[r] = a = dve.op(lambda e, i=i, r=r: e.scalar_tensor_tensor(
                out=x_sb[:, i, :], in0=yga[:, r, 1, :], scalar=mg[:, i, 1:2], in1=x_sb[:, i, :], op0=ALU.mult,
                op1=ALU.add))
            sp.wait(a)
            t_o = sp.dma(lambda e, i=i: e.dma_start(out.rearrange("(i b) q d -> i (b q) d", b=2)[i],
                                                    x_sb[:, i, :]), d_out, at)
        sp.wait(t_o)

        block = root.enter_context(nc.Block())

        @block.sync
        def _(eng):
            sp.run(eng)

        @block.gpsimd
        def _(eng):
            pool.run(eng)

        @block.scalar
        def _(eng):
            act.run(eng)

        @block.vector
        def _(eng):
            dve.run(eng)

        @block.tensor
        def _(eng):
            pe.run(eng)


def kernel(**inputs):
    import numpy as _np
    import concourse.bacc as _bacc
    from concourse import mybir as _mybir
    from concourse.bass_utils import run_bass_kernel_spmd as _run

    v = {k: _np.asarray(a) for k, a in inputs.items()}
    NC, CW, K = 4, 404, 1601
    lead = NC * CW - K

    def kmajor(w):
        return w.reshape(4, 128, -1).transpose(1, 0, 2)

    ctx = _np.concatenate([_np.zeros((16, lead, 512), _np.float32), v["ctx_1024"]], 1)
    mask = _np.concatenate([_np.zeros((64, lead), _np.int32), v["mask_1x1xSxS2_ik0"][0, 0]], 1)
    excl = _np.zeros((NC, 128, CW), _np.float32)
    excl[0, :, :lead] = -3e38
    cst = _np.zeros((128, 384), _np.float32)
    cst[:, 0:128] = _np.eye(128)
    cst[0:4, 128:132] = _np.eye(4)
    cst[0:4, 132:136] = _np.triu(_np.ones((4, 4)))
    cst[0, 136:140] = _np.arange(4)
    cst[:, 140] = -0.5
    cst[:, 160:180] = _np.arange(20)
    cst[:, 256:384] = 2.0 * _np.kron(_np.eye(4), _np.ones((32, 32)))

    cs2 = _np.zeros((128, 660), _np.float32)
    cs2[:, 0:128] = _np.triu(_np.ones((128, 128)), 1)
    cs2[:, 128:256] = 1.0
    cs2[0:20, 256:276] = _np.triu(_np.ones((20, 20)), 1)
    cs2[0:20, 276:296] = _np.triu(_np.ones((20, 20)))
    cs2[0:20, 300:307] = 128.0 * _np.arange(1, 8)
    cs2[:, 320:340] = 128.0 * _np.arange(20)
    cs2[:, 340:360] = 128.0 * (19 - _np.arange(20))
    cs2[:, 360:660] = _np.repeat(_np.arange(15), 20)

    def heads(w):
        return w.reshape(2, 4, 2, 32, -1).transpose(1, 3, 0, 2, 4).reshape(128, 4, -1)

    wqkv, bqkv = v["L0_attn_w_qkv"], v["L0_attn_b_qkv"]
    bro = _np.zeros((128, 568), _np.float32)
    bro[:, 0:512] = v["L0_attn_b_proj"]
    bro[:, 512:516] = bqkv[0:512].reshape(4, 128).T
    bro[:, 516:520] = bqkv[512:1024].reshape(4, 128).T
    bro[:, 520:524] = heads(bqkv[1024:1536])[:, :, 0]
    bro[:, 528:548] = v["L0_ffn_bg2"][:20]
    wg2 = _np.zeros((128, 24), _np.float32)
    wg2[:, 0:20] = v["L0_ffn_wg2"][:, :20]
    wg2[:, 20] = v["L0_ffn_bg1"]
    lora = _np.stack([_np.tile(v["L0_attn_a_q"].T, (1, 4)), _np.tile(v["L0_attn_b_q"], (1, 4)),
                      _np.tile(v["L0_attn_a_v"].T, (1, 4)), _np.tile(v["L0_attn_b_v"], (1, 4))], 1)
    arrays = {
        "x": v["x"],
        "ctx": ctx.reshape(16, NC, CW, 4, 128).transpose(0, 1, 4, 3, 2),
        "mask": mask.reshape(64, NC, CW).transpose(1, 0, 2),
        "excl": excl,
        "cst": cst,
        "cs2": cs2,
        "bro": bro,
        "wq": kmajor(v["L0_xattn_w_q"].T),
        "wk": kmajor(v["L0_xattn_w_k"].T),
        "wv": kmajor(v["L0_xattn_w_v"].T),
        "wo": heads(v["L0_xattn_w_o"].T),
        "w2q": kmajor(wqkv[:, 0:512].T),
        "w2k": kmajor(wqkv[:, 512:1024]),
        "w2v": kmajor(wqkv[:, 1024:1536].T),
        "wproj": heads(v["L0_attn_w_proj"]),
        "lora": lora,
        "wg1": kmajor(v["L0_ffn_wg1"]),
        "wg2": wg2,
        "be": v["L0_ffn_be"],
        "We": v["L0_ffn_We"].reshape(20, 4, 128, 512).transpose(0, 2, 1, 3),
    }
    nc = _bacc.Bacc("TRN2", target_bir_lowering=False, num_devices=1)
    fed, t = {}, {}
    for name, a in arrays.items():
        a = _np.ascontiguousarray(a)
        fed[f"in_{name}"] = a
        t[name] = nc.dram_tensor(f"in_{name}", a.shape, _mybir.dt.from_np(a.dtype), kind="ExternalInput").ap()
    for name in ("xg", "yg"):
        t[name] = nc.dram_tensor(f"scratch_{name}", (35 * 128, 512), _mybir.dt.float32, kind="Internal").ap()
    out = nc.dram_tensor("out_0_dram", (16, 64, 512), _mybir.dt.float32, kind="ExternalOutput").ap()
    perceiver(nc, t, out)
    r = _run(nc, [fed], core_ids=[0])
    return r.results[0]["out_0_dram"]
```
